# Optimizing a Trainium2 kernel written in Bass

```python
import numpy as np
import jax
import jax.numpy as jnp

def _softmax(x, axis=-1):
    return jax.nn.softmax(x, axis=axis)

def _gelu(x):
    return jax.nn.gelu(x, approximate=True)

def _silu(x):
    return jax.nn.silu(x)

def _sigmoid(x):
    return jax.nn.sigmoid(x)

def _layernorm(x, axis=-1, eps=1e-05):
    m = jnp.mean(x, axis=axis, keepdims=True)
    v = jnp.var(x, axis=axis, keepdims=True)
    return (x - m) / jnp.sqrt(v + eps)

def _scatter_add(tgt, idx, src, axis=0):
    return tgt.at[idx].add(src)

def _segment_sum(src, seg, n):
    return jax.ops.segment_sum(src, seg, n)
kernel_name = 'mk_gnn_preln_d4_gnn_r16_1fc772'

def setup_inputs(seed: int=0):
    np.random.seed(seed)
    _w = jnp.asarray

    def _rec_inputs():
        import jax
        import jax.numpy as jnp
        _gk = jax.random.key(seed)
        x = -0.0003713 + 1 * jax.random.normal(jax.random.fold_in(_gk, 1), (6250, 128), jnp.float32)
        _s = jax.random.randint(jax.random.fold_in(_gk, 2), (100000,), 0, 6250, jnp.int32)
        _d = jax.random.randint(jax.random.fold_in(_gk, 3), (100000,), 0, 6250, jnp.int32)
        _loop = jnp.arange(6250, dtype=jnp.int32)
        src = jnp.concatenate([_s, _d, _loop])
        dst = jnp.concatenate([_d, _s, _loop])
        _o = jnp.argsort(dst, stable=True)
        src = src[_o]
        dst = dst[_o]
        edge_attr_64 = 0.000102155 + 1.00015 * jax.random.normal(jax.random.fold_in(_gk, 12), (206250, 64), jnp.float32)
        edge_type_8 = jax.random.randint(jax.random.fold_in(_gk, 14), (206250,), 0, 8, jnp.int32)
        edge_type_9 = jax.random.randint(jax.random.fold_in(_gk, 15), (206250,), 0, 9, jnp.int32)
        edge_weight = jax.random.uniform(jax.random.fold_in(_gk, 16), (206250,), jnp.float32, 0.0, 0.999999)
        edge_weight1 = jax.random.uniform(jax.random.fold_in(_gk, 17), (206250, 1), jnp.float32, 0.0, 0.999999)
        return (x, src, dst, edge_attr_64, edge_type_8, edge_type_9, edge_weight, edge_weight1)
    x, src, dst, edge_attr_64, edge_type_8, edge_type_9, edge_weight, edge_weight1 = _rec_inputs()

    def _L0_gnn_setup():
        import jax, jax.numpy as jnp
        import numpy as np
        N_NODES = 6250
        N_EDGES = 37500
        FEAT = 128
        N_RELS = 8
        key = jax.random.key(seed)
        k1, k2, k3, k4, k5, k6, k7 = jax.random.split(key, 7)
        return {'h': jax.random.normal(k1, (N_NODES, FEAT), dtype=jnp.float32), 'weight': jax.random.normal(k2, (N_RELS, FEAT, FEAT), dtype=jnp.float32) * (1.0 / np.sqrt(FEAT)), 'gate_weight': jax.random.normal(k3, (N_RELS, FEAT, 1), dtype=jnp.float32) * (1.0 / np.sqrt(FEAT)), 'norm': jax.random.uniform(k4, (N_EDGES, 1), dtype=jnp.float32), 'src': jax.random.randint(k5, (N_EDGES,), 0, N_NODES, dtype=jnp.int32), 'dst': jax.random.randint(k6, (N_EDGES,), 0, N_NODES, dtype=jnp.int32), 'rel_type': jax.random.randint(k7, (N_EDGES,), 0, N_RELS, dtype=jnp.int32)}
    _L0_gnn_all = _L0_gnn_setup()
    _L0_gnn_in = {k: v for k, v in _L0_gnn_all.items() if k in ('weight', 'gate_weight')}
    del _L0_gnn_all

    def _L1_gnn_setup():
        import jax, jax.numpy as jnp
        import numpy as np
        N_NODES = 6250
        N_EDGES = 31250
        IN_CH = 128
        EDGE_CH = 64

        def _glorot(key, shape):
            fan_in, fan_out = (shape[0], shape[1])
            lim = (6.0 / (fan_in + fan_out)) ** 0.5
            return jax.random.uniform(key, shape, jnp.float32, -lim, lim)
        key = jax.random.key(seed)
        ks = jax.random.split(key, 14)
        x = jax.random.normal(ks[0], (N_NODES, IN_CH), jnp.float32)
        edge_index = jax.random.randint(ks[1], (2, N_EDGES), 0, N_NODES, jnp.int64)
        edge_attr = jax.random.normal(ks[2], (N_EDGES, EDGE_CH), jnp.float32)
        timestamps = jax.random.uniform(ks[3], (N_EDGES,), jnp.float32)
        We1 = _glorot(ks[4], (EDGE_CH, 2 * EDGE_CH))
        be1 = jnp.zeros((2 * EDGE_CH,), jnp.float32)
        We2 = _glorot(ks[5], (2 * EDGE_CH, IN_CH))
        be2 = jnp.zeros((IN_CH,), jnp.float32)
        Wt = _glorot(ks[6], (1, IN_CH))
        bt = jnp.zeros((IN_CH,), jnp.float32)
        Wn1 = _glorot(ks[7], (2 * IN_CH, IN_CH))
        bn1 = jnp.zeros((IN_CH,), jnp.float32)
        Wn2 = _glorot(ks[8], (IN_CH, IN_CH))
        bn2 = jnp.zeros((IN_CH,), jnp.float32)
        return {'x': x, 'edge_index': edge_index, 'edge_attr': edge_attr, 'timestamps': timestamps, 'We1': We1, 'be1': be1, 'We2': We2, 'be2': be2, 'Wt': Wt, 'bt': bt, 'Wn1': Wn1, 'bn1': bn1, 'Wn2': Wn2, 'bn2': bn2}
    _L1_gnn_all = _L1_gnn_setup()
    _L1_gnn_in = {k: v for k, v in _L1_gnn_all.items() if k in ('We1', 'be1', 'We2', 'be2', 'Wt', 'bt', 'Wn1', 'bn1', 'Wn2', 'bn2')}
    del _L1_gnn_all

    def _L2_gnn_setup():
        import jax, jax.numpy as jnp
        import numpy as np
        NUM_EDGE_TYPES = 8
        HIDDEN = 128
        N_NODES = 3125
        N_EDGES = 37500

        def _gru_cell(x, h, W_ih, W_hh, b_ih, b_hh):
            H = h.shape[-1]
            gi = x @ W_ih.T + b_ih
            gh = h @ W_hh.T + b_hh
            i_r, i_z, i_n = (gi[:, :H], gi[:, H:2 * H], gi[:, 2 * H:])
            h_r, h_z, h_n = (gh[:, :H], gh[:, H:2 * H], gh[:, 2 * H:])
            r = jax.nn.sigmoid(i_r + h_r)
            z = jax.nn.sigmoid(i_z + h_z)
            n = jnp.tanh(i_n + r * h_n)
            return (1.0 - z) * n + z * h
        key = jax.random.key(seed)
        ks = jax.random.split(key, 10)
        H = HIDDEN
        h = jax.random.normal(ks[0], (N_NODES, H), dtype=jnp.float32)
        edge_index = jax.random.randint(ks[1], (2, N_EDGES), 0, N_NODES, dtype=jnp.int32)
        edge_type = jax.random.randint(ks[2], (N_EDGES,), 0, NUM_EDGE_TYPES + 1, dtype=jnp.int32)
        s = 1.0 / np.sqrt(H)
        W_msg = jax.random.uniform(ks[3], (H, H), jnp.float32, -s, s)
        b_msg = jax.random.uniform(ks[4], (H,), jnp.float32, -s, s)
        edge_embed = jax.random.normal(ks[5], (NUM_EDGE_TYPES + 1, H), dtype=jnp.float32)
        W_ih = jax.random.uniform(ks[6], (3 * H, H), jnp.float32, -s, s)
        W_hh = jax.random.uniform(ks[7], (3 * H, H), jnp.float32, -s, s)
        b_ih = jax.random.uniform(ks[8], (3 * H,), jnp.float32, -s, s)
        b_hh = jax.random.uniform(ks[9], (3 * H,), jnp.float32, -s, s)
        return {'h': h, 'edge_index': edge_index, 'edge_type': edge_type, 'num_nodes': N_NODES, 'W_msg': W_msg, 'b_msg': b_msg, 'edge_embed': edge_embed, 'W_ih': W_ih, 'W_hh': W_hh, 'b_ih': b_ih, 'b_hh': b_hh}
    _L2_gnn_all = _L2_gnn_setup()
    _L2_gnn_in = {k: v for k, v in _L2_gnn_all.items() if k in ('W_msg', 'b_msg', 'edge_embed', 'W_ih', 'W_hh', 'b_ih', 'b_hh')}
    del _L2_gnn_all

    def _L3_gnn_setup():
        import jax, jax.numpy as jnp
        import numpy as np
        N = 3125
        E = 37500
        IN_DIM = 128
        HID = 128

        def gcn_conv(x, edge_index, W, b):
            n = x.shape[0]
            loop = jnp.arange(n, dtype=edge_index.dtype)
            src = jnp.concatenate([edge_index[0], loop])
            dst = jnp.concatenate([edge_index[1], loop])
            deg = jax.ops.segment_sum(jnp.ones(src.shape[0], dtype=x.dtype), dst, num_segments=n)
            dinv = jnp.where(deg > 0, jax.lax.rsqrt(jnp.maximum(deg, 1.0)), 0.0)
            norm = dinv[src] * dinv[dst]
            h = x @ W.T
            msg = h[src] * norm[:, None]
            out = jax.ops.segment_sum(msg, dst, num_segments=n)
            return out + b
        key = jax.random.key(seed)
        ks = jax.random.split(key, 8)
        x = jax.random.normal(ks[0], (N, IN_DIM), dtype=jnp.float32)
        edge_index = jax.random.randint(ks[1], (2, E), 0, N, dtype=jnp.int64)
        s_in = 1.0 / np.sqrt(IN_DIM)
        s_h = 1.0 / np.sqrt(HID)
        W1 = jax.random.uniform(ks[2], (HID, IN_DIM), jnp.float32, -s_in, s_in)
        W2 = jax.random.uniform(ks[3], (HID, HID), jnp.float32, -s_h, s_h)
        W3 = jax.random.uniform(ks[4], (HID, HID), jnp.float32, -s_h, s_h)
        b1 = jnp.zeros((HID,), jnp.float32)
        b2 = jnp.zeros((HID,), jnp.float32)
        b3 = jnp.zeros((HID,), jnp.float32)
        return {'x': x, 'edge_index': edge_index, 'W1': W1, 'b1': b1, 'W2': W2, 'b2': b2, 'W3': W3, 'b3': b3}
    _L3_gnn_all = _L3_gnn_setup()
    _L3_gnn_in = {k: v for k, v in _L3_gnn_all.items() if k in ('W1', 'b1', 'W2', 'b2', 'W3', 'b3')}
    del _L3_gnn_all
    return {'x': x, 'src': src, 'dst': dst, 'edge_attr_64': edge_attr_64, 'edge_type_8': edge_type_8, 'edge_type_9': edge_type_9, 'edge_weight': edge_weight, 'edge_weight1': edge_weight1, 'L0_gnn_weight': _L0_gnn_in['weight'], 'L0_gnn_gate_weight': _L0_gnn_in['gate_weight'], 'L1_gnn_We1': _L1_gnn_in['We1'], 'L1_gnn_be1': _L1_gnn_in['be1'], 'L1_gnn_We2': _L1_gnn_in['We2'], 'L1_gnn_be2': _L1_gnn_in['be2'], 'L1_gnn_Wt': _L1_gnn_in['Wt'], 'L1_gnn_bt': _L1_gnn_in['bt'], 'L1_gnn_Wn1': _L1_gnn_in['Wn1'], 'L1_gnn_bn1': _L1_gnn_in['bn1'], 'L1_gnn_Wn2': _L1_gnn_in['Wn2'], 'L1_gnn_bn2': _L1_gnn_in['bn2'], 'L2_gnn_W_msg': _L2_gnn_in['W_msg'], 'L2_gnn_b_msg': _L2_gnn_in['b_msg'], 'L2_gnn_edge_embed': _L2_gnn_in['edge_embed'], 'L2_gnn_W_ih': _L2_gnn_in['W_ih'], 'L2_gnn_W_hh': _L2_gnn_in['W_hh'], 'L2_gnn_b_ih': _L2_gnn_in['b_ih'], 'L2_gnn_b_hh': _L2_gnn_in['b_hh'], 'L3_gnn_W1': _L3_gnn_in['W1'], 'L3_gnn_b1': _L3_gnn_in['b1'], 'L3_gnn_W2': _L3_gnn_in['W2'], 'L3_gnn_b2': _L3_gnn_in['b2'], 'L3_gnn_W3': _L3_gnn_in['W3'], 'L3_gnn_b3': _L3_gnn_in['b3']}

def reference(x, src, dst, edge_attr_64, edge_type_8, edge_type_9, edge_weight, edge_weight1, L0_gnn_weight, L0_gnn_gate_weight, L1_gnn_We1, L1_gnn_be1, L1_gnn_We2, L1_gnn_be2, L1_gnn_Wt, L1_gnn_bt, L1_gnn_Wn1, L1_gnn_bn1, L1_gnn_Wn2, L1_gnn_bn2, L2_gnn_W_msg, L2_gnn_b_msg, L2_gnn_edge_embed, L2_gnn_W_ih, L2_gnn_W_hh, L2_gnn_b_ih, L2_gnn_b_hh, L3_gnn_W1, L3_gnn_b1, L3_gnn_W2, L3_gnn_b2, L3_gnn_W3, L3_gnn_b3):
    import jax
    import jax.numpy as jnp

    def _L0_gnn_ref(h, weight, gate_weight, norm, src, dst, rel_type):
        import jax, jax.numpy as jnp
        import numpy as np
        N_NODES = 6250
        N_EDGES = 37500
        FEAT = 128
        N_RELS = 8
        h_all = jnp.einsum('nd,rdf->nrf', h, weight)
        gate_all = jnp.einsum('nd,rdo->nro', h, gate_weight)[..., 0]
        msg = h_all[src, rel_type] * norm
        gate = jax.nn.sigmoid(gate_all[src, rel_type])[:, None]
        msg = msg * gate
        out = jax.ops.segment_sum(msg, dst, num_segments=h.shape[0])
        return jax.nn.relu(out)

    def _L1_gnn_ref(x, edge_index, edge_attr, timestamps, We1, be1, We2, be2, Wt, bt, Wn1, bn1, Wn2, bn2):
        import jax, jax.numpy as jnp
        import numpy as np
        N_NODES = 6250
        N_EDGES = 31250
        IN_CH = 128
        EDGE_CH = 64

        def _glorot(key, shape):
            fan_in, fan_out = (shape[0], shape[1])
            lim = (6.0 / (fan_in + fan_out)) ** 0.5
            return jax.random.uniform(key, shape, jnp.float32, -lim, lim)
        ts = timestamps[:, None]
        ef = jax.nn.relu(edge_attr @ We1 + be1) @ We2 + be2
        tw = jax.nn.sigmoid(ts @ Wt + bt)
        ef = ef * tw
        row, col = (edge_index[0], edge_index[1])
        combined = jnp.concatenate([x[row], ef], axis=1)
        msg = jax.nn.relu(combined @ Wn1 + bn1) @ Wn2 + bn2
        out = jax.ops.segment_sum(msg, col, num_segments=x.shape[0])
        return out + x

    def _L2_gnn_ref(h, edge_index, edge_type, num_nodes, W_msg, b_msg, edge_embed, W_ih, W_hh, b_ih, b_hh):
        import jax, jax.numpy as jnp
        import numpy as np
        NUM_EDGE_TYPES = 8
        HIDDEN = 128
        N_NODES = 3125
        N_EDGES = 37500

        def _gru_cell(x, h, W_ih, W_hh, b_ih, b_hh):
            H = h.shape[-1]
            gi = x @ W_ih.T + b_ih
            gh = h @ W_hh.T + b_hh
            i_r, i_z, i_n = (gi[:, :H], gi[:, H:2 * H], gi[:, 2 * H:])
            h_r, h_z, h_n = (gh[:, :H], gh[:, H:2 * H], gh[:, 2 * H:])
            r = jax.nn.sigmoid(i_r + h_r)
            z = jax.nn.sigmoid(i_z + h_z)
            n = jnp.tanh(i_n + r * h_n)
            return (1.0 - z) * n + z * h
        src = edge_index[0]
        dst = edge_index[1]
        src_h = h[src] @ W_msg.T + b_msg
        emb = edge_embed[jnp.clip(edge_type, 0, NUM_EDGE_TYPES)]
        msg = src_h + emb
        messages = jax.ops.segment_sum(msg, dst, num_segments=num_nodes)
        h_new = _gru_cell(messages, h[:num_nodes], W_ih, W_hh, b_ih, b_hh)
        result = jnp.zeros_like(h).at[:num_nodes].set(h_new)
        return result

    def _L3_gnn_ref(x, edge_index, W1, b1, W2, b2, W3, b3):
        import jax, jax.numpy as jnp
        import numpy as np
        N = 3125
        E = 37500
        IN_DIM = 128
        HID = 128

        def gcn_conv(x, edge_index, W, b):
            n = x.shape[0]
            loop = jnp.arange(n, dtype=edge_index.dtype)
            src = jnp.concatenate([edge_index[0], loop])
            dst = jnp.concatenate([edge_index[1], loop])
            deg = jax.ops.segment_sum(jnp.ones(src.shape[0], dtype=x.dtype), dst, num_segments=n)
            dinv = jnp.where(deg > 0, jax.lax.rsqrt(jnp.maximum(deg, 1.0)), 0.0)
            norm = dinv[src] * dinv[dst]
            h = x @ W.T
            msg = h[src] * norm[:, None]
            out = jax.ops.segment_sum(msg, dst, num_segments=n)
            return out + b
        h = jax.nn.relu(gcn_conv(x, edge_index, W1, b1))
        h = jax.nn.relu(gcn_conv(h, edge_index, W2, b2))
        return gcn_conv(h, edge_index, W3, b3)
    edge_index = jnp.stack([src, dst])
    h = jnp.maximum(_layernorm(x, axis=-1), 0.0)
    x = x + _L0_gnn_ref(h, L0_gnn_weight, L0_gnn_gate_weight, edge_weight1, src, dst, edge_type_8)
    h = jnp.maximum(_layernorm(x, axis=-1), 0.0)
    x = x + _L1_gnn_ref(h, edge_index, edge_attr_64, edge_weight, L1_gnn_We1, L1_gnn_be1, L1_gnn_We2, L1_gnn_be2, L1_gnn_Wt, L1_gnn_bt, L1_gnn_Wn1, L1_gnn_bn1, L1_gnn_Wn2, L1_gnn_bn2)
    h = jnp.maximum(_layernorm(x, axis=-1), 0.0)
    x = x + _L2_gnn_ref(h, edge_index, edge_type_9, 6250, L2_gnn_W_msg, L2_gnn_b_msg, L2_gnn_edge_embed, L2_gnn_W_ih, L2_gnn_W_hh, L2_gnn_b_ih, L2_gnn_b_hh)
    h = jnp.maximum(_layernorm(x, axis=-1), 0.0)
    x = x + _L3_gnn_ref(h, edge_index, L3_gnn_W1, L3_gnn_b1, L3_gnn_W2, L3_gnn_b2, L3_gnn_W3, L3_gnn_b3)
    return x

_drawn_inputs = setup_inputs


def setup_inputs(seed=0):
    import zlib

    import numpy as np

    out = dict(_drawn_inputs(seed))
    spreads = {'L1_gnn_be1': (0.0, 0.358),
     'L1_gnn_be2': (0.0, 0.1),
     'L1_gnn_bt': (0.0, 2.0),
     'L1_gnn_bn1': (0.0, 0.1),
     'L1_gnn_bn2': (0.0, 0.1),
     'L3_gnn_b1': (0.0, 0.8),
     'L3_gnn_b2': (0.0, 0.8),
     'L3_gnn_b3': (0.0, 2.0)}
    factors = {'edge_weight': 200.0,
     'L1_gnn_Wt': 7.492,
     'L2_gnn_b_msg': 14.329,
     'L2_gnn_W_hh': 25.78,
     'L2_gnn_b_ih': 64.0,
     'L2_gnn_b_hh': 200.0,
     'L3_gnn_W1': 8.0,
     'L3_gnn_W2': 8.0,
     'L3_gnn_W3': 8.0}
    for name, (base, spread) in spreads.items():
        noise = np.random.default_rng([zlib.crc32(name.encode()), seed]).standard_normal(out[name].shape)
        drawn = base * np.exp(spread * noise) if base else spread * noise
        out[name] = jnp.asarray(drawn.astype(out[name].dtype))
    for name, factor in factors.items():
        out[name] = (out[name] * factor).astype(out[name].dtype)
    return out
```

```python
import concourse.bass as bass
from concourse import mybir
from contextlib import ExitStack

F32 = mybir.dt.float32
I32 = mybir.dt.int32
ALU = mybir.AluOpType
ACT = mybir.ActivationFunctionType
AXX = mybir.AxisListType.X

P = 128
N = 6250
E = 206250
D = 128
NT = -(-N // P)
NP = NT * P
J = 4
CH = J * P
NB = 4
ROUNDS = -(-E // (CH * NB))
NC = ROUNDS * NB
EP = NC * CH
COLS = EP // P
W = 64
ACCW = NP + W
R = 8
NTYPE = 9
TP = 16
EC = 64
EPS = 1e-5
BANK = 512


def bass_gnn(nc, A):
    root = ExitStack()
    with root:
        used = []

        def sem(stack, name):
            used.append(stack.enter_context(nc.semaphore(name)))
            return used[-1]

        def clear_semaphores():
            for one in used:
                nc.gpsimd.sem_clear(one)
            used.clear()
            nc.all_engine_barrier()

        def sbuf(stack, name, shape, dt=F32):
            return stack.enter_context(nc.sbuf_tensor(name, shape, dt))

        def psum(stack, name, shape=(P, BANK), dt=F32):
            return stack.enter_context(nc.psum_tensor(name, list(shape), dt))

        x = sbuf(root, "x", [P, NT, D])
        acc = sbuf(root, "acc", [P, ACCW])
        typeT = sbuf(root, "typeT", [TP, ACCW])
        dst_rel = sbuf(root, "dst_rel", [P, COLS])
        src_idx = sbuf(root, "src_idx", [P, COLS], I32)
        meta = sbuf(root, "meta", [1, ROUNDS, 2, NB], I32)
        ident = sbuf(root, "ident", [P, P])
        iota_w = sbuf(root, "iota_w", [P, W])
        neg_w = sbuf(root, "neg_w", [P, NP // W + 2])
        mean = sbuf(root, "mean", [P, NT])
        ssq = sbuf(root, "ssq", [P, NT])
        var = sbuf(root, "var", [P, NT])
        std = sbuf(root, "std", [P, NT])
        rstd = sbuf(root, "rstd", [P, NT])
        dinv = sbuf(root, "dinv", [P, NT])
        square = sbuf(root, "square", [P, 2, D])
        ones = sbuf(root, "ones", [P, P])

        def norm_sems(st, tag):
            return {n: sem(st, f"{tag}_{n}") for n in
                    ("summed", "mean", "centered", "squared", "var", "std", "rstd", "h")}

        def norm_vector(dve, s, h, extra_scale=None):
            nc.vector.tensor_reduce(mean[:, :], x[:, :, :], AXX, ALU.add).then_inc(s["summed"], 1)
            dve.wait_ge(s["summed"], 1)
            nc.vector.tensor_scalar(mean[:, :], mean[:, :], 1.0 / D, None, ALU.mult).then_inc(s["mean"], 1)
            dve.wait_ge(s["mean"], 1)
            with dve.Fori(0, NT) as t:
                nc.vector.tensor_scalar(h[:, bass.ds(t, 1), :], x[:, bass.ds(t, 1), :],
                                        mean[:, bass.ds(t, 1)], None, ALU.subtract).then_inc(s["centered"], 1)
            dve.wait_ge(s["squared"], NT + 2)
            nc.vector.tensor_scalar(var[:, :], ssq[:, :], 1.0 / D, EPS, ALU.mult, ALU.add).then_inc(s["var"], 1)
            dve.wait_ge(s["std"], 1)
            nc.vector.reciprocal(rstd[:, :], std[:, :]).then_inc(s["rstd"], 1)
            if extra_scale is not None:
                dve.wait_ge(s["rstd"], 1)
                nc.vector.tensor_tensor(rstd[:, :], rstd[:, :], extra_scale[:, :], ALU.mult).then_inc(s["rstd"], 1)

        def norm_scalar(act, s, h, scalings=1):
            act.sem_inc(s["squared"], 2)
            with act.Fori(0, NT) as t:
                act.wait_ge(s["squared"], t + 1)
                act.wait_ge(s["centered"], t + 1)
                nc.scalar.activation(square[:, bass.ds(t & 1, 1), :], h[:, bass.ds(t, 1), :], ACT.Square,
                                     accum_out=ssq[:, bass.ds(t, 1)]).then_inc(s["squared"], 1)
            act.wait_ge(s["var"], 1)
            nc.scalar.activation(std[:, :], var[:, :], ACT.Sqrt).then_inc(s["std"], 1)
            act.wait_ge(s["rstd"], scalings)
            with act.Fori(0, NT) as t:
                nc.scalar.activation(h[:, bass.ds(t, 1), :], h[:, bass.ds(t, 1), :], ACT.Relu,
                                     scale=rstd[:, bass.ds(t, 1)]).then_inc(s["h"], 1)

        def window_tensor(pe, s, q, span, rows, onehot, win, counts=None):
            pe.sem_inc(s["summing"], 1)
            with pe.Fori(0, (span >> 6) + 1):
                n = pe.snap(q, min_val=0, max_val=1 << 24)
                pe.wait_ge(s["onehot"], n + 1)
                pe.wait_ge(s["added"], n + 1)
                for j in range(J):
                    last = nc.tensor.matmul(win[:, 0:W], rows[:, j, :], onehot[:, j, :],
                                            start=(j == 0), stop=(j == J - 1))
                if counts is not None:
                    for j in range(J):
                        last = nc.tensor.matmul(win[0:TP, W:2 * W], counts[:, j, :], onehot[:, j, :],
                                                start=(j == 0), stop=(j == J - 1))
                last.then_inc(s["window"], 1)
                pe.reg_add(q, q, 1)

        def window_vector(dve, s, q, first, chunk, least, span, onehot, win, weight=None, counts=False):
            cols = dst_rel[:, bass.ds(chunk * J, J)].unsqueeze(2).to_broadcast([P, J, W])
            dve.reg_mov(first, least)
            with dve.Fori(0, (span >> 6) + 1) as w:
                n = dve.snap(q, min_val=0, max_val=1 << 24)
                made = nc.vector.scalar_tensor_tensor(
                    onehot[:, :, :], cols, neg_w[:, bass.ds(w, 1)],
                    iota_w[:, :].unsqueeze(1).to_broadcast([P, J, W]), ALU.add, ALU.is_equal)
                if weight is None:
                    made.then_inc(s["onehot"], 1)
                else:
                    made.then_inc(s["compared"], 1)
                    dve.wait_ge(s["compared"], n + 1)
                    nc.vector.tensor_tensor(onehot[:, :, :], onehot[:, :, :],
                                            weight[:, bass.ds(chunk * J, J)].unsqueeze(2)
                                            .to_broadcast([P, J, W]), ALU.mult).then_inc(s["onehot"], 1)
                dve.wait_ge(s["window"], n + 1)
                at = dve.snap(first, min_val=0, max_val=NP)
                if counts:
                    nc.vector.tensor_tensor(typeT[:, bass.ds(at, W)], typeT[:, bass.ds(at, W)],
                                            win[0:TP, W:2 * W], ALU.add)
                nc.vector.tensor_tensor(acc[:, bass.ds(at, W)], acc[:, bass.ds(at, W)],
                                        win[:, 0:W], ALU.add).then_inc(s["added"], 1)
                dve.wait_ge(s["added"], n + 2)
                dve.reg_add(q, q, 1)
                dve.reg_add(first, first, W)
            dve.sem_inc(s["chunk_done"], 1)

        def round_meta(eng, regs, o):
            eng.load(regs, meta[0:1, bass.ds(o, 1), :, :].rearrange("a b c d -> a (b c d)"))
            v = [eng.snap(r, min_val=0, max_val=NP - 1) for r in regs]
            return v[:NB], v[NB:]

        rows_in = [root.enter_context(nc.semaphore(f"rows_in{b}")) for b in range(NB)]
        passes = []

        def gathers():
            passes.append(len(passes) * 16 * J * ROUNDS)
            return passes[-1]

        def aggregate(tag, table, index, weight=None, keep_acc=False):
            with ExitStack() as st:
                rows = sbuf(st, f"{tag}_rows", [P, NB, J, D])
                staged = sbuf(st, f"{tag}_staged", [P, NB, J], I32)
                onehot = sbuf(st, f"{tag}_onehot", [P, J, W])
                win = psum(st, f"{tag}_win")
                s = {n: sem(st, f"{tag}_{n}") for n in
                     ("onehot", "added", "window", "compared", "cleared", "chunk_done", "begun", "summing")}
                index_in = [sem(st, f"{tag}_index{b}") for b in range(NB)]
                base = gathers()
                st.callback(clear_semaphores)
                block = st.enter_context(nc.Block())

                @block.sync
                def _(sp):
                    def load(b, c):
                        sp.dma_start(staged[:, b, :], index[:, bass.ds(c * J, J)]).then_inc(index_in[b], 16)
                    for b in range(NB):
                        load(b, b)
                    with sp.Fori(1, ROUNDS) as o:
                        for b in range(NB):
                            sp.wait_ge(rows_in[b], base + 16 * J * o)
                            load(b, o * NB + b)

                @block.gpsimd
                def _(pool):
                    with pool.Fori(0, ROUNDS) as o:
                        for b in range(NB):
                            pool.wait_ge(index_in[b], 16 * o + 16)
                            pool.wait_ge(s["chunk_done"], o * NB + b + 1)
                            pool.sem_inc(s["begun"], 1)
                            for j in range(J):
                                pool.indirect_dma_start(
                                    rows[:, b, j, :], None, table,
                                    bass.IndirectOffsetOnAxis(ap=staged[:, b, j:j + 1], axis=0),
                                ).then_inc(rows_in[b], 16)

                @block.tensor
                def _(pe):
                    q = pe.alloc_register(f"{tag}_pe_q")
                    regs = [pe.alloc_register(f"{tag}_pe_m{k}") for k in range(2 * NB)]
                    pe.reg_mov(q, 0)
                    with pe.Fori(0, ROUNDS) as o:
                        _, span = round_meta(pe, regs, o)
                        for b in range(NB):
                            pe.wait_ge(rows_in[b], base + 16 * J * o + 16 * J)
                            window_tensor(pe, s, q, span[b], rows[:, b, :, :], onehot, win)

                @block.vector
                def _(dve):
                    q = dve.alloc_register(f"{tag}_dve_q")
                    first = dve.alloc_register(f"{tag}_dve_first")
                    regs = [dve.alloc_register(f"{tag}_dve_m{k}") for k in range(2 * NB)]
                    nc.vector.memset(acc[:, NP if keep_acc else 0:ACCW], 0.0).then_inc(s["cleared"], 1)
                    dve.wait_ge(s["cleared"], 1)
                    dve.reg_mov(q, 0)
                    dve.sem_inc(s["added"], 1)
                    dve.sem_inc(s["chunk_done"], NB)
                    with dve.Fori(0, ROUNDS) as o:
                        least, span = round_meta(dve, regs, o)
                        for b in range(NB):
                            window_vector(dve, s, q, first, o * NB + b, least[b], span[b], onehot, win, weight)

        with ExitStack() as l0:
            weight0 = sbuf(l0, "weight0", [P, COLS])
            idx8 = sbuf(l0, "idx8", [P, COLS], I32)
            rel = sbuf(l0, "rel", [P, COLS], I32)
            w0 = sbuf(l0, "w0", [P, R * D])
            g0 = sbuf(l0, "g0", [P, R])
            with ExitStack() as st:
                dst_rows = sbuf(st, "dst_rows", [ROUNDS, NB, CH], I32)
                dst_cols = sbuf(st, "dst_cols", [P, NC, J], I32)
                base = sbuf(st, "base", [P, NC], I32)
                low = sbuf(st, "low", [ROUNDS, 2, NB], I32)
                high = sbuf(st, "high", [ROUNDS, NB], I32)
                s_rows, s_cols, s_src, s_rel, s_x, s_w = (sem(st, f"in_{n}") for n in
                                                          ("rows", "cols", "src", "rel", "x", "w"))
                s_low, s_high, s_span, s_meta_out, s_meta_in, s_base_in, s_ready, s_id, s_neg = (
                    sem(st, f"setup_{n}") for n in
                    ("low", "high", "span", "meta_out", "meta_in", "base_in", "ready", "id", "neg"))
                st.callback(clear_semaphores)
                block = st.enter_context(nc.Block())

                @block.sync
                def _(sp):
                    sp.dma_start(dst_rows[:, :, :], A["dst_rows"].rearrange("(p k) e -> p k e", k=NB)).then_inc(s_rows, 16)
                    sp.dma_start(dst_cols[:, :, :].rearrange("p c j -> p (c j)"), A["dst_cols"]).then_inc(s_cols, 16)
                    sp.dma_start(src_idx[:, :], A["src_cols"]).then_inc(s_src, 16)
                    sp.dma_start(rel[:, :], A["rel_cols"]).then_inc(s_rel, 16)
                    sp.wait_ge(s_span, 1)
                    sp.dma_start(A["meta"].rearrange("(r a) b -> r (a b)", a=2),
                                 low[:, :, :].rearrange("r a b -> r (a b)")).then_inc(s_meta_out, 16)
                    sp.wait_ge(s_meta_out, 16)
                    m = A["meta"].rearrange("(r a) b -> r a b", a=2)
                    sp.dma_start(meta[:, :, :, :], m.unsqueeze(0)).then_inc(s_meta_in, 16)
                    sp.dma_start(base[:, :].rearrange("p (r b) -> p r b", b=NB),
                                 m[:, 0, :].unsqueeze(0).to_broadcast([P, ROUNDS, NB])).then_inc(s_base_in, 16)
                    sp.wait_ge(s_meta_in, 16)

                @block.scalar
                def _(act):
                    act.dma_start(x[:, :, :], A["x"].rearrange("(t p) d -> p t d", p=P)).then_inc(s_x, 16)
                    act.dma_start(w0[:, :].rearrange("p (r d) -> p r d", r=R), A["w0"].rearrange("r k d -> k r d")).then_inc(s_w, 16)
                    with nc.allow_non_contiguous_dma(reason="1024 gate weights, once"):
                        act.dma_start(g0[:, :], A["g0"].rearrange("r k a -> k (r a)")).then_inc(s_w, 16)
                    act.dma_start(weight0[:, :], A["weight_cols"]).then_inc(s_w, 16)
                    act.wait_ge(s_x, 16)
                    act.wait_ge(s_w, 48)

                @block.gpsimd
                def _(pool):
                    pool.memset(ident[:, :], 0.0).then_inc(s_id, 1)
                    pool.memset(ones[:, :], 1.0).then_inc(s_id, 1)
                    pool.wait_ge(s_id, 2)
                    pool.affine_select(out=ident[:, :], in_=ident[:, :], compare_op=ALU.not_equal, fill=1.0,
                                       base=0, pattern=[[-1, P]], channel_multiplier=1).then_inc(s_id, 1)
                    pool.iota(iota_w[:, :], pattern=[[1, W]], base=0, channel_multiplier=0,
                              allow_small_or_imprecise_dtypes=True).then_inc(s_id, 1)
                    pool.iota(neg_w[:, :], pattern=[[-W, NP // W + 2]], base=0, channel_multiplier=0,
                              allow_small_or_imprecise_dtypes=True).then_inc(s_id, 1)
                    pool.wait_ge(s_id, 5)

                @block.vector
                def _(dve):
                    dve.wait_ge(s_rows, 16)
                    nc.vector.tensor_reduce(low[:, 0, :], dst_rows[:, :, :], AXX, ALU.min).then_inc(s_low, 1)
                    nc.vector.tensor_reduce(high[:, :], dst_rows[:, :, :], AXX, ALU.max).then_inc(s_high, 1)
                    dve.wait_ge(s_low, 1)
                    dve.wait_ge(s_high, 1)
                    nc.vector.tensor_tensor(low[:, 1, :], high[:, :], low[:, 0, :], ALU.subtract).then_inc(s_span, 1)
                    dve.wait_ge(s_src, 16)
                    dve.wait_ge(s_rel, 16)
                    nc.vector.scalar_tensor_tensor(idx8[:, :], src_idx[:, :], float(R), rel[:, :],
                                                   ALU.mult, ALU.add).then_inc(s_ready, 1)
                    dve.wait_ge(s_cols, 16)
                    dve.wait_ge(s_base_in, 16)
                    nc.vector.tensor_tensor(dst_rel[:, :].rearrange("p (c j) -> p c j", j=J), dst_cols[:, :, :],
                                            base[:, :].unsqueeze(2).to_broadcast([P, NC, J]),
                                            ALU.subtract).then_inc(s_ready, 1)
                    dve.wait_ge(s_ready, 2)

            with ExitStack() as st:
                h = sbuf(st, "h0", [P, NT, D])
                hT = sbuf(st, "h0T", [P, 2, P])
                gate = sbuf(st, "gate", [P, 2, R])
                out = sbuf(st, "table0_tile", [P, 2, R, D])
                pT = psum(st, "pT", [P, 2, BANK])
                pW = psum(st, "pW", [P, 4, BANK])
                pG = psum(st, "pG", [P, 2, BANK])
                s = norm_sems(st, "n0")
                s_T, s_hT, s_prod, s_gate, s_out = (sem(st, f"n0_{n}") for n in ("T", "hT", "prod", "gate", "out"))
                s_store = [sem(st, f"n0_store{k}") for k in range(2)]
                st.callback(clear_semaphores)
                block = st.enter_context(nc.Block())
                steps = range(NT)

                @block.vector
                def _(dve):
                    norm_vector(dve, s, h)
                    for t in steps:
                        if t >= 2:
                            dve.wait_ge(s_store[t % 2], 16 * (t // 2))
                        dve.wait_ge(s_gate, t + 1)
                        for k in range(2):
                            last = nc.vector.tensor_tensor(
                                out[:, t % 2, 4 * k:4 * k + 4, :],
                                pW[:, 2 * (t % 2) + k, :].rearrange("p (r d) -> p r d", d=D),
                                gate[:, t % 2, 4 * k:4 * k + 4].unsqueeze(2).to_broadcast([P, 4, D]), ALU.mult)
                        last.then_inc(s_out, 1)

                @block.scalar
                def _(act):
                    norm_scalar(act, s, h)
                    for t in steps:
                        act.wait_ge(s_T, t + 1)
                        if t >= 2:
                            act.wait_ge(s_prod, t - 1)
                        nc.scalar.activation(hT[:, t % 2, :], pT[:, t % 2, 0:P], ACT.Copy).then_inc(s_hT, 1)
                        act.wait_ge(s_prod, t + 1)
                        if t >= 2:
                            act.wait_ge(s_out, t - 1)
                        nc.scalar.activation(gate[:, t % 2, :], pG[:, t % 2, 0:R], ACT.Sigmoid).then_inc(s_gate, 1)

                @block.tensor
                def _(pe):
                    pe.wait_ge(s["h"], NT)
                    for t in range(NT + 1):
                        if t < NT:
                            if t >= 2:
                                pe.wait_ge(s_hT, t - 1)
                            nc.tensor.transpose(pT[:, t % 2, 0:P], h[:, t, :], ident[:, :]).then_inc(s_T, 1)
                        if t >= 1:
                            u = t - 1
                            pe.wait_ge(s_hT, u + 1)
                            if u >= 2:
                                pe.wait_ge(s_out, u - 1)
                            for k in range(2):
                                nc.tensor.matmul(pW[:, 2 * (u % 2) + k, :], hT[:, u % 2, :],
                                                 w0[:, k * BANK:(k + 1) * BANK], start=True, stop=True)
                            nc.tensor.matmul(pG[:, u % 2, 0:R], hT[:, u % 2, :], g0[:, :],
                                             start=True, stop=True).then_inc(s_prod, 1)

                @block.sync
                def _(sp):
                    for t in steps:
                        sp.wait_ge(s_out, t + 1)
                        sp.dma_start(A["table0"][t * P * R:(t + 1) * P * R, :].rearrange("(p r) d -> p (r d)", r=R),
                                     out[:, t % 2, :, :].rearrange("p r d -> p (r d)")).then_inc(s_store[t % 2], 16)
                    for k in range(2):
                        sp.wait_ge(s_store[k], 16 * len(range(k, NT, 2)))

            aggregate("e0", A["table0"], idx8, weight0)

        w_l1 = ExitStack()
        root.enter_context(w_l1)
        wn1a = sbuf(w_l1, "wn1a", [P, D])
        wn1b = sbuf(w_l1, "wn1b", [P, D])
        wn2 = sbuf(w_l1, "wn2", [P, D])
        we1 = sbuf(w_l1, "we1", [EC, D])
        we2 = sbuf(w_l1, "we2", [P, D])
        cols1 = sbuf(w_l1, "cols1", [P, 4])
        bn1_row = sbuf(w_l1, "bn1_row", [P, D])
        bn2_row = sbuf(w_l1, "bn2_row", [TP, D])

        with ExitStack() as st:
            h = sbuf(st, "h1", [P, NT, D])
            hT = sbuf(st, "h1T", [P, 2, P])
            relu_sum = sbuf(st, "relu_sum", [P, 2, D])
            pT = psum(st, "p1T", [P, 2, BANK])
            pU = psum(st, "p1U", [P, 2, BANK])
            pO = psum(st, "p1O", [P, 2, BANK])
            s = norm_sems(st, "n1")
            s_w, s_T, s_relu, s_x, s_U, s_hT, s_prod, s_out, s_store, s_xh, s_w2 = (
                sem(st, f"n1_{n}") for n in ("w", "T", "relu", "x", "U", "hT", "prod", "out", "store", "xh", "w2"))
            st.callback(clear_semaphores)
            block = st.enter_context(nc.Block())

            @block.sync
            def _(sp):
                sp.dma_start(wn1a[:, :], A["wn1"][0:D, :]).then_inc(s_w, 16)
                sp.dma_start(wn1b[:, :], A["wn1"][D:2 * D, :]).then_inc(s_w, 16)
                sp.dma_start(wn2[:, :], A["wn2"]).then_inc(s_w, 16)
                sp.dma_start(we1[:, :], A["we1"]).then_inc(s_w, 16)
                sp.dma_start(we2[:, :], A["we2"]).then_inc(s_w, 16)
                sp.dma_start(bn1_row[:, :], A["bn1"].unsqueeze(0).to_broadcast([P, D])).then_inc(s_w, 16)
                sp.dma_start(bn2_row[:, :], A["bn2"].unsqueeze(0).to_broadcast([TP, D])).then_inc(s_w, 16)
                with nc.allow_non_contiguous_dma(reason="four columns of biases, once"):
                    for k, name in enumerate(("be1", "be2", "wt", "bt")):
                        sp.dma_start(cols1[:, k:k + 1], A[name].unsqueeze(1)).then_inc(s_w2, 16)
                sp.wait_ge(s_w, 112)
                sp.wait_ge(s_w2, 64)
                sp.wait_ge(s_out, NT)
                sp.dma_start(A["table1"].rearrange("(t p) d -> p t d", p=P), h[:, :, :]).then_inc(s_store, 16)
                sp.wait_ge(s_store, 16)

            @block.tensor
            def _(pe):
                for t in range(NT):
                    if t >= 2:
                        pe.wait_ge(s_relu, t - 1)
                    nc.tensor.transpose(pT[:, t % 2, 0:P], acc[:, t * P:(t + 1) * P], ident[:, :]).then_inc(s_T, 1)
                pe.wait_ge(s["h"], NT)
                pe.wait_ge(s_w, 112)
                for t in range(NT + 1):
                    if t < NT:
                        if t >= 2:
                            pe.wait_ge(s_hT, t - 1)
                        nc.tensor.transpose(pU[:, t % 2, 0:P], h[:, t, :], ident[:, :]).then_inc(s_U, 1)
                    if t >= 1:
                        u = t - 1
                        pe.wait_ge(s_hT, u + 1)
                        if u >= 2:
                            pe.wait_ge(s_out, u - 1)
                        nc.tensor.matmul(pO[:, u % 2, 0:D], hT[:, u % 2, :], wn1a[:, :],
                                         start=True, stop=True).then_inc(s_prod, 1)

            @block.scalar
            def _(act):
                for t in range(NT):
                    act.wait_ge(s_T, t + 1)
                    if t >= 2:
                        act.wait_ge(s_x, t - 1)
                    nc.scalar.activation(relu_sum[:, t % 2, :], pT[:, t % 2, 0:D], ACT.Relu).then_inc(s_relu, 1)
                norm_scalar(act, s, h)
                for t in range(NT):
                    act.wait_ge(s_U, t + 1)
                    if t >= 2:
                        act.wait_ge(s_prod, t - 1)
                    nc.scalar.activation(hT[:, t % 2, :], pU[:, t % 2, 0:P], ACT.Copy).then_inc(s_hT, 1)

            @block.vector
            def _(dve):
                for t in range(NT):
                    dve.wait_ge(s_relu, t + 1)
                    nc.vector.tensor_tensor(x[:, t, :], x[:, t, :], relu_sum[:, t % 2, :], ALU.add).then_inc(s_x, 1)
                dve.wait_ge(s_x, NT)
                norm_vector(dve, s, h)
                dve.wait_ge(s["h"], NT)
                nc.vector.tensor_tensor(x[:, :, :], x[:, :, :], h[:, :, :], ALU.add).then_inc(s_xh, 1)
                dve.wait_ge(s_xh, 1)
                for t in range(NT):
                    dve.wait_ge(s_prod, t + 1)
                    nc.vector.tensor_tensor(h[:, t, :], pO[:, t % 2, 0:D], bn1_row[:, :], ALU.add).then_inc(s_out, 1)

        with ExitStack() as st:
            type_f = sbuf(st, "type_f", [P, COLS])
            type_i = sbuf(st, "type_i", [P, COLS], I32)
            rows = sbuf(st, "e1_rows", [P, NB, J, D])
            staged = sbuf(st, "e1_staged", [P, NB, J], I32)
            onehot = sbuf(st, "e1_onehot", [P, J, W])
            oh_type = sbuf(st, "e1_oh_type", [P, 2, J, TP])
            edge_in = sbuf(st, "e1_edge", [EC, NB, CH])
            time_in = sbuf(st, "e1_time", [P, NB, CH])
            hid = sbuf(st, "e1_hid", [P, 2, CH])
            tw = sbuf(st, "e1_tw", [P, 2, CH])
            ef = sbuf(st, "e1_ef", [P, 2, CH])
            z = sbuf(st, "e1_z", [P, 2, CH])
            msg = sbuf(st, "e1_msg", [P, 2, J, D])
            win = psum(st, "e1_win")
            p1 = psum(st, "e1_p1", [P, 2, BANK])
            p2 = psum(st, "e1_p2", [P, 2, BANK])
            p3 = psum(st, "e1_p3", [P, 2, BANK])
            s = {n: sem(st, f"e1_{n}") for n in
                 ("onehot", "added", "window", "cleared", "chunk_done", "begun", "summing", "type", "types",
                  "p1", "hid", "p2", "tw", "ef", "p3", "z", "msg", "type_in")}
            index_in, edges_in, times_in = (
                [sem(st, f"e1_{n}{b}") for b in range(NB)] for n in ("index_in", "edges_in", "times_in"))
            base = gathers()
            st.callback(clear_semaphores)
            block = st.enter_context(nc.Block())

            LAG = 3

            def run_steps(eng, step, before_round):
                before_round(0)
                for c in range(NB):
                    step(c, c, True)
                with eng.Fori(1, ROUNDS) as o:
                    before_round(o)
                    for b in range(NB):
                        step(o * NB + b, b, False)
                before_round(None)
                for c in range(NC, NC + LAG):
                    step(c, c, True)

            def live(c, edge):
                return not edge or 0 <= c < NC

            @block.sync
            def _(sp):
                def load(b, c, o):
                    if o is not None:
                        sp.wait_ge(rows_in[b], base + 16 * J * o)
                    sp.dma_start(staged[:, b, :], src_idx[:, bass.ds(c * J, J)]).then_inc(index_in[b], 16)
                    if o is not None:
                        sp.wait_ge(s["p1"], c - (NB - 1))
                    sp.dma_start(edge_in[:, b, :], A["edge_T"][bass.ds(c, 1), :, :]
                                 .rearrange("a k e -> (a k) e")).then_inc(edges_in[b], 16)
                sp.dma_start(type_i[:, :], A["type_cols"]).then_inc(s["type_in"], 16)
                for b in range(NB):
                    load(b, b, None)
                with sp.Fori(1, ROUNDS) as o:
                    for b in range(NB):
                        load(b, o * NB + b, o)

            @block.gpsimd
            def _(pool):
                def gather(b, c, o, first):
                    pool.wait_ge(index_in[b], o * 16 + 16)
                    if not first:
                        pool.wait_ge(s["z"], c - (NB - 1))
                    pool.sem_inc(s["begun"], 1)
                    for j in range(J):
                        pool.indirect_dma_start(
                            rows[:, b, j, :], None, A["table1"],
                            bass.IndirectOffsetOnAxis(ap=staged[:, b, j:j + 1], axis=0),
                        ).then_inc(rows_in[b], 16)
                for b in range(NB):
                    gather(b, b, 0, True)
                with pool.Fori(1, ROUNDS) as o:
                    for b in range(NB):
                        gather(b, o * NB + b, o, False)

            @block.tensor
            def _(pe):
                q = pe.alloc_register("e1_pe_q")
                regs = [[pe.alloc_register(f"e1_pe_m{i}_{k}") for k in range(2 * NB)] for i in range(2)]
                pe.reg_mov(q, 0)
                spans = {}

                def before_round(o):
                    if o is None:
                        return
                    if isinstance(o, int):
                        _, spans["now"] = round_meta(pe, regs[0], 0)
                        return
                    _, spans["was"] = round_meta(pe, regs[1], o - 1)
                    _, spans["now"] = round_meta(pe, regs[0], o)

                def step(c, b, edge):
                    if live(c, edge):
                        o16 = (c // NB) * 16 + 16 if edge else None
                        pe.wait_ge(edges_in[b % NB], o16 if edge else (c - b) * 4 + 16)
                        if not edge or c >= 2:
                            pe.wait_ge(s["hid"], c - 1)
                        nc.tensor.matmul(p1[:, b % 2, :], we1[:, :], edge_in[:, b % NB, :],
                                         start=True, stop=True).then_inc(s["p1"], 1)
                    if live(c - 1, edge):
                        pe.wait_ge(s["hid"], c)
                        if not edge or c - 1 >= 2:
                            pe.wait_ge(s["ef"], c - 2)
                        nc.tensor.matmul(p2[:, (b - 1) % 2, :], we2[:, :], hid[:, (b - 1) % 2, :],
                                         start=True, stop=True).then_inc(s["p2"], 1)
                    if live(c - 2, edge):
                        pe.wait_ge(s["ef"], c - 1)
                        if not edge or c - 2 >= 2:
                            pe.wait_ge(s["z"], c - 3)
                        for j in range(J):
                            last = nc.tensor.matmul(p3[:, (b - 2) % 2, j * P:(j + 1) * P],
                                                    ef[:, (b - 2) % 2, j * P:(j + 1) * P], wn1b[:, :],
                                                    start=True, stop=True)
                        last.then_inc(s["p3"], 1)
                    if live(c - 3, edge):
                        pe.wait_ge(s["msg"], c - 2)
                        if edge:
                            span = spans["now"][(c - 3) % NB]
                        else:
                            span = spans["was"][b + 1] if b < LAG else spans["now"][0]
                        window_tensor(pe, s, q, span, msg[:, (b - 3) % 2, :, :], onehot, win,
                                      oh_type[:, (b - 3) % 2, :, :])
                run_steps(pe, step, before_round)

            @block.scalar
            def _(act):
                def load_time(c, b):
                    act.dma_start(time_in[:, b % NB, :], A["time_rows"][bass.ds(c, 1), :]
                                  .to_broadcast([P, CH])).then_inc(times_in[b % NB], 16)
                for b in range(NB - 1):
                    load_time(b, b)

                def step(c, b, edge):
                    ahead = c + NB - 1
                    if (edge and c < NB) or not edge:
                        if not edge or c >= 1:
                            act.wait_ge(s["tw"], c)
                        load_time(ahead, b + NB - 1)
                    if live(c, edge):
                        act.wait_ge(times_in[b % NB], (c // NB) * 16 + 16 if edge else (c - b) * 4 + 16)
                        if not edge or c >= 2:
                            act.wait_ge(s["ef"], c - 1)
                        nc.scalar.activation(tw[:, b % 2, :], time_in[:, b % NB, :], ACT.Sigmoid,
                                             bias=cols1[:, 3:4], scale=cols1[:, 2:3]).then_inc(s["tw"], 1)
                        act.wait_ge(s["p1"], c + 1)
                        if not edge or c >= 2:
                            act.wait_ge(s["p2"], c - 1)
                        nc.scalar.activation(hid[:, b % 2, :], p1[:, b % 2, :], ACT.Relu,
                                             bias=cols1[:, 0:1]).then_inc(s["hid"], 1)
                    if live(c - 2, edge):
                        act.wait_ge(s["z"], c - 1)
                        if not edge or c - 2 >= 2:
                            act.wait_ge(s["chunk_done"], c - 3)
                        nc.scalar.activation(msg[:, (b - 2) % 2, :, :].rearrange("p j d -> p (j d)"),
                                             z[:, (b - 2) % 2, :], ACT.Relu).then_inc(s["msg"], 1)

                for c in range(NB):
                    step(c, c, True)
                with act.Fori(1, ROUNDS - 1) as o:
                    for b in range(NB):
                        step(o * NB + b, b, False)
                for c in range(NC - NB, NC + LAG):
                    b = c
                    ahead = c + NB - 1
                    if ahead < NC:
                        act.wait_ge(s["tw"], c)
                        load_time(ahead, ahead)
                    if c < NC:
                        act.wait_ge(times_in[b % NB], (c // NB) * 16 + 16)
                        act.wait_ge(s["ef"], c - 1)
                        nc.scalar.activation(tw[:, b % 2, :], time_in[:, b % NB, :], ACT.Sigmoid,
                                             bias=cols1[:, 3:4], scale=cols1[:, 2:3]).then_inc(s["tw"], 1)
                        act.wait_ge(s["p1"], c + 1)
                        act.wait_ge(s["p2"], c - 1)
                        nc.scalar.activation(hid[:, b % 2, :], p1[:, b % 2, :], ACT.Relu,
                                             bias=cols1[:, 0:1]).then_inc(s["hid"], 1)
                    if c - 2 < NC:
                        act.wait_ge(s["z"], c - 1)
                        act.wait_ge(s["chunk_done"], c - 3)
                        nc.scalar.activation(msg[:, (b - 2) % 2, :, :].rearrange("p j d -> p (j d)"),
                                             z[:, (b - 2) % 2, :], ACT.Relu).then_inc(s["msg"], 1)

            @block.vector
            def _(dve):
                q = dve.alloc_register("e1_dve_q")
                first = dve.alloc_register("e1_dve_first")
                regs = [[dve.alloc_register(f"e1_dve_m{i}_{k}") for k in range(2 * NB)] for i in range(2)]
                nc.vector.memset(acc[:, :], 0.0).then_inc(s["cleared"], 1)
                nc.vector.memset(typeT[:, :], 0.0).then_inc(s["cleared"], 1)
                dve.wait_ge(s["type_in"], 16)
                nc.vector.tensor_scalar(type_f[:, :], type_i[:, :], 0.0, float(NTYPE - 1),
                                        ALU.max, ALU.min).then_inc(s["cleared"], 1)
                dve.wait_ge(s["cleared"], 3)
                dve.reg_mov(q, 0)
                dve.sem_inc(s["added"], 1)
                m = {}

                def before_round(o):
                    if o is None:
                        return
                    if isinstance(o, int):
                        m["now"] = round_meta(dve, regs[0], 0)
                        return
                    m["was"] = round_meta(dve, regs[1], o - 1)
                    m["now"] = round_meta(dve, regs[0], o)

                def step(c, b, edge):
                    if live(c - 1, edge):
                        dve.wait_ge(s["p2"], c)
                        dve.wait_ge(s["tw"], c)
                        if not edge or c - 1 >= 2:
                            dve.wait_ge(s["p3"], c - 2)
                        k = (b - 1) % 2
                        nc.vector.scalar_tensor_tensor(ef[:, k, :], p2[:, k, :], cols1[:, 1:2], tw[:, k, :],
                                                       ALU.add, ALU.mult).then_inc(s["ef"], 1)
                    if live(c - 2, edge):
                        dve.wait_ge(s["p3"], c - 1)
                        k = (b - 2) % 2
                        if edge:
                            dve.wait_ge(rows_in[(c - 2) % NB], base + 16 * J * ((c - 2) // NB + 1))
                        elif b >= 2:
                            dve.wait_ge(rows_in[b - 2], base + (c - b) * 16 + 64)
                        else:
                            dve.wait_ge(rows_in[b + 2], base + (c - b) * 16)
                        if not edge or c - 2 >= 2:
                            dve.wait_ge(s["msg"], c - 3)
                        nc.vector.tensor_tensor(z[:, k, :], p3[:, k, :],
                                                rows[:, (b - 2) % NB, :, :].rearrange("p j d -> p (j d)"),
                                                ALU.add).then_inc(s["z"], 1)
                    if live(c - 3, edge):
                        if edge:
                            least, span = (v[(c - 3) % NB] for v in m["now"])
                        elif b < LAG:
                            least, span = (v[b + 1] for v in m["was"])
                        else:
                            least, span = (v[0] for v in m["now"])
                        k = (b - 3) % 2
                        nc.vector.tensor_tensor(
                            oh_type[:, k, :, :], iota_w[:, 0:TP].unsqueeze(1).to_broadcast([P, J, TP]),
                            type_f[:, bass.ds((c - 3) * J, J)].unsqueeze(2).to_broadcast([P, J, TP]),
                            ALU.is_equal).then_inc(s["types"], 1)
                        window_vector(dve, s, q, first, c - 3, least, span, onehot, win, counts=True)
                run_steps(dve, step, before_round)

        hT2 = sbuf(w_l1, "hT2", [P, NP])
        h2_scope = ExitStack()
        w_l1.enter_context(h2_scope)
        h2 = sbuf(h2_scope, "h2", [P, NT, D])
        with ExitStack() as st:
            pO = psum(st, "p2O", [P, 2, BANK])
            pD = psum(st, "p2D")
            pT = psum(st, "p2T", [P, 2, BANK])
            s = norm_sems(st, "n2")
            s_O, s_x, s_D, s_deg, s_root, s_T, s_hT, s_store = (
                sem(st, f"n2_{n}") for n in ("O", "x", "D", "deg", "root", "T", "hT", "store"))
            st.callback(clear_semaphores)
            block = st.enter_context(nc.Block())

            @block.tensor
            def _(pe):
                for t in range(NT):
                    nc.tensor.matmul(pD[:, t:t + 1], typeT[:, t * P:(t + 1) * P], ones[0:TP, 0:1],
                                     start=True, stop=True).then_inc(s_D, 1)
                for t in range(NT):
                    if t >= 2:
                        pe.wait_ge(s_x, t - 1)
                    nc.tensor.matmul(pO[:, t % 2, 0:D], acc[:, t * P:(t + 1) * P], wn2[:, :], start=True, stop=False)
                    nc.tensor.matmul(pO[:, t % 2, 0:D], typeT[:, t * P:(t + 1) * P], bn2_row[:, :],
                                     start=False, stop=True).then_inc(s_O, 1)
                pe.wait_ge(s["h"], NT)
                for t in range(NT):
                    if t >= 2:
                        pe.wait_ge(s_hT, t - 1)
                    nc.tensor.transpose(pT[:, t % 2, 0:P], h2[:, t, :], ident[:, :]).then_inc(s_T, 1)

            @block.vector
            def _(dve):
                dve.wait_ge(s_D, NT)
                nc.vector.tensor_scalar(dinv[:, :], pD[:, 0:NT], 1.0, 1.0, ALU.add, ALU.max).then_inc(s_deg, 1)
                for t in range(NT):
                    dve.wait_ge(s_O, t + 1)
                    nc.vector.tensor_tensor(x[:, t, :], x[:, t, :], pO[:, t % 2, 0:D], ALU.add).then_inc(s_x, 1)
                dve.wait_ge(s_x, NT)
                norm_vector(dve, s, h2)
                dve.wait_ge(s_root, 1)
                nc.vector.reciprocal(dinv[:, :], dinv[:, :]).then_inc(s_deg, 1)
                dve.wait_ge(s_deg, 2)

            @block.scalar
            def _(act):
                act.wait_ge(s_deg, 1)
                nc.scalar.activation(dinv[:, :], dinv[:, :], ACT.Sqrt).then_inc(s_root, 1)
                norm_scalar(act, s, h2)
                for t in range(NT):
                    act.wait_ge(s_T, t + 1)
                    nc.scalar.activation(hT2[:, t * P:(t + 1) * P], pT[:, t % 2, 0:P], ACT.Copy).then_inc(s_hT, 1)
                act.wait_ge(s_hT, NT)

            @block.sync
            def _(sp):
                sp.wait_ge(s["h"], NT)
                sp.dma_start(A["table2"].rearrange("(t p) d -> p t d", p=P), h2[:, :, :]).then_inc(s_store, 16)
                sp.wait_ge(s_store, 16)

        aggregate("e2", A["table2"], src_idx)

        with ExitStack() as st:
            wmsg = sbuf(st, "wmsg", [P, D])
            emb = sbuf(st, "emb", [TP, D])
            bmsg = sbuf(st, "bmsg", [TP, D])
            wih = sbuf(st, "wih", [P, 3 * D])
            whh = sbuf(st, "whh", [P, 3 * D])
            bih = sbuf(st, "bih", [1, 3 * D])
            bhh = sbuf(st, "bhh", [1, 3 * D])
            mT = sbuf(st, "mT", [P, 2, P])
            rz = sbuf(st, "rz", [P, 2, 2 * D])
            pre = sbuf(st, "pre", [P, 2, D])
            new = sbuf(st, "new", [P, 2, D])
            diff = sbuf(st, "diff", [P, 2, D])
            pM = psum(st, "p3M", [P, 2, BANK])
            pR = psum(st, "p3R", [P, 2, BANK])
            pN = psum(st, "p3N", [P, 2, BANK])
            pT = psum(st, "p3T", [P, 2, BANK])
            s = norm_sems(st, "n3")
            s_w, s_M, s_m, s_R, s_N, s_rz, s_pre, s_new, s_x, s_T, s_acc, s_store, s_v, s_diff, s_e0 = (
                sem(st, f"n3_{n}") for n in ("w", "M", "m", "R", "N", "rz", "pre", "new", "x", "T", "acc", "store",
                                             "v", "diff", "e0"))
            st.callback(clear_semaphores)
            block = st.enter_context(nc.Block())

            @block.sync
            def _(sp):
                sp.dma_start(wmsg[:, :], A["wmsgT"]).then_inc(s_w, 16)
                sp.dma_start(emb[:, :], A["emb"]).then_inc(s_w, 16)
                sp.dma_start(bmsg[:, :], A["bmsg"].unsqueeze(0).to_broadcast([TP, D])).then_inc(s_w, 16)
                sp.dma_start(wih[:, :], A["wihT"]).then_inc(s_w, 16)
                sp.dma_start(whh[:, :], A["whhT"]).then_inc(s_w, 16)
                sp.dma_start(bih[:, :], A["bih"].unsqueeze(0)).then_inc(s_w, 16)
                sp.dma_start(bhh[:, :], A["bhh"].unsqueeze(0)).then_inc(s_w, 16)
                sp.wait_ge(s["h"], NT)
                sp.dma_start(A["table3"].rearrange("(t p) d -> p t d", p=P), h2[:, :, :]).then_inc(s_store, 16)
                sp.wait_ge(s_store, 16)

            @block.tensor
            def _(pe):
                pe.wait_ge(s_w, 112)
                for t in range(NT + 1):
                    if t < NT:
                        tile = slice(t * P, (t + 1) * P)
                        if t >= 2:
                            pe.wait_ge(s_m, t - 1)
                        nc.tensor.matmul(pM[:, t % 2, 0:P], wmsg[:, :], acc[:, tile], start=True, stop=False)
                        nc.tensor.matmul(pM[:, t % 2, 0:P], emb[:, :], typeT[:, tile], start=False, stop=False)
                        nc.tensor.matmul(pM[:, t % 2, 0:P], bmsg[:, :], typeT[:, tile],
                                         start=False, stop=True).then_inc(s_M, 1)
                    if t >= 1:
                        u = t - 1
                        k = u % 2
                        tile = slice(u * P, (u + 1) * P)
                        pe.wait_ge(s_m, u + 1)
                        if u >= 2:
                            pe.wait_ge(s_rz, u - 1)
                            pe.wait_ge(s_pre, u - 1)
                        g = slice(0, 2 * D)
                        nc.tensor.matmul(pR[:, k, 0:2 * D], mT[:, k, :], wih[:, g], start=True, stop=False)
                        nc.tensor.matmul(pR[:, k, 0:2 * D], hT2[:, tile], whh[:, g], start=False, stop=False)
                        nc.tensor.matmul(pR[:, k, 0:2 * D], ones[0:1, :], bih[:, g], start=False, stop=False)
                        nc.tensor.matmul(pR[:, k, 0:2 * D], ones[0:1, :], bhh[:, g], start=False,
                                         stop=True).then_inc(s_R, 1)
                        g = slice(2 * D, 3 * D)
                        nc.tensor.matmul(pN[:, k, 0:D], mT[:, k, :], wih[:, g], start=True, stop=False)
                        nc.tensor.matmul(pN[:, k, 0:D], ones[0:1, :], bih[:, g], start=False, stop=True)
                        nc.tensor.matmul(pN[:, k, D:2 * D], hT2[:, tile], whh[:, g], start=True, stop=False)
                        nc.tensor.matmul(pN[:, k, D:2 * D], ones[0:1, :], bhh[:, g], start=False,
                                         stop=True).then_inc(s_N, 1)
                pe.wait_ge(s["h"], NT)
                for t in range(NT):
                    if t >= 2:
                        pe.wait_ge(s_acc, t - 1)
                    nc.tensor.transpose(pT[:, t % 2, 0:P], h2[:, t, :], ident[:, :]).then_inc(s_T, 1)

            @block.scalar
            def _(act):
                for t in range(NT + 1):
                    if t < NT:
                        act.wait_ge(s_M, t + 1)
                        if t >= 2:
                            act.wait_ge(s_N, t - 1)
                        nc.scalar.activation(mT[:, t % 2, :], pM[:, t % 2, 0:P], ACT.Copy).then_inc(s_m, 1)
                    if t >= 1:
                        u = t - 1
                        k = u % 2
                        act.wait_ge(s_R, u + 1)
                        if u >= 2:
                            act.wait_ge(s_x, u - 1)
                        nc.scalar.activation(rz[:, k, :], pR[:, k, 0:2 * D], ACT.Sigmoid).then_inc(s_rz, 1)
                        act.wait_ge(s_pre, u + 1)
                        nc.scalar.activation(new[:, k, :], pre[:, k, :], ACT.Tanh).then_inc(s_new, 1)
                norm_scalar(act, s, h2, scalings=2)
                for t in range(NT):
                    act.wait_ge(s_T, t + 1)
                    nc.scalar.activation(acc[:, t * P:(t + 1) * P], pT[:, t % 2, 0:P], ACT.Copy).then_inc(s_acc, 1)
                act.wait_ge(s_acc, NT)

            @block.vector
            def _(dve):
                for u in range(NT):
                    k = u % 2
                    dve.wait_ge(s_rz, u + 1)
                    dve.wait_ge(s_N, u + 1)
                    if u >= 2:
                        dve.wait_ge(s_new, u - 1)
                    nc.vector.tensor_tensor(pre[:, k, :], rz[:, k, 0:D], pN[:, k, D:2 * D], ALU.mult).then_inc(s_v, 1)
                    dve.wait_ge(s_v, u + 1)
                    nc.vector.tensor_tensor(pre[:, k, :], pre[:, k, :], pN[:, k, 0:D], ALU.add).then_inc(s_pre, 1)
                    dve.wait_ge(s_new, u + 1)
                    nc.vector.tensor_tensor(diff[:, k, :], h2[:, u, :], new[:, k, :], ALU.subtract).then_inc(s_diff, 1)
                    nc.vector.tensor_tensor(x[:, u, :], x[:, u, :], new[:, k, :], ALU.add).then_inc(s_diff, 1)
                    dve.wait_ge(s_diff, 3 * u + 2)
                    nc.vector.tensor_tensor(diff[:, k, :], diff[:, k, :], rz[:, k, D:2 * D], ALU.mult).then_inc(s_diff, 1)
                    dve.wait_ge(s_diff, 3 * u + 3)
                    nc.vector.tensor_tensor(x[:, u, :], x[:, u, :], diff[:, k, :], ALU.add).then_inc(s_x, 1)
                dve.wait_ge(s_x, NT)
                norm_vector(dve, s, h2, extra_scale=dinv)

        for conv in range(3):
            last_conv = conv == 2
            aggregate(f"e3{conv}", A[f"table{3 + conv}"], src_idx, keep_acc=True)
            with ExitStack() as st:
                w = sbuf(st, f"c{conv}_w", [P, D])
                bias = sbuf(st, f"c{conv}_bias", [P, D])
                y = sbuf(st, f"c{conv}_y", [P, 2, D])
                pO = psum(st, f"c{conv}_pO", [P, 2, BANK])
                pT = psum(st, f"c{conv}_pT", [P, 2, BANK])
                s_w, s_O, s_y, s_h, s_T, s_acc, s_store, s_x = (
                    sem(st, f"c{conv}_{n}") for n in ("w", "O", "y", "h", "T", "acc", "store", "x"))
                st.callback(clear_semaphores)
                block = st.enter_context(nc.Block())

                @block.sync
                def _(sp):
                    sp.dma_start(w[:, :], A[f"convT{conv}"]).then_inc(s_w, 16)
                    sp.dma_start(bias[:, :], A[f"conv_b{conv}"].unsqueeze(0).to_broadcast([P, D])).then_inc(s_w, 16)
                    if last_conv:
                        sp.wait_ge(s_x, NT)
                        whole = N // P
                        sp.dma_start(A["out"][0:whole * P, :].rearrange("(t p) d -> p t d", p=P),
                                     x[:, 0:whole, :]).then_inc(s_store, 16)
                        sp.dma_start(A["out"][whole * P:N, :], x[0:N - whole * P, whole, :]).then_inc(s_store, 16)
                        sp.wait_ge(s_store, 32)
                    else:
                        sp.wait_ge(s_h, NT)
                        sp.dma_start(A[f"table{4 + conv}"].rearrange("(t p) d -> p t d", p=P),
                                     h2[:, :, :]).then_inc(s_store, 16)
                        sp.wait_ge(s_store, 16)

                @block.tensor
                def _(pe):
                    pe.wait_ge(s_w, 32)
                    for t in range(NT + 1):
                        if t < NT:
                            if t >= 2:
                                pe.wait_ge(s_y, t - 1)
                            nc.tensor.matmul(pO[:, t % 2, 0:D], acc[:, t * P:(t + 1) * P], w[:, :],
                                             start=True, stop=True).then_inc(s_O, 1)
                        if t >= 1 and not last_conv:
                            u = t - 1
                            pe.wait_ge(s_h, u + 1)
                            if u >= 2:
                                pe.wait_ge(s_acc, u - 1)
                            nc.tensor.transpose(pT[:, u % 2, 0:P], h2[:, u, :], ident[:, :]).then_inc(s_T, 1)

                @block.vector
                def _(dve):
                    dve.wait_ge(s_w, 32)
                    for t in range(NT):
                        dve.wait_ge(s_O, t + 1)
                        if t >= 2 and not last_conv:
                            dve.wait_ge(s_h, t - 1)
                        if last_conv and t >= 2:
                            dve.wait_ge(s_x, t - 1)
                        nc.vector.scalar_tensor_tensor(y[:, t % 2, :], pO[:, t % 2, 0:D], dinv[:, t:t + 1],
                                                       bias[:, :], ALU.mult, ALU.add).then_inc(s_y, 1)
                        if last_conv:
                            dve.wait_ge(s_y, t + 1)
                            nc.vector.tensor_tensor(x[:, t, :], x[:, t, :], y[:, t % 2, :], ALU.add).then_inc(s_x, 1)

                @block.scalar
                def _(act):
                    if last_conv:
                        return
                    for t in range(NT + 1):
                        if t < NT:
                            act.wait_ge(s_y, t + 1)
                            nc.scalar.activation(h2[:, t, :], y[:, t % 2, :], ACT.Relu,
                                                 scale=dinv[:, t:t + 1]).then_inc(s_h, 1)
                        if t >= 1:
                            u = t - 1
                            act.wait_ge(s_T, u + 1)
                            nc.scalar.activation(acc[:, u * P:(u + 1) * P], pT[:, u % 2, 0:P],
                                                 ACT.Copy).then_inc(s_acc, 1)
                    act.wait_ge(s_acc, NT)


def kernel(**inputs):
    import numpy as np
    import concourse.bacc as bacc
    from concourse.bass_utils import run_bass_kernel_spmd

    a = {k: np.asarray(v) for k, v in inputs.items()}

    def edges(name, fill=0):
        v = a[name].reshape(E)
        return np.concatenate([v, np.full(EP - E, fill, v.dtype)])

    def by_partition(v):
        return np.ascontiguousarray(v.reshape(COLS, P).T)

    dst = edges("dst", N)
    attr = np.concatenate([a["edge_attr_64"], np.zeros((EP - E, EC), np.float32)])
    arrays = {
        "x": np.concatenate([a["x"], np.zeros((NP - N, D), np.float32)]),
        "src_cols": by_partition(edges("src")),
        "rel_cols": by_partition(edges("edge_type_8")),
        "type_cols": by_partition(edges("edge_type_9")),
        "dst_cols": by_partition(dst),
        "dst_rows": dst.reshape(NC, CH),
        "weight_cols": by_partition(edges("edge_weight1")),
        "time_rows": edges("edge_weight").reshape(NC, CH),
        "edge_T": np.ascontiguousarray(attr.reshape(NC, CH, EC).transpose(0, 2, 1)),
        "w0": a["L0_gnn_weight"], "g0": a["L0_gnn_gate_weight"],
        "we1": a["L1_gnn_We1"], "be1": a["L1_gnn_be1"], "we2": a["L1_gnn_We2"], "be2": a["L1_gnn_be2"],
        "wt": a["L1_gnn_Wt"].reshape(D), "bt": a["L1_gnn_bt"],
        "wn1": a["L1_gnn_Wn1"], "bn1": a["L1_gnn_bn1"], "wn2": a["L1_gnn_Wn2"], "bn2": a["L1_gnn_bn2"],
        "wmsgT": a["L2_gnn_W_msg"].T, "bmsg": a["L2_gnn_b_msg"],
        "emb": np.concatenate([a["L2_gnn_edge_embed"], np.zeros((TP - NTYPE, D), np.float32)]),
        "wihT": a["L2_gnn_W_ih"].T, "whhT": a["L2_gnn_W_hh"].T, "bih": a["L2_gnn_b_ih"], "bhh": a["L2_gnn_b_hh"],
        "convT0": a["L3_gnn_W1"].T, "conv_b0": a["L3_gnn_b1"],
        "convT1": a["L3_gnn_W2"].T, "conv_b1": a["L3_gnn_b2"],
        "convT2": a["L3_gnn_W3"].T, "conv_b2": a["L3_gnn_b3"],
    }
    nc = bacc.Bacc("TRN2", target_bir_lowering=False, num_devices=1)
    aps = {}
    for name in arrays:
        arrays[name] = np.ascontiguousarray(arrays[name])
        aps[name] = nc.dram_tensor(f"in_{name}", arrays[name].shape, mybir.dt.from_np(arrays[name].dtype),
                                   kind="ExternalInput").ap()
    scratch = {"meta": ([ROUNDS * 2, NB], I32), "table0": ([NP * R, D], F32)}
    scratch.update({f"table{k}": ([NP, D], F32) for k in range(1, 6)})
    for name, (shape, dt) in scratch.items():
        aps[name] = nc.dram_tensor(f"scratch_{name}", shape, dt, kind="Internal").ap()
    aps["out"] = nc.dram_tensor("out_x", [N, D], F32, kind="ExternalOutput").ap()
    bass_gnn(nc, aps)
    result = run_bass_kernel_spmd(nc, [{f"in_{k}": v for k, v in arrays.items()}], core_ids=[0])
    return result.results[0]["out_x"]
```

```python
import concourse.bass as bass
from concourse import mybir
from contextlib import ExitStack

F32 = mybir.dt.float32
I32 = mybir.dt.int32
ALU = mybir.AluOpType
ACT = mybir.ActivationFunctionType
AXX = mybir.AxisListType.X

P = 128
N = 6250
E = 206250
D = 128
NT = -(-N // P)
NP = NT * P
J = 4
CH = J * P
NB = 4
ROUNDS = -(-E // (CH * NB))
NC = ROUNDS * NB
EP = NC * CH
COLS = EP // P
W = 64
ACCW = NP + W
R = 8
NTYPE = 9
TP = 16
EC = 64
EPS = 1e-5
GD = 8
GROUPS = NP // GD
GPR = 8
GROUNDS = GROUPS // GPR
GW = NT * GD
HALF = 256
HALVES = -(-NP // HALF)
GPH = HALF // GD
PLANES = 3
PAIRS = 4
BANKS = 4
PIECES = 7
PT = NT // PIECES
NCH = 512
CHUNKS = -(-NP // NCH)
GP = GROUNDS
GB = GPR
BF16 = mybir.dt.bfloat16
F16 = mybir.dt.float16
BANK = 512


def bass_gnn(nc, A):
    root = ExitStack()
    with root:
        used = []

        def sem(stack, name):
            used.append(stack.enter_context(nc.semaphore(name)))
            return used[-1]

        def clear_semaphores():
            for one in used:
                nc.gpsimd.sem_clear(one)
            used.clear()
            nc.all_engine_barrier()

        def sbuf(stack, name, shape, dt=F32):
            return stack.enter_context(nc.sbuf_tensor(name, shape, dt))

        def psum(stack, name, shape=(P, BANK), dt=F32):
            return stack.enter_context(nc.psum_tensor(name, list(shape), dt))

        x = sbuf(root, "x", [P, NT, D])
        type_mem = sbuf(root, "type_mem", [P, ACCW])
        typeT = type_mem[0:TP, :]
        ident = sbuf(root, "ident", [P, P])
        ident_b = sbuf(root, "ident_b", [P, P], BF16)
        mean = sbuf(root, "mean", [P, NT])
        ssq = sbuf(root, "ssq", [P, NT])
        var = sbuf(root, "var", [P, NT])
        std = sbuf(root, "std", [P, NT])
        rstd = sbuf(root, "rstd", [P, NT])
        dinv = sbuf(root, "dinv", [P, NT])
        square = sbuf(root, "square", [P, 2, D])
        ones = sbuf(root, "ones", [P, P])
        h = sbuf(root, "h", [P, NT, D])
        more = sbuf(root, "more", [1, 1], I32)
        edge_scope = ExitStack()
        root.enter_context(edge_scope)
        acc = sbuf(edge_scope, "acc", [P, ACCW])
        dst_rel = sbuf(edge_scope, "dst_rel", [P, COLS])
        src_idx = sbuf(edge_scope, "src_idx", [P, COLS], I32)
        meta = sbuf(edge_scope, "meta", [1, NC, 2], I32)
        iota_w = sbuf(edge_scope, "iota_w", [P, W])
        over = sbuf(edge_scope, "over", [P, GROUPS])
        neg_w = sbuf(edge_scope, "neg_w", [P, NP // W + 2])

        def norm_sems(st, tag):
            return {n: sem(st, f"{tag}_{n}") for n in
                    ("summed", "mean", "centered", "squared", "var", "std", "rstd", "h")}

        def norm_vector(dve, s, h, extra_scale=None):
            nc.vector.tensor_reduce(mean[:, :], x[:, :, :], AXX, ALU.add).then_inc(s["summed"], 1)
            dve.wait_ge(s["summed"], 1)
            nc.vector.tensor_scalar(mean[:, :], mean[:, :], 1.0 / D, None, ALU.mult).then_inc(s["mean"], 1)
            dve.wait_ge(s["mean"], 1)
            with dve.Fori(0, NT) as t:
                nc.vector.tensor_scalar(h[:, bass.ds(t, 1), :], x[:, bass.ds(t, 1), :],
                                        mean[:, bass.ds(t, 1)], None, ALU.subtract).then_inc(s["centered"], 1)
            dve.wait_ge(s["squared"], NT + 2)
            nc.vector.tensor_scalar(var[:, :], ssq[:, :], 1.0 / D, EPS, ALU.mult, ALU.add).then_inc(s["var"], 1)
            dve.wait_ge(s["std"], 1)
            nc.vector.reciprocal(rstd[:, :], std[:, :]).then_inc(s["rstd"], 1)
            if extra_scale is not None:
                dve.wait_ge(s["rstd"], 1)
                nc.vector.tensor_tensor(rstd[:, :], rstd[:, :], extra_scale[:, :], ALU.mult).then_inc(s["rstd"], 1)

        def norm_scalar(act, s, h, scalings=1):
            act.sem_inc(s["squared"], 2)
            with act.Fori(0, NT) as t:
                act.wait_ge(s["squared"], t + 1)
                act.wait_ge(s["centered"], t + 1)
                nc.scalar.activation(square[:, bass.ds(t & 1, 1), :], h[:, bass.ds(t, 1), :], ACT.Square,
                                     accum_out=ssq[:, bass.ds(t, 1)]).then_inc(s["squared"], 1)
            act.wait_ge(s["var"], 1)
            nc.scalar.activation(std[:, :], var[:, :], ACT.Sqrt).then_inc(s["std"], 1)
            act.wait_ge(s["rstd"], scalings)
            with act.Fori(0, NT) as t:
                nc.scalar.activation(h[:, bass.ds(t, 1), :], h[:, bass.ds(t, 1), :], ACT.Relu,
                                     scale=rstd[:, bass.ds(t, 1)]).then_inc(s["h"], 1)

        def window_products(rows, onehot, win, counts, onehot_b):
            for j in range(J):
                last = nc.tensor.matmul(win[:, 0:W], rows[:, j, :], onehot[:, j, :],
                                        start=(j == 0), stop=(j == J - 1))
            for j in range(J if counts is not None else 0):
                last = nc.tensor.matmul(win[0:TP, W:2 * W], counts[:, j, :], onehot_b[:, j, :],
                                        start=(j == 0), stop=(j == J - 1))
            return last

        def window_tensor(pe, s, c, rows, onehot, win, counts=None, onehot_b=None):
            pe.wait_ge(s["onehot"], c + 1)
            window_products(rows, onehot, win, counts, onehot_b).then_inc(s["window"], 1)

        def more_windows_tensor(pe, s, q, span, rows, onehot, win, counts=None, onehot_b=None):
            with pe.If(span > W - 1):
                with pe.Fori(0, span >> 6):
                    n = pe.snap(q, min_val=0, max_val=1 << 24)
                    pe.wait_ge(s["x_onehot"], n + 1)
                    window_products(rows, onehot, win, counts, onehot_b).then_inc(s["x_window"], 1)
                    pe.reg_add(q, q, 1)

        def one_hot(c, w, onehot):
            return nc.vector.scalar_tensor_tensor(
                onehot[:, :, :], dst_rel[:, bass.ds(c * J, J)].unsqueeze(2).to_broadcast([P, J, W]),
                neg_w[:, bass.ds(w, 1)], iota_w[:, :].unsqueeze(1).to_broadcast([P, J, W]),
                ALU.add, ALU.is_equal)

        def weigh(c, onehot, weight):
            return nc.vector.tensor_tensor(onehot[:, :, :], onehot[:, :, :],
                                           weight[:, bass.ds(c * J, J)].unsqueeze(2)
                                           .to_broadcast([P, J, W]), ALU.mult)

        def open_window(dve, s, c, onehot, weight=None, onehot_b=None):
            if onehot_b is not None:
                one_hot(c, 0, onehot_b)
            made = one_hot(c, 0, onehot)
            if weight is not None:
                made.then_inc(s["compared"], 1)
                dve.wait_ge(s["compared"], c + 1)
                made = weigh(c, onehot, weight)
            made.then_inc(s["onehot"], 1)

        def add_window(at, win, counts):
            if counts:
                nc.vector.tensor_tensor(typeT[:, bass.ds(at, W)], typeT[:, bass.ds(at, W)],
                                        win[0:TP, W:2 * W], ALU.add)
            return nc.vector.tensor_tensor(acc[:, bass.ds(at, W)], acc[:, bass.ds(at, W)],
                                           win[:, 0:W], ALU.add)

        def close_window(dve, s, q, first, c, least, span, onehot, win, weight=None, onehot_b=None):
            dve.wait_ge(s["added"], c + 1)
            dve.wait_ge(s["window"], c + 1)
            add_window(least, win, onehot_b is not None).then_inc(s["added"], 1)
            with dve.If(span > W - 1):
                dve.reg_mov(first, least)
                with dve.Fori(1, (span >> 6) + 1) as w:
                    n = dve.snap(q, min_val=0, max_val=1 << 24)
                    if onehot_b is not None:
                        one_hot(c, w, onehot_b)
                    made = one_hot(c, w, onehot)
                    made.then_inc(s["x_made"], 1)
                    dve.wait_ge(s["x_made"], n + 1)
                    if weight is not None:
                        weigh(c, onehot, weight).then_inc(s["x_weighed"], 1)
                        dve.wait_ge(s["x_weighed"], n + 1)
                    dve.reg_add(first, first, W)
                    dve.sem_inc(s["x_onehot"], 1)
                    dve.wait_ge(s["x_window"], n + 1)
                    at = dve.snap(first, min_val=0, max_val=NP)
                    add_window(at, win, onehot_b is not None).then_inc(s["x_added"], 1)
                    dve.wait_ge(s["x_added"], n + 1)
                    dve.reg_add(q, q, 1)
            dve.sem_inc(s["chunk_done"], 1)

        WINDOW_SEMS = ("onehot", "added", "window", "compared", "cleared", "chunk_done", "begun",
                       "x_onehot", "x_window", "x_made", "x_weighed", "x_added")

        rows_in = [root.enter_context(nc.semaphore(f"rows_in{b}")) for b in range(NB)]
        passes = []
        weights_in = [root.enter_context(nc.semaphore("weights_in"))]
        seen = [112]

        def weights_seen(more_of):
            seen.append(seen[-1] + more_of)
            return seen[-2]

        def gathers():
            passes.append(len(passes) * 16 * J * ROUNDS)
            return passes[-1]

        def round_meta(eng, regs, first_chunk):
            eng.load(regs, meta[0:1, bass.ds(first_chunk, len(regs) // 2), :].rearrange("a c k -> a (c k)"))
            v = [eng.snap(r, min_val=0, max_val=NP - 1) for r in regs]
            return v[0::2], v[1::2]

        def load_flag(eng, s, reg):
            eng.sem_inc(s["begun"], 1)
            eng.load([reg], more[0:1, 0:1])
            return eng.snap(reg, min_val=0, max_val=1)

        with ExitStack() as l0:
            weight0 = sbuf(l0, "weight0", [P, COLS])
            idx8 = sbuf(l0, "idx8", [P, COLS], I32)
            keys = sbuf(l0, "keys", [P, COLS, 2])
            group_at = sbuf(l0, "group_at", [P, GROUPS, 2])
            iota_lo = sbuf(l0, "iota_lo", [P, P], BF16)
            iota_hi = sbuf(l0, "iota_hi", [P, GW], F16)
            record = sbuf(l0, "record", [1, ROUNDS, 3, GPR], I32)
            w0 = sbuf(l0, "w0", [P, R * D])
            g0 = sbuf(l0, "g0", [P, R])
            with ExitStack() as st:
                dst_rows = sbuf(st, "dst_rows", [ROUNDS, NB * J, P], I32)
                rel = sbuf(st, "rel", [P, COLS], I32)
                low_t = sbuf(st, "low_t", [ROUNDS, 2, NB * J])
                tiles_lo = h[:, :, :].rearrange("p t d -> p (t d)")[0:GP, 0 * COLS:1 * COLS]
                tiles_hi = h[:, :, :].rearrange("p t d -> p (t d)")[0:GP, 1 * COLS:2 * COLS]
                hit = h[:, :, :].rearrange("p t d -> p (t d)")[0:GP, 2 * COLS:3 * COLS]
                scratch_t = acc[:, :][0:GP, 2 * COLS:3 * COLS]
                up = acc[:, :][0:GP, 0 * COLS:1 * COLS]
                down = acc[:, :][0:GP, 1 * COLS:2 * COLS]
                edge_lo = sbuf(st, "edge_lo", [GP, GB])
                edge_hi = sbuf(st, "edge_hi", [GP, GB])
                gfirst = sbuf(st, "gfirst", [GP, GB])
                glast = sbuf(st, "glast", [GP, GB])
                gcount = sbuf(st, "gcount", [GP, GB])
                gout = sbuf(st, "gout", [GP, 2, GB], I32)
                part_a = sbuf(st, "part_a", [P, COLS], I32)
                part_b = sbuf(st, "part_b", [P, COLS], I32)
                dst_cols = sbuf(st, "dst_cols", [P, NC, J], I32)
                both = sbuf(st, "both", [P, NC, 2], I32)
                low = sbuf(st, "low", [ROUNDS, NB, 2], I32)
                high = sbuf(st, "high", [ROUNDS, NB], I32)
                s_rows, s_cols, s_src, s_rel, s_x, s_w = (sem(st, f"in_{n}") for n in
                                                          ("rows", "cols", "src", "rel", "x", "w"))
                s_low, s_high, s_span, s_meta_out, s_meta_in, s_base_in, s_ready, s_id, s_neg = (
                    sem(st, f"setup_{n}") for n in
                    ("low", "high", "span", "meta_out", "meta_in", "base_in", "ready", "id", "neg"))
                s_tile, s_tile_out, s_tile_in, s_hit, s_hits, s_gout, s_g_out, s_g_in, s_parts = (
                    sem(st, f"setup_{n}") for n in ("tile", "tile_out", "tile_in", "hit", "hits", "gout",
                                                    "g_out", "g_in", "parts"))
                st.callback(clear_semaphores)
                block = st.enter_context(nc.Block())

                @block.sync
                def _(sp):
                    sp.dma_start(dst_rows[:, :, :].rearrange("p t e -> p (t e)"),
                                 A["dst_rows"].rearrange("(p k) e -> p (k e)", k=NB)).then_inc(s_rows, 16)
                    sp.dma_start(dst_cols[:, :, :].rearrange("p c j -> p (c j)"), A["dst_cols"]).then_inc(s_cols, 16)
                    sp.dma_start(src_idx[:, :], A["src_cols"]).then_inc(s_src, 16)
                    sp.dma_start(rel[:, :], A["rel_cols"]).then_inc(s_rel, 16)
                    sp.wait_ge(s_span, 1)
                    sp.dma_start(A["meta"].rearrange("(r b) k -> r (b k)", b=NB),
                                 low[:, :, :].rearrange("r b k -> r (b k)")).then_inc(s_meta_out, 16)
                    sp.wait_ge(s_meta_out, 16)
                    sp.dma_start(meta[:, :, :], A["meta"].unsqueeze(0)).then_inc(s_meta_in, 16)
                    sp.dma_start(record[:, :, 2, :], A["meta"].rearrange("(r b) k -> r (b k)", b=NB)
                                 .unsqueeze(0)).then_inc(s_meta_in, 16)
                    sp.dma_start(both[:, :, :], A["meta"].unsqueeze(0).to_broadcast([P, NC, 2])).then_inc(s_base_in, 16)
                    sp.wait_ge(s_tile, 2)
                    for k, rows in enumerate((tiles_lo, tiles_hi)):
                        sp.dma_start(A["tiles"][k:k + 1, :].rearrange("a (r t) -> (a r) t", r=ROUNDS),
                                     low_t[:, k, :]).then_inc(s_tile_out, 16)
                    sp.wait_ge(s_tile_out, 32)
                    for k, rows in enumerate((tiles_lo, tiles_hi)):
                        sp.dma_start(rows[:, :], A["tiles"][k:k + 1, :].to_broadcast([GP, COLS])).then_inc(s_tile_in, 16)
                    sp.wait_ge(s_gout, 2)
                    sp.dma_start(A["groups"].rearrange("(r a) b -> r a b", a=2), gout[:, :, :]).then_inc(s_g_out, 16)
                    sp.wait_ge(s_g_out, 16)
                    sp.dma_start(record[:, 0:GROUNDS, 0:2, :], A["groups"].rearrange("(r a) b -> r a b", a=2)
                                 .unsqueeze(0)).then_inc(s_g_in, 16)
                    sp.wait_ge(s_g_in, 16)
                    sp.wait_ge(s_meta_in, 32)

                @block.scalar
                def _(act):
                    act.dma_start(x[:, :, :], A["x"].rearrange("(t p) d -> p t d", p=P)).then_inc(s_x, 16)
                    act.dma_start(w0[:, :].rearrange("p (r d) -> p r d", r=R), A["w0"].rearrange("r k d -> k r d")).then_inc(s_w, 16)
                    with nc.allow_non_contiguous_dma(reason="1024 gate weights, once"):
                        act.dma_start(g0[:, :], A["g0"].rearrange("r k a -> k (r a)")).then_inc(s_w, 16)
                    act.dma_start(weight0[:, :], A["weight_cols"]).then_inc(s_w, 16)
                    act.wait_ge(s_x, 16)
                    act.wait_ge(s_w, 48)

                @block.gpsimd
                def _(pool):
                    pool.memset(ident[:, :], 0.0).then_inc(s_id, 1)
                    pool.memset(ones[:, :], 1.0).then_inc(s_id, 1)
                    pool.wait_ge(s_id, 2)
                    pool.affine_select(out=ident[:, :], in_=ident[:, :], compare_op=ALU.not_equal, fill=1.0,
                                       base=0, pattern=[[-1, P]], channel_multiplier=1).then_inc(s_id, 1)
                    pool.iota(iota_w[:, :], pattern=[[1, W]], base=0, channel_multiplier=0,
                              allow_small_or_imprecise_dtypes=True).then_inc(s_id, 1)
                    pool.iota(neg_w[:, :], pattern=[[-W, NP // W + 2]], base=0, channel_multiplier=0,
                              allow_small_or_imprecise_dtypes=True).then_inc(s_id, 1)
                    pool.iota(iota_lo[:, :], pattern=[[1, P]], base=0, channel_multiplier=0,
                              allow_small_or_imprecise_dtypes=True).then_inc(s_id, 1)
                    pool.iota(iota_hi[:, :], pattern=[[1, GW]], base=0, channel_multiplier=0,
                              allow_small_or_imprecise_dtypes=True).then_inc(s_id, 1)
                    pool.iota(group_at[:, :, :], pattern=[[P, GROUPS], [0, 2]], base=0, channel_multiplier=0,
                              allow_small_or_imprecise_dtypes=True).then_inc(s_id, 1)
                    pool.iota(up[:, :], pattern=[[1, COLS]], base=1, channel_multiplier=0,
                              allow_small_or_imprecise_dtypes=True).then_inc(s_id, 1)
                    pool.iota(down[:, :], pattern=[[-1, COLS]], base=COLS, channel_multiplier=0,
                              allow_small_or_imprecise_dtypes=True).then_inc(s_id, 1)
                    pool.iota(edge_lo[:, :], pattern=[[GD, GB]], base=0, channel_multiplier=GD * GB,
                              allow_small_or_imprecise_dtypes=True).then_inc(s_id, 1)
                    pool.iota(edge_hi[:, :], pattern=[[GD, GB]], base=GD - 1, channel_multiplier=GD * GB,
                              allow_small_or_imprecise_dtypes=True).then_inc(s_id, 1)
                    pool.wait_ge(s_id, 3)
                    pool.tensor_copy(ident_b[:, :], ident[:, :]).then_inc(s_id, 1)
                    pool.wait_ge(s_id, 13)
                    pool.memset(group_at[:, :, 1:2], 0.0).then_inc(s_id, 1)
                    pool.wait_ge(s_id, 14)

                @block.vector
                def _(dve):
                    dve.wait_ge(s_rows, 16)
                    nc.vector.tensor_reduce(low_t[:, 0, :], dst_rows[:, :, :], AXX, ALU.min).then_inc(s_tile, 1)
                    nc.vector.tensor_reduce(low_t[:, 1, :], dst_rows[:, :, :], AXX, ALU.max).then_inc(s_tile, 1)
                    dve.wait_ge(s_tile, 2)
                    by_chunk = low_t[:, :, :].rearrange("r a (b j) -> r a b j", j=J)
                    nc.vector.tensor_reduce(low[:, :, 0], by_chunk[:, 0, :, :], AXX, ALU.min).then_inc(s_low, 1)
                    nc.vector.tensor_reduce(high[:, :], by_chunk[:, 1, :, :], AXX, ALU.max).then_inc(s_high, 1)
                    dve.wait_ge(s_low, 1)
                    dve.wait_ge(s_high, 1)
                    nc.vector.tensor_tensor(low[:, :, 1], high[:, :], low[:, :, 0], ALU.subtract).then_inc(s_span, 1)
                    dve.wait_ge(s_src, 16)
                    dve.wait_ge(s_rel, 16)
                    nc.vector.scalar_tensor_tensor(idx8[:, :], src_idx[:, :], float(R), rel[:, :],
                                                   ALU.mult, ALU.add).then_inc(s_ready, 1)
                    dve.wait_ge(s_cols, 16)
                    dve.wait_ge(s_base_in, 16)
                    nc.vector.tensor_tensor(dst_rel[:, :].rearrange("p (c j) -> p c j", j=J), dst_cols[:, :, :],
                                            both[:, :, 0:1].to_broadcast([P, NC, J]),
                                            ALU.subtract).then_inc(s_ready, 1)
                    flat = dst_cols[:, :, :].rearrange("p c j -> p (c j)")
                    nc.vector.tensor_scalar(part_a[:, :], src_idx[:, :], P - 1, None, ALU.bitwise_and).then_inc(s_parts, 1)
                    nc.vector.tensor_scalar(part_b[:, :], flat, 3, None, ALU.logical_shift_right).then_inc(s_parts, 1)
                    dve.wait_ge(s_parts, 2)
                    nc.vector.scalar_tensor_tensor(keys[:, :, 0], part_b[:, :], float(P), part_a[:, :],
                                                   ALU.mult, ALU.add).then_inc(s_parts, 1)
                    dve.wait_ge(s_parts, 3)
                    nc.vector.tensor_scalar(part_a[:, :], src_idx[:, :], 7, None, ALU.logical_shift_right).then_inc(s_parts, 1)
                    nc.vector.tensor_scalar(part_b[:, :], flat, GD - 1, None, ALU.bitwise_and).then_inc(s_parts, 1)
                    dve.wait_ge(s_parts, 5)
                    nc.vector.scalar_tensor_tensor(keys[:, :, 1], part_a[:, :], float(GD), part_b[:, :],
                                                   ALU.mult, ALU.add).then_inc(s_parts, 1)
                    dve.wait_ge(s_tile_in, 32)
                    dve.wait_ge(s_id, 13)
                    for k in range(GB):
                        nc.vector.tensor_scalar(hit[:, :], tiles_hi[:, :], edge_lo[:, k:k + 1], None,
                                                ALU.is_ge).then_inc(s_hit, 1)
                        dve.wait_ge(s_hit, 5 * k + 1)
                        nc.vector.scalar_tensor_tensor(hit[:, :], tiles_lo[:, :], edge_hi[:, k:k + 1], hit[:, :],
                                                       ALU.is_le, ALU.mult).then_inc(s_hit, 1)
                        dve.wait_ge(s_hit, 5 * k + 2)
                        for to, weight_of in ((glast, up), (gfirst, down)):
                            nc.vector.tensor_tensor(scratch_t[:, :], hit[:, :], weight_of[:, :], ALU.mult).then_inc(s_hit, 1)
                            dve.wait_ge(s_hit, 5 * k + (3 if to is glast else 4))
                            nc.vector.tensor_reduce(to[:, k:k + 1], scratch_t[:, :], AXX, ALU.max).then_inc(s_hits, 1)
                            dve.wait_ge(s_hits, 2 * k + (1 if to is glast else 2))
                        nc.vector.memset(scratch_t[:, 0:1], 0.0).then_inc(s_hit, 1)
                    nc.vector.tensor_scalar(gfirst[:, :], gfirst[:, :], -1.0, float(COLS), ALU.mult, ALU.add).then_inc(s_parts, 1)
                    dve.wait_ge(s_parts, 7)
                    nc.vector.tensor_scalar(gfirst[:, :], gfirst[:, :], float(COLS - PAIRS), None, ALU.min).then_inc(s_parts, 1)
                    dve.wait_ge(s_parts, 8)
                    nc.vector.tensor_tensor(gcount[:, :], glast[:, :], gfirst[:, :], ALU.subtract).then_inc(s_parts, 1)
                    dve.wait_ge(s_parts, 9)
                    nc.vector.tensor_scalar(gout[:, 1, :], gcount[:, :], float(PAIRS), float(PAIRS), ALU.max, ALU.subtract).then_inc(s_gout, 1)
                    nc.vector.tensor_copy(gout[:, 0, :], gfirst[:, :]).then_inc(s_gout, 1)
                    dve.wait_ge(s_ready, 2)
                    dve.wait_ge(s_gout, 2)

            with ExitStack() as st:
                hT = sbuf(st, "h0T", [P, 2, P])
                gate = sbuf(st, "gate", [P, 2, R])
                out = sbuf(st, "table0_tile", [P, 2, R, D])
                pT = psum(st, "pT", [P, 2, BANK])
                pW = psum(st, "pW", [P, 4, BANK])
                pG = psum(st, "pG", [P, 2, BANK])
                s = norm_sems(st, "n0")
                s_T, s_hT, s_prod, s_gate, s_out = (sem(st, f"n0_{n}") for n in ("T", "hT", "prod", "gate", "out"))
                s_store = [sem(st, f"n0_store{k}") for k in range(2)]
                st.callback(clear_semaphores)
                block = st.enter_context(nc.Block())
                steps = range(NT)

                @block.vector
                def _(dve):
                    norm_vector(dve, s, h)
                    for t in steps:
                        if t >= 2:
                            dve.wait_ge(s_store[t % 2], 16 * (t // 2))
                        dve.wait_ge(s_gate, t + 1)
                        for k in range(2):
                            last = nc.vector.tensor_tensor(
                                out[:, t % 2, 4 * k:4 * k + 4, :],
                                pW[:, 2 * (t % 2) + k, :].rearrange("p (r d) -> p r d", d=D),
                                gate[:, t % 2, 4 * k:4 * k + 4].unsqueeze(2).to_broadcast([P, 4, D]), ALU.mult)
                        last.then_inc(s_out, 1)

                @block.scalar
                def _(act):
                    norm_scalar(act, s, h)
                    for t in steps:
                        act.wait_ge(s_T, t + 1)
                        if t >= 2:
                            act.wait_ge(s_prod, t - 1)
                        nc.scalar.activation(hT[:, t % 2, :], pT[:, t % 2, 0:P], ACT.Copy).then_inc(s_hT, 1)
                        act.wait_ge(s_prod, t + 1)
                        if t >= 2:
                            act.wait_ge(s_out, t - 1)
                        nc.scalar.activation(gate[:, t % 2, :], pG[:, t % 2, 0:R], ACT.Sigmoid).then_inc(s_gate, 1)

                @block.tensor
                def _(pe):
                    pe.wait_ge(s["h"], NT)
                    for t in range(NT + 1):
                        if t < NT:
                            if t >= 2:
                                pe.wait_ge(s_hT, t - 1)
                            nc.tensor.transpose(pT[:, t % 2, 0:P], h[:, t, :], ident[:, :]).then_inc(s_T, 1)
                        if t >= 1:
                            u = t - 1
                            pe.wait_ge(s_hT, u + 1)
                            if u >= 2:
                                pe.wait_ge(s_out, u - 1)
                            for k in range(2):
                                nc.tensor.matmul(pW[:, 2 * (u % 2) + k, :], hT[:, u % 2, :],
                                                 w0[:, k * BANK:(k + 1) * BANK], start=True, stop=True)
                            nc.tensor.matmul(pG[:, u % 2, 0:R], hT[:, u % 2, :], g0[:, :],
                                             start=True, stop=True).then_inc(s_prod, 1)

                @block.sync
                def _(sp):
                    for t in steps:
                        sp.wait_ge(s_out, t + 1)
                        sp.dma_start(A["table0"][t * P * R:(t + 1) * P * R, :].rearrange("(p r) d -> p (r d)", r=R),
                                     out[:, t % 2, :, :].rearrange("p r d -> p (r d)")).then_inc(s_store[t % 2], 16)
                    for k in range(2):
                        sp.wait_ge(s_store[k], 16 * len(range(k, NT, 2)))

            def make_pair(key, lo_hot, hi_hot):
                nc.vector.tensor_scalar(lo_hot, iota_lo[:, :], key[:, 0:1], None, ALU.is_equal)
                return nc.vector.tensor_scalar(hi_hot, iota_hi[:, :], key[:, 1:2], None, ALU.is_equal)

            def group_keys(at, size, g, key):
                return nc.vector.tensor_tensor(key, keys[:, bass.ds(at, size), :],
                                               group_at[:, bass.ds(g, 1), :].to_broadcast([P, size, 2]),
                                               ALU.subtract)

            def group_vector(dve, s, r, t, g, k, first, more_tiles, key, lo_hot, hi_hot):
                half = k % 2
                dve.wait_ge(s["made"], g + 1)
                group_keys(first, PAIRS, g, key[:, half, :, :]).then_inc(s["keyed"], 1)
                dve.wait_ge(s["keyed"], g + 1)
                dve.wait_ge(s["taken"], g + 1)
                for j in range(PAIRS):
                    last = make_pair(key[:, half, j, :], lo_hot[:, half * PAIRS + j, :], hi_hot[:, half * PAIRS + j, :])
                last.then_inc(s["made"], 1)
                with dve.If(more_tiles > 0):
                    dve.reg_mov(t, first + PAIRS)
                    with dve.Fori(0, more_tiles):
                        n = dve.snap(r, min_val=0, max_val=1 << 24)
                        tile = dve.snap(t, min_val=0, max_val=COLS - 1)
                        group_keys(tile, 1, g, key[:, 2, 0:1, :]).then_inc(s["y_keyed"], 1)
                        dve.wait_ge(s["y_keyed"], n + 1)
                        make_pair(key[:, 2, 0, :], lo_hot[:, 2 * PAIRS, :], hi_hot[:, 2 * PAIRS, :]).then_inc(s["y_made"], 1)
                        dve.reg_add(t, t, 1)
                        dve.wait_ge(s["y_taken"], n + 1)
                        dve.reg_add(r, r, 1)

            def group_tensor(pe, s, r, g, k, more_tiles, bank, lo_hot, hi_hot):
                def product(slot, start, stop):
                    return nc.tensor.matmul(bank, lo_hot[:, slot, :], hi_hot[:, slot, :], start=start, stop=stop)
                half = k % 2
                pe.wait_ge(s["flushed"], g + 1)
                pe.wait_ge(s["made"], g + 3)
                for j in range(PAIRS - 1):
                    product(half * PAIRS + j, j == 0, False)
                with pe.If(more_tiles > 0):
                    with pe.Fori(0, more_tiles):
                        n = pe.snap(r, min_val=0, max_val=1 << 24)
                        pe.wait_ge(s["y_made"], n + 1)
                        product(2 * PAIRS, False, False).then_inc(s["y_taken"], 1)
                        pe.reg_add(r, r, 1)
                product(half * PAIRS + PAIRS - 1, False, True).then_inc(s["taken"], 1)

            def load_record(eng, regs, o, groups=True):
                at = 0 if groups else 2
                eng.load(regs[at * GPR:], record[0:1, bass.ds(o, 1), at:3, :].rearrange("a b c d -> a (b c d)"))
                v = [eng.snap(r, min_val=0, max_val=COLS - PAIRS) for r in regs[:GPR]] if groups else None
                m = [eng.snap(r, min_val=0, max_val=COLS) for r in regs[GPR:2 * GPR]] if groups else None
                c = [eng.snap(r, min_val=0, max_val=NP - 1) for r in regs[2 * GPR:]]
                return v, m, c[0::2], c[1::2]

            with ExitStack() as st:
                rows = sbuf(st, "e0_rows", [P, NB, J, D])
                staged = sbuf(st, "e0_staged", [P, NB, J], I32)
                onehot = sbuf(st, "e0_onehot", [P, J, W])
                lo_hot = sbuf(st, "lo_hot", [P, 2 * PAIRS + 1, P], BF16)
                hi_hot = sbuf(st, "hi_hot", [P, 2 * PAIRS + 1, GW], BF16)
                key = sbuf(st, "key", [P, 3, PAIRS, 2])
                block_out = [h[:, :, :].bitcast(BF16),
                             type_mem[:, 0:NP].bitcast(BF16).rearrange("p (t d) -> p t d", d=HALF)]
                excess = sbuf(st, "excess", [P, 2, GW], BF16)
                limit = sbuf(st, "limit", [P, 1])
                win = psum(st, "e0_win")
                banks = psum(st, "e0_banks", [P, BANKS, BANK])
                s = {n: sem(st, f"e0_{n}") for n in WINDOW_SEMS +
                     ("taken", "made", "keyed", "flushed", "copied", "limit", "y_keyed", "y_made", "y_taken")}
                index_in = [sem(st, f"e0_index{b}") for b in range(NB)]
                stored = [sem(st, f"e0_stored{k}") for k in range(2)]
                base = gathers()
                st.callback(clear_semaphores)
                block = st.enter_context(nc.Block())

                @block.sync
                def _(sp):
                    def load(b, c):
                        sp.dma_start(staged[:, b, :], idx8[:, bass.ds(c * J, J)]).then_inc(index_in[b], 16)
                    for b in range(NB):
                        load(b, b)
                    with sp.Fori(1, ROUNDS) as o:
                        for b in range(NB):
                            sp.wait_ge(rows_in[b], base + 16 * J * o)
                            load(b, o * NB + b)

                @block.gpsimd
                def _(pool):
                    with pool.Fori(0, ROUNDS) as o:
                        for b in range(NB):
                            pool.wait_ge(index_in[b], 16 * o + 16)
                            pool.wait_ge(s["chunk_done"], o * NB + b + 1)
                            pool.sem_inc(s["begun"], 1)
                            for j in range(J):
                                pool.indirect_dma_start(
                                    rows[:, b, j, :], None, A["table0"],
                                    bass.IndirectOffsetOnAxis(ap=staged[:, b, j:j + 1], axis=0),
                                ).then_inc(rows_in[b], 16)

                @block.tensor
                def _(pe):
                    q = pe.alloc_register("e0_pe_q")
                    r = pe.alloc_register("e0_pe_r")
                    regs = [pe.alloc_register(f"e0_pe_m{k}") for k in range(3 * GPR)]
                    pe.reg_mov(q, 0)
                    pe.reg_mov(r, 0)
                    pe.sem_inc(s["taken"], 2)

                    def one_round(o, groups):
                        _, more_tiles, _, span = load_record(pe, regs, o, groups)
                        for b in range(NB):
                            pe.wait_ge(rows_in[b], base + 16 * J * o + 16 * J)
                            window_tensor(pe, s, o * NB + b, rows[:, b, :, :], onehot, win)
                            for k in range(2 * b, 2 * b + 2) if groups else ():
                                group_tensor(pe, s, r, o * GPR + k, k, more_tiles[k], banks[:, k % BANKS, 0:GW],
                                             lo_hot, hi_hot)
                            more_windows_tensor(pe, s, q, span[b], rows[:, b, :, :], onehot, win)
                    with pe.Fori(0, GROUNDS) as o:
                        one_round(o, True)
                    with pe.Fori(GROUNDS, ROUNDS) as o:
                        one_round(o, False)

                @block.vector
                def _(dve):
                    q = dve.alloc_register("e0_dve_q")
                    first = dve.alloc_register("e0_dve_first")
                    r = dve.alloc_register("e0_dve_r")
                    t = dve.alloc_register("e0_dve_t")
                    regs = [dve.alloc_register(f"e0_dve_m{k}") for k in range(3 * GPR)]
                    nc.vector.memset(acc[:, :], 0.0).then_inc(s["cleared"], 1)
                    nc.vector.memset(limit[:, :], -256.0).then_inc(s["limit"], 1)
                    dve.wait_ge(s["cleared"], 1)
                    dve.wait_ge(s["limit"], 1)
                    dve.reg_mov(q, 0)
                    dve.reg_mov(r, 0)
                    dve.sem_inc(s["added"], 1)
                    dve.sem_inc(s["made"], 2)
                    dve.sem_inc(s["chunk_done"], NB)

                    def one_round(o, groups):
                        gfirst, more_tiles, least, span = load_record(dve, regs, o, groups)
                        for b in range(NB):
                            open_window(dve, s, o * NB + b, onehot, weight0)
                            for k in range(2 * b, 2 * b + 2) if groups else ():
                                group_vector(dve, s, r, t, o * GPR + k, k, gfirst[k], more_tiles[k],
                                             key, lo_hot, hi_hot)
                            close_window(dve, s, q, first, o * NB + b, least[b], span[b], onehot, win, weight0)
                    with dve.Fori(0, GROUNDS) as o:
                        one_round(o, True)
                    with dve.Fori(GROUNDS, ROUNDS) as o:
                        one_round(o, False)

                @block.scalar
                def _(act):
                    act.sem_inc(s["flushed"], BANKS)
                    act.wait_ge(s["limit"], 1)

                    def flush(g, k, half, at):
                        act.wait_ge(s["flushed"], g + BANKS - 1)
                        act.wait_ge(s["taken"], g + 3)
                        bank = banks[:, k % BANKS, 0:GW]
                        nc.scalar.activation(block_out[half][:, :, bass.ds(at, GD)],
                                             bank.rearrange("p (t d) -> p t d", d=GD), ACT.Copy).then_inc(s["copied"], 1)
                        nc.scalar.activation(excess[:, k % 2, :], bank, ACT.Relu, bias=limit[:, 0:1],
                                             accum_out=over[:, bass.ds(g, 1)]).then_inc(s["flushed"], 1)

                    def block_of(h, half, groups, before):
                        if before is not None:
                            act.wait_ge(stored[half], before)
                        with act.Fori(0, groups // GPR) as i:
                            for k in range(GPR):
                                flush(h * GPH + i * GPR + k, k, half, i * (GPR * GD) + k * GD)
                        act.wait_ge(s["copied"], h * GPH + groups)
                        cols = groups * GD
                        if cols == HALF:
                            act.dma_start(A["counts"][bass.ds(h, 1), :, :].rearrange("a p n -> (a p) n"),
                                          block_out[half].rearrange("p t d -> p (t d)")).then_inc(stored[half], 16)
                        else:
                            act.dma_start(A["counts"][h, :, :].rearrange("p (t d) -> p t d", d=HALF)[:, :, 0:cols],
                                          block_out[half][:, :, 0:cols]).then_inc(stored[half], 16)

                    whole = NP // HALF
                    block_of(0, 0, GPH, None)
                    block_of(1, 1, GPH, None)
                    with act.Fori(1, whole // 2) as i:
                        for half in range(2):
                            block_of(2 * i + half, half, GPH, 16 * i)
                    block_of(whole, 0, GROUPS - whole * GPH, 16 * (whole // 2))
                    act.wait_ge(stored[0], 16 * (whole // 2 + 1))
                    act.wait_ge(stored[1], 16 * (whole // 2))
                    act.wait_ge(s["flushed"], GROUPS + BANKS)

            with ExitStack() as st:
                lo_hot = sbuf(st, "m_lo_hot", [P, 2 * PAIRS + 1, P], BF16)
                hi_hot = sbuf(st, "m_hi_hot", [P, 2 * PAIRS + 1, GW], BF16)
                key = sbuf(st, "m_key", [P, 3, PAIRS, 2])
                first_digit = sbuf(st, "first_digit", [P, GW], BF16)
                rest = sbuf(st, "rest", [P, GW])
                digits = [h[:, :, :].bitcast(BF16),
                          type_mem[:, 0:NP].bitcast(BF16).rearrange("p (t d) -> p t d", d=HALF)]
                top = sbuf(st, "top", [P, 1])
                flag = sbuf(st, "flag", [1, 1])
                pF = psum(st, "m_pF")
                banks = psum(st, "m_banks", [P, 2, BANK])
                s = {n: sem(st, f"m_{n}") for n in
                     ("top", "row", "flag", "taken", "made", "keyed", "flushed", "split_a", "split_b", "split", "stored",
                      "y_keyed", "y_made", "y_taken", "begun")}
                st.callback(clear_semaphores)
                block = st.enter_context(nc.Block())

                @block.sync
                def _(sp):
                    flag_reg = sp.alloc_register("m_sp_flag")
                    sp.wait_ge(s["flag"], 2)
                    above = load_flag(sp, s, flag_reg)

                    def store(h_at, cols, groups):
                        sp.wait_ge(s["split"], groups)
                        for k in range(2):
                            sp.dma_start(A["counts"][bass.ds(h_at + (k + 1) * HALVES, 1), :, :]
                                         .rearrange("a p (t d) -> (a p) t d", d=HALF)[:, :, 0:cols],
                                         digits[k][:, :, 0:cols]).then_inc(s["stored"], 16)
                    with sp.If(above > 0):
                        sp.sem_inc(s["stored"], 1)
                        with sp.Fori(0, NP // HALF) as b:
                            store(b, HALF, b * GPH + GPH)
                        store(NP // HALF, NP % HALF, GROUPS)
                        sp.wait_ge(s["stored"], HALVES * 32 + 1)

                @block.tensor
                def _(pe):
                    r = pe.alloc_register("m_pe_r")
                    flag_reg = pe.alloc_register("m_pe_flag")
                    regs = [pe.alloc_register(f"m_pe_g{k}") for k in range(3 * GPR)]
                    pe.wait_ge(s["top"], 1)
                    nc.tensor.transpose(pF[0:1, 0:P], top[:, 0:1], ident[:, :]).then_inc(s["row"], 1)
                    pe.wait_ge(s["flag"], 2)
                    above = load_flag(pe, s, flag_reg)
                    with pe.If(above > 0):
                        pe.reg_mov(r, 0)
                        pe.sem_inc(s["taken"], 2)
                        with pe.Fori(0, GROUNDS) as o:
                            _, more_tiles, _, _ = load_record(pe, regs, o)
                            for k in range(GPR):
                                group_tensor(pe, s, r, o * GPR + k, k, more_tiles[k], banks[:, k % 2, 0:GW],
                                             lo_hot, hi_hot)

                @block.vector
                def _(dve):
                    r = dve.alloc_register("m_dve_r")
                    t = dve.alloc_register("m_dve_t")
                    flag_reg = dve.alloc_register("m_dve_flag")
                    regs = [dve.alloc_register(f"m_dve_g{k}") for k in range(3 * GPR)]
                    nc.vector.tensor_reduce(top[:, :], over[:, :], AXX, ALU.max).then_inc(s["top"], 1)
                    dve.wait_ge(s["row"], 1)
                    nc.vector.tensor_reduce(flag[:, :], pF[0:1, 0:P], AXX, ALU.max).then_inc(s["flag"], 1)
                    dve.wait_ge(s["flag"], 1)
                    nc.vector.tensor_scalar(more[:, :], flag[:, :], 0.0, None, ALU.is_gt).then_inc(s["flag"], 1)
                    dve.wait_ge(s["flag"], 2)
                    above = load_flag(dve, s, flag_reg)

                    def split(g, k, at):
                        bank = banks[:, k % 2, 0:GW]
                        dve.wait_ge(s["taken"], g + 3)
                        nc.vector.tensor_copy(first_digit[:, :], bank).then_inc(s["split_a"], 1)
                        dve.wait_ge(s["split_a"], g + 1)
                        nc.vector.tensor_tensor(rest[:, :], bank, first_digit[:, :], ALU.subtract).then_inc(s["flushed"], 1)
                        dve.wait_ge(s["flushed"], g + 3)
                        second, third = (v[:, :, bass.ds(at, GD)] for v in digits)
                        rest_td = rest[:, :].rearrange("p (t d) -> p t d", d=GD)
                        nc.vector.tensor_copy(second, rest_td).then_inc(s["split_b"], 1)
                        dve.wait_ge(s["split_b"], g + 1)
                        nc.vector.tensor_tensor(third, rest_td, second, ALU.subtract).then_inc(s["split"], 1)
                        dve.wait_ge(s["split"], g + 1)
                    with dve.If(above > 0):
                        dve.reg_mov(r, 0)
                        dve.sem_inc(s["made"], 2)
                        dve.sem_inc(s["flushed"], 2)
                        with dve.Fori(0, GROUNDS) as o:
                            gfirst, more_tiles, _, _ = load_record(dve, regs, o)
                            dve.wait_ge(s["stored"], (o >> 2) * 32 + 1)
                            for k in range(GPR):
                                group_vector(dve, s, r, t, o * GPR + k, k, gfirst[k], more_tiles[k],
                                             key, lo_hot, hi_hot)
                                split(o * GPR + k, k, (o & 3) * (GPR * GD) + k * GD)

        w_l1 = edge_scope
        wn1a = sbuf(w_l1, "wn1a", [P, D])
        wn1b = sbuf(w_l1, "wn1b", [P, D])
        wn2 = sbuf(w_l1, "wn2", [P, D])
        we1 = sbuf(w_l1, "we1", [EC, D])
        we2 = sbuf(w_l1, "we2", [P, D])
        cols1 = sbuf(w_l1, "cols1", [P, 4])
        bn1_row = sbuf(w_l1, "bn1_row", [P, D])
        bn2_row = sbuf(w_l1, "bn2_row", [TP, D])

        with ExitStack() as st:
            hT = sbuf(st, "h1T", [P, 2, P])
            relu_sum = sbuf(st, "relu_sum", [P, 2, D])
            pT = psum(st, "p1T", [P, 2, BANK])
            pU = psum(st, "p1U", [P, 2, BANK])
            pO = psum(st, "p1O", [P, 2, BANK])
            s = norm_sems(st, "n1")
            s_w, s_T, s_relu, s_x, s_U, s_hT, s_prod, s_out, s_store, s_xh, s_w2 = (
                sem(st, f"n1_{n}") for n in ("w", "T", "relu", "x", "U", "hT", "prod", "out", "store", "xh", "w2"))
            st.callback(clear_semaphores)
            block = st.enter_context(nc.Block())

            @block.sync
            def _(sp):
                sp.dma_start(wn1a[:, :], A["wn1"][0:D, :]).then_inc(s_w, 16)
                sp.dma_start(wn1b[:, :], A["wn1"][D:2 * D, :]).then_inc(s_w, 16)
                sp.dma_start(wn2[:, :], A["wn2"]).then_inc(s_w, 16)
                sp.dma_start(we1[:, :], A["we1"]).then_inc(s_w, 16)
                sp.dma_start(we2[:, :], A["we2"]).then_inc(s_w, 16)
                sp.dma_start(bn1_row[:, :], A["bn1"].unsqueeze(0).to_broadcast([P, D])).then_inc(s_w, 16)
                sp.dma_start(bn2_row[:, :], A["bn2"].unsqueeze(0).to_broadcast([TP, D])).then_inc(s_w, 16)
                with nc.allow_non_contiguous_dma(reason="four columns of biases, once"):
                    for k, name in enumerate(("be1", "be2", "wt", "bt")):
                        sp.dma_start(cols1[:, k:k + 1], A[name].unsqueeze(1)).then_inc(s_w2, 16)
                sp.wait_ge(s_w, 112)
                sp.wait_ge(s_w2, 64)
                sp.wait_ge(s_out, NT)
                sp.dma_start(A["table1"].rearrange("(t p) d -> p t d", p=P), h[:, :, :]).then_inc(s_store, 16)
                sp.wait_ge(s_store, 16)

            @block.tensor
            def _(pe):
                for t in range(NT):
                    if t >= 2:
                        pe.wait_ge(s_relu, t - 1)
                    nc.tensor.transpose(pT[:, t % 2, 0:P], acc[:, t * P:(t + 1) * P], ident[:, :]).then_inc(s_T, 1)
                pe.wait_ge(s["h"], NT)
                pe.wait_ge(s_w, 112)
                for t in range(NT + 1):
                    if t < NT:
                        if t >= 2:
                            pe.wait_ge(s_hT, t - 1)
                        nc.tensor.transpose(pU[:, t % 2, 0:P], h[:, t, :], ident[:, :]).then_inc(s_U, 1)
                    if t >= 1:
                        u = t - 1
                        pe.wait_ge(s_hT, u + 1)
                        if u >= 2:
                            pe.wait_ge(s_out, u - 1)
                        nc.tensor.matmul(pO[:, u % 2, 0:D], hT[:, u % 2, :], wn1a[:, :],
                                         start=True, stop=True).then_inc(s_prod, 1)

            @block.scalar
            def _(act):
                for t in range(NT):
                    act.wait_ge(s_T, t + 1)
                    if t >= 2:
                        act.wait_ge(s_x, t - 1)
                    nc.scalar.activation(relu_sum[:, t % 2, :], pT[:, t % 2, 0:D], ACT.Relu).then_inc(s_relu, 1)
                norm_scalar(act, s, h)
                for t in range(NT):
                    act.wait_ge(s_U, t + 1)
                    if t >= 2:
                        act.wait_ge(s_prod, t - 1)
                    nc.scalar.activation(hT[:, t % 2, :], pU[:, t % 2, 0:P], ACT.Copy).then_inc(s_hT, 1)

            @block.vector
            def _(dve):
                for t in range(NT):
                    dve.wait_ge(s_relu, t + 1)
                    nc.vector.tensor_tensor(x[:, t, :], x[:, t, :], relu_sum[:, t % 2, :], ALU.add).then_inc(s_x, 1)
                dve.wait_ge(s_x, NT)
                norm_vector(dve, s, h)
                dve.wait_ge(s["h"], NT)
                nc.vector.tensor_tensor(x[:, :, :], x[:, :, :], h[:, :, :], ALU.add).then_inc(s_xh, 1)
                dve.wait_ge(s_xh, 1)
                for t in range(NT):
                    dve.wait_ge(s_prod, t + 1)
                    nc.vector.tensor_tensor(h[:, t, :], pO[:, t % 2, 0:D], bn1_row[:, :], ALU.add).then_inc(s_out, 1)

        with ExitStack() as st:
            type_f = sbuf(st, "type_f", [P, COLS])
            type_i = sbuf(st, "type_i", [P, COLS], I32)
            rows = sbuf(st, "e1_rows", [P, NB, J, D])
            staged = sbuf(st, "e1_staged", [P, NB, J], I32)
            onehot = sbuf(st, "e1_onehot", [P, 2, J, W])
            onehot_b = sbuf(st, "e1_onehot_b", [P, 2, J, W], BF16)
            oh_type = sbuf(st, "e1_oh_type", [P, 2, J, TP], BF16)
            edge_in = sbuf(st, "e1_edge", [EC, NB, CH])
            time_in = sbuf(st, "e1_time", [P, NB, CH])
            hid = sbuf(st, "e1_hid", [P, 2, CH])
            tw = sbuf(st, "e1_tw", [P, 2, CH])
            ef = sbuf(st, "e1_ef", [P, 2, CH])
            z = sbuf(st, "e1_z", [P, 2, CH])
            msg = sbuf(st, "e1_msg", [P, 2, J, D])
            win = psum(st, "e1_win")
            p1 = psum(st, "e1_p1", [P, 2, BANK])
            p2 = psum(st, "e1_p2", [P, 2, BANK])
            p3 = psum(st, "e1_p3", [P, 2, BANK])
            s = {n: sem(st, f"e1_{n}") for n in WINDOW_SEMS +
                 ("types", "p1", "hid", "p2", "tw", "ef", "p3", "z", "msg", "type_in")}
            index_in, edges_in, times_in = (
                [sem(st, f"e1_{n}{b}") for b in range(NB)] for n in ("index_in", "edges_in", "times_in"))
            base = gathers()
            st.callback(clear_semaphores)
            block = st.enter_context(nc.Block())

            LAG = 3
            SPR = 2 * NB

            def run_steps(eng, step, load_meta=lambda first: None):
                load_meta(0)
                for c in range(NB):
                    step(c, c, True)
                with eng.Fori(0, (NC - NB) // SPR) as o:
                    load_meta(o * SPR + NB - LAG)
                    for b in range(SPR):
                        step(o * SPR + NB + b, b, False)
                load_meta(NC - SPR)
                for c in range(NC, NC + LAG):
                    step(c, c, True)

            def summed(c, b, edge):
                return b if not edge else 0 if c < NB else c - LAG - (NC - SPR)

            def live(c, edge):
                return not edge or 0 <= c < NC

            @block.sync
            def _(sp):
                def load(b, c, o):
                    if o is not None:
                        sp.wait_ge(rows_in[b], base + 16 * J * o)
                    sp.dma_start(staged[:, b, :], src_idx[:, bass.ds(c * J, J)]).then_inc(index_in[b], 16)
                    if o is not None:
                        sp.wait_ge(s["p1"], c - (NB - 1))
                    sp.dma_start(edge_in[:, b, :], A["edge_T"][bass.ds(c, 1), :, :]
                                 .rearrange("a k e -> (a k) e")).then_inc(edges_in[b], 16)
                sp.dma_start(type_i[:, :], A["type_cols"]).then_inc(s["type_in"], 16)
                for b in range(NB):
                    load(b, b, None)
                with sp.Fori(1, ROUNDS) as o:
                    for b in range(NB):
                        load(b, o * NB + b, o)

            @block.gpsimd
            def _(pool):
                def gather(b, c, o, first):
                    pool.wait_ge(index_in[b], o * 16 + 16)
                    if not first:
                        pool.wait_ge(s["z"], c - (NB - 1))
                    pool.sem_inc(s["begun"], 1)
                    for j in range(J):
                        pool.indirect_dma_start(
                            rows[:, b, j, :], None, A["table1"],
                            bass.IndirectOffsetOnAxis(ap=staged[:, b, j:j + 1], axis=0),
                        ).then_inc(rows_in[b], 16)
                for b in range(NB):
                    gather(b, b, 0, True)
                with pool.Fori(1, ROUNDS) as o:
                    for b in range(NB):
                        gather(b, o * NB + b, o, False)

            @block.tensor
            def _(pe):
                q = pe.alloc_register("e1_pe_q")
                regs = [pe.alloc_register(f"e1_pe_m{k}") for k in range(2 * SPR)]
                pe.reg_mov(q, 0)
                spans = []

                def load_meta(first):
                    spans[:] = round_meta(pe, regs, first)[1]

                def step(c, b, edge):
                    if live(c, edge):
                        pe.wait_ge(edges_in[b % NB], (c - b % NB) * (16 // NB) + 16)
                        if not edge or c >= 2:
                            pe.wait_ge(s["hid"], c - 1)
                        nc.tensor.matmul(p1[:, b % 2, :], we1[:, :], edge_in[:, b % NB, :],
                                         start=True, stop=True).then_inc(s["p1"], 1)
                    if live(c - 1, edge):
                        pe.wait_ge(s["hid"], c)
                        if not edge or c - 1 >= 2:
                            pe.wait_ge(s["ef"], c - 2)
                        nc.tensor.matmul(p2[:, (b - 1) % 2, :], we2[:, :], hid[:, (b - 1) % 2, :],
                                         start=True, stop=True).then_inc(s["p2"], 1)
                    if live(c - 3, edge):
                        pe.wait_ge(s["msg"], c - 2)
                        sources = msg[:, (b - 3) % 2, :, :], onehot[:, (b - 3) % 2, :, :], win, \
                            oh_type[:, (b - 3) % 2, :, :], onehot_b[:, (b - 3) % 2, :, :]
                        window_tensor(pe, s, c - 3, *sources)
                    if live(c - 2, edge):
                        pe.wait_ge(s["ef"], c - 1)
                        if not edge or c - 2 >= 2:
                            pe.wait_ge(s["z"], c - 3)
                        for j in range(J):
                            last = nc.tensor.matmul(p3[:, (b - 2) % 2, j * P:(j + 1) * P],
                                                    ef[:, (b - 2) % 2, j * P:(j + 1) * P], wn1b[:, :],
                                                    start=True, stop=True)
                        last.then_inc(s["p3"], 1)
                    if live(c - 3, edge):
                        more_windows_tensor(pe, s, q, spans[summed(c, b, edge)], *sources)
                run_steps(pe, step, load_meta)

            @block.scalar
            def _(act):
                def load_time(c, b):
                    act.dma_start(time_in[:, b % NB, :], A["time_rows"][bass.ds(c, 1), :]
                                  .to_broadcast([P, CH])).then_inc(times_in[b % NB], 16)
                for b in range(NB - 1):
                    load_time(b, b)

                def step(c, b, edge):
                    if not edge or c + NB - 1 < NC:
                        if not edge or c >= 1:
                            act.wait_ge(s["tw"], c)
                        load_time(c + NB - 1, b + NB - 1)
                    if live(c, edge):
                        act.wait_ge(times_in[b % NB], (c - b % NB) * (16 // NB) + 16)
                        if not edge or c >= 2:
                            act.wait_ge(s["ef"], c - 1)
                        nc.scalar.activation(tw[:, b % 2, :], time_in[:, b % NB, :], ACT.Sigmoid,
                                             bias=cols1[:, 3:4], scale=cols1[:, 2:3]).then_inc(s["tw"], 1)
                        act.wait_ge(s["p1"], c + 1)
                        if not edge or c >= 2:
                            act.wait_ge(s["p2"], c - 1)
                        nc.scalar.activation(hid[:, b % 2, :], p1[:, b % 2, :], ACT.Relu,
                                             bias=cols1[:, 0:1]).then_inc(s["hid"], 1)
                    if live(c - 2, edge):
                        act.wait_ge(s["z"], c - 1)
                        if not edge or c - 2 >= 2:
                            act.wait_ge(s["chunk_done"], c - 3)
                        nc.scalar.activation(msg[:, (b - 2) % 2, :, :].rearrange("p j d -> p (j d)"),
                                             z[:, (b - 2) % 2, :], ACT.Relu).then_inc(s["msg"], 1)

                for c in range(NB):
                    step(c, c, True)
                with act.Fori(0, (NC - NB) // SPR - 1) as o:
                    for b in range(SPR):
                        step(o * SPR + NB + b, NB + b, False)
                for c in range(NC - SPR, NC + LAG):
                    step(c, c, True)

            @block.vector
            def _(dve):
                q = dve.alloc_register("e1_dve_q")
                first = dve.alloc_register("e1_dve_first")
                regs = [dve.alloc_register(f"e1_dve_m{k}") for k in range(2 * SPR)]
                nc.vector.memset(acc[:, :], 0.0).then_inc(s["cleared"], 1)
                nc.vector.memset(typeT[:, :], 0.0).then_inc(s["cleared"], 1)
                dve.wait_ge(s["type_in"], 16)
                nc.vector.tensor_scalar(type_f[:, :], type_i[:, :], 0.0, float(NTYPE - 1),
                                        ALU.max, ALU.min).then_inc(s["cleared"], 1)
                dve.wait_ge(s["cleared"], 3)
                dve.reg_mov(q, 0)
                dve.sem_inc(s["added"], 1)
                dve.reg_mov(q, 0)
                m = []

                def load_meta(first_chunk):
                    m[:] = round_meta(dve, regs, first_chunk)

                def step(c, b, edge):
                    if live(c - 2, edge):
                        k = (b - 2) % 2
                        nc.vector.tensor_tensor(
                            oh_type[:, k, :, :], iota_w[:, 0:TP].unsqueeze(1).to_broadcast([P, J, TP]),
                            type_f[:, bass.ds((c - 2) * J, J)].unsqueeze(2).to_broadcast([P, J, TP]),
                            ALU.is_equal).then_inc(s["types"], 1)
                        open_window(dve, s, c - 2, onehot[:, k, :, :], onehot_b=onehot_b[:, k, :, :])
                    if live(c - 1, edge):
                        dve.wait_ge(s["p2"], c)
                        dve.wait_ge(s["tw"], c)
                        if not edge or c - 1 >= 2:
                            dve.wait_ge(s["p3"], c - 2)
                        k = (b - 1) % 2
                        nc.vector.scalar_tensor_tensor(ef[:, k, :], p2[:, k, :], cols1[:, 1:2], tw[:, k, :],
                                                       ALU.add, ALU.mult).then_inc(s["ef"], 1)
                    if live(c - 3, edge):
                        least, span = (v[summed(c, b, edge)] for v in m)
                        k = (b - 3) % 2
                        close_window(dve, s, q, first, c - 3, least, span, onehot[:, k, :, :], win,
                                     onehot_b=onehot_b[:, k, :, :])
                    if live(c - 2, edge):
                        dve.wait_ge(s["p3"], c - 1)
                        k = (b - 2) % 2
                        slot = (b - 2) % NB
                        dve.wait_ge(rows_in[slot], base + (c - 2 - slot) * (16 * J // NB) + 16 * J)
                        if not edge or c - 2 >= 2:
                            dve.wait_ge(s["msg"], c - 3)
                        nc.vector.tensor_tensor(z[:, k, :], p3[:, k, :],
                                                rows[:, (b - 2) % NB, :, :].rearrange("p j d -> p (j d)"),
                                                ALU.add).then_inc(s["z"], 1)
                run_steps(dve, step, load_meta)

        with ExitStack() as st:
            pO = psum(st, "p2O", [P, 2, BANK])
            pD = psum(st, "p2D")
            s = norm_sems(st, "n2")
            s_O, s_x, s_D, s_deg, s_root = (sem(st, f"n2_{n}") for n in ("O", "x", "D", "deg", "root"))
            st.callback(clear_semaphores)
            block = st.enter_context(nc.Block())

            @block.tensor
            def _(pe):
                for t in range(NT):
                    nc.tensor.matmul(pD[:, t:t + 1], typeT[:, t * P:(t + 1) * P], ones[0:TP, 0:1],
                                     start=True, stop=True).then_inc(s_D, 1)
                for t in range(NT):
                    if t >= 2:
                        pe.wait_ge(s_x, t - 1)
                    nc.tensor.matmul(pO[:, t % 2, 0:D], acc[:, t * P:(t + 1) * P], wn2[:, :], start=True, stop=False)
                    nc.tensor.matmul(pO[:, t % 2, 0:D], typeT[:, t * P:(t + 1) * P], bn2_row[:, :],
                                     start=False, stop=True).then_inc(s_O, 1)

            @block.vector
            def _(dve):
                dve.wait_ge(s_D, NT)
                nc.vector.tensor_scalar(dinv[:, :], pD[:, 0:NT], 1.0, 1.0, ALU.add, ALU.max).then_inc(s_deg, 1)
                for t in range(NT):
                    dve.wait_ge(s_O, t + 1)
                    nc.vector.tensor_tensor(x[:, t, :], x[:, t, :], pO[:, t % 2, 0:D], ALU.add).then_inc(s_x, 1)
                dve.wait_ge(s_x, NT)
                norm_vector(dve, s, h)
                dve.wait_ge(s_root, 1)
                nc.vector.reciprocal(dinv[:, :], dinv[:, :]).then_inc(s_deg, 1)
                dve.wait_ge(s_deg, 2)

            @block.scalar
            def _(act):
                act.wait_ge(s_deg, 1)
                nc.scalar.activation(dinv[:, :], dinv[:, :], ACT.Sqrt).then_inc(s_root, 1)
                norm_scalar(act, s, h)
                act.wait_ge(s["h"], NT)

        edge_scope.close()

        def split_scalar(act, s, parts, source, at, size, count, gap):
            dst = [parts[k][:, bass.ds(at, size), :] for k in range(3)]
            nc.scalar.activation(dst[0], source, ACT.Copy).then_inc(s["part"], 1)
            act.wait_ge(s["rest"], 2 * count + 1)
            nc.scalar.activation(dst[1], gap, ACT.Copy).then_inc(s["part"], 1)
            act.wait_ge(s["rest"], 2 * count + 2)
            nc.scalar.activation(dst[2], gap, ACT.Copy).then_inc(s["part"], 1)

        def split_vector(dve, s, parts, source, at, size, count, gap):
            dve.wait_ge(s["part"], 3 * count + 1)
            nc.vector.tensor_tensor(gap, source, parts[0][:, bass.ds(at, size), :], ALU.subtract).then_inc(s["rest"], 1)
            dve.wait_ge(s["part"], 3 * count + 2)
            nc.vector.tensor_tensor(gap, gap, parts[1][:, bass.ds(at, size), :], ALU.subtract).then_inc(s["rest"], 1)

        def split_all(tag, parts):
            with ExitStack() as st:
                gap = sbuf(st, f"{tag}_gap", [P, 2, PT, D])
                s = {n: sem(st, f"{tag}_{n}") for n in ("part", "rest")}
                st.callback(clear_semaphores)
                block = st.enter_context(nc.Block())

                @block.scalar
                def _(act):
                    for k in range(PIECES):
                        split_scalar(act, s, parts, h[:, k * PT:(k + 1) * PT, :], k * PT, PT, k, gap[:, k % 2, :, :])
                    act.wait_ge(s["part"], 3 * PIECES)

                @block.vector
                def _(dve):
                    for k in range(PIECES):
                        if k >= 2:
                            dve.wait_ge(s["part"], 3 * (k - 1))
                        split_vector(dve, s, parts, h[:, k * PT:(k + 1) * PT, :], k * PT, PT, k, gap[:, k % 2, :, :])

        whole_chunks = NP // NCH
        last_tiles = NT - whole_chunks * (NCH // P)

        def run_chunks(step):
            def go(eng):
                tiles = NCH // P
                step(0, 0, tiles, 0)
                with eng.Fori(0, (whole_chunks - 2) // 2) as i:
                    step(2 * i + 1, 1, tiles, tiles)
                    step(2 * i + 2, 0, tiles, tiles)
                step(whole_chunks - 1, 1, tiles, tiles)
                step(whole_chunks, 0, last_tiles, tiles)
                step(whole_chunks + 1, 1, 0, last_tiles)
            return go

        def counts_in(to, c, plane, at, tiles):
            n = PT * HALF
            if tiles == NCH // P:
                src = A["counts"][bass.ds(c * 2 + plane * HALVES, 2), :, bass.ds(at, n)]
                return to[:, :, :, :].rearrange("p h t d -> p h (t d)"), src.rearrange("h p n -> p h n")
            src = A["counts"][bass.ds(c * 2 + plane * HALVES, 1), :, bass.ds(at, n)]
            return (to[:, 0, :, 0:tiles * P],
                    src.rearrange("h p (t d) -> (h p) t d", d=HALF)[:, :, 0:tiles * P])

        def load_counts(sp, s, loaded, ring, digit_ring):
            flag_reg = sp.alloc_register(f"flag_{s['used'].name}")
            above = load_flag(sp, s, flag_reg)

            def chunk(c, tiles):
                for j in range(PIECES):
                    sp.wait_ge(s["used"], c * PIECES + j + 1)
                    sp.dma_start(*counts_in(ring[:, j, :, :, :], c, 0, j * PT * HALF, tiles)).then_inc(loaded[j], 16)
                with sp.If(above > 0):
                    with sp.Fori(1, PLANES) as plane:
                        with sp.Fori(0, PIECES) as j:
                            sp.wait_ge(s["d_used"], (c * (PLANES - 1) + plane - 1) * PIECES + j + 1)
                            sp.dma_start(*counts_in(digit_ring, c, plane, j * (PT * HALF), tiles)).then_inc(s["d_loaded"], 16)
            with sp.Fori(0, whole_chunks) as c:
                chunk(c, NCH // P)
            chunk(whole_chunks, last_tiles)

        def product_setup(pe, s):
            pe.sem_inc(s["used"], PIECES)
            pe.sem_inc(s["d_used"], 1)
            return load_flag(pe, s, pe.alloc_register(f"flag_pe_{s['used'].name}"))

        def product(pe, s, above, loaded, ring, digit_ring, parts, sums, c, k, tiles, self_loops):
            width = tiles * P

            def tile_products(block, i, t, start=False, stop=False):
                if tiles == NCH // P:
                    counts, to = block[:, :, i, :], sums[:, k, :].rearrange("p (h d) -> p h d", d=HALF)
                else:
                    counts, to = block[:, 0, i, 0:width], sums[:, k, 0:width]
                for part in range(3):
                    last = nc.tensor.matmul(to, parts[part][:, bass.ds(t, 1), :], counts,
                                            start=(start and part == 0), stop=(stop and part == 2))
                return last

            pe.wait_ge(s["out"], c + 1)
            for j in range(PIECES):
                pe.wait_ge(loaded[j], c * 16 + 16)
                if j == PIECES - 1:
                    with pe.If(above > 0):
                        with pe.Fori(1, PLANES) as plane:
                            with pe.Fori(0, PIECES) as m:
                                n = (c * (PLANES - 1) + plane - 1) * PIECES + m
                                pe.wait_ge(s["d_loaded"], n * 16 + 16)
                                for i in range(PT):
                                    last = tile_products(digit_ring, i, m * PT + i)
                                last.then_inc(s["d_used"], 1)
                for i in range(PT):
                    t = j * PT + i
                    last = tile_products(ring[:, j, :, :, :], i, t, t == 0, t == NT - 1)
                last.then_inc(s["used"], 1)
                for i in range(tiles if self_loops and j == 0 else 0):
                    for part in range(3):
                        nc.tensor.matmul(sums[:, k, i * P:(i + 1) * P],
                                         parts[part][:, bass.ds(c * (NCH // P) + i, 1), :], ident_b[:, :],
                                         start=False, stop=False, skip_group_check=True)

        with ExitStack() as l2:
            parts = [sbuf(l2, f"parts2{k}", [P, NT, D], BF16)[:, :, :] for k in range(3)]
            split_all("split2", parts)
            with ExitStack() as st:
                ring = sbuf(st, "ring2", [P, PIECES, 2, PT, HALF], BF16)
                digit_ring = sbuf(st, "digit_ring2", [P, 2, PT, HALF], BF16)
                agg = sbuf(st, "agg2", [P, 2, NCH])
                wmsg = sbuf(st, "wmsg", [P, D])
                emb = sbuf(st, "emb", [TP, D])
                bmsg = sbuf(st, "bmsg", [TP, D])
                wih = sbuf(st, "wih", [P, 3 * D])
                whh = sbuf(st, "whh", [P, 3 * D])
                bih = sbuf(st, "bih", [1, 3 * D])
                bhh = sbuf(st, "bhh", [1, 3 * D])
                held = sbuf(st, "held", [P, 2, 4, D])
                mT = sbuf(st, "mT", [P, NCH])
                hT = sbuf(st, "hT", [P, NCH])
                rz = sbuf(st, "rz", [P, 4, 2 * D])
                pre = sbuf(st, "pre", [P, 4, D])
                new = sbuf(st, "new", [P, 4, D])
                sums = psum(st, "p3S", [P, 2, BANK])
                pM = psum(st, "p3M")
                pT = psum(st, "p3T")
                pR = psum(st, "p3R", [P, 2, BANK])
                pN = psum(st, "p3N", [P, 2, BANK])
                s = {n: sem(st, f"n3_{n}") for n in
                     ("used", "out", "w", "bias", "MT", "mh", "gates", "rz", "pre", "new", "v", "x", "held",
                      "begun", "d_used", "d_loaded")}
                loaded = [sem(st, f"n3_loaded{j}") for j in range(PIECES)]
                st.callback(clear_semaphores)
                block = st.enter_context(nc.Block())
                G2 = slice(0, 2 * D)
                G1 = slice(2 * D, 3 * D)

                @block.sync
                def _(sp):
                    load_counts(sp, s, loaded, ring, digit_ring)

                @block.gpsimd
                def _(pool):
                    pool.dma_start(wmsg[:, :], A["wmsgT"]).then_inc(weights_in[0], 16)
                    pool.dma_start(emb[:, :], A["emb"]).then_inc(weights_in[0], 16)
                    pool.dma_start(bmsg[:, :], A["bmsg"].unsqueeze(0).to_broadcast([TP, D])).then_inc(weights_in[0], 16)
                    pool.dma_start(wih[:, :], A["wihT"]).then_inc(weights_in[0], 16)
                    pool.dma_start(whh[:, :], A["whhT"]).then_inc(weights_in[0], 16)
                    pool.dma_start(bih[:, :], A["bih"].unsqueeze(0)).then_inc(weights_in[0], 16)
                    pool.dma_start(bhh[:, :], A["bhh"].unsqueeze(0)).then_inc(weights_in[0], 16)

                @block.tensor
                def _(pe):
                    above = product_setup(pe, s)
                    pe.wait_ge(weights_in[0], 112)

                    def step(c, k, tiles, before):
                        if tiles:
                            product(pe, s, above, loaded, ring, digit_ring, parts, sums, c, k, tiles, False)
                        if not before:
                            return
                        u = c - 1
                        width = before * P
                        cols = bass.ds(u * NCH, width)
                        pe.wait_ge(s["out"], u + 3)
                        pe.wait_ge(s["held"], u + 1)
                        nc.tensor.matmul(pM[:, 0:width], wmsg[:, :], agg[:, (k + 1) % 2, 0:width], start=True, stop=False)
                        nc.tensor.matmul(pM[:, 0:width], emb[:, :], typeT[:, cols], start=False, stop=False)
                        nc.tensor.matmul(pM[:, 0:width], bmsg[:, :], typeT[:, cols], start=False, stop=True)
                        for i in range(before):
                            last = nc.tensor.transpose(pT[:, i * P:(i + 1) * P],
                                                       held[:, (k + 1) % 2, i, :], ident[:, :])
                        last.then_inc(s["MT"], 1)
                        pe.wait_ge(s["mh"], u + 1)
                        for i in range(before):
                            tile = slice(i * P, (i + 1) * P)
                            to = pR[:, i // 2, (i % 2) * 2 * D:(i % 2 + 1) * 2 * D]
                            nc.tensor.matmul(to, mT[:, tile], wih[:, G2], start=True, stop=False)
                            nc.tensor.matmul(to, hT[:, tile], whh[:, G2], start=False, stop=False)
                            nc.tensor.matmul(to, ones[0:1, :], bih[:, G2], start=False, stop=True)
                            to = pN[:, i // 2, (i % 2) * 2 * D:(i % 2) * 2 * D + D]
                            nc.tensor.matmul(to, mT[:, tile], wih[:, G1], start=True, stop=False)
                            nc.tensor.matmul(to, ones[0:1, :], bih[:, G1], start=False, stop=True)
                            to = pN[:, i // 2, (i % 2) * 2 * D + D:(i % 2 + 1) * 2 * D]
                            nc.tensor.matmul(to, hT[:, tile], whh[:, G1], start=True, stop=False)
                            last = nc.tensor.matmul(to, ones[0:1, :], bhh[:, G1], start=False, stop=True)
                        last.then_inc(s["gates"], 1)
                    pe.wait_ge(s["bias"], 1)
                    run_chunks(step)(pe)

                @block.scalar
                def _(act):
                    act.sem_inc(s["out"], 2)

                    def step(c, k, tiles, before):
                        if before:
                            u = c - 1
                            width = before * P
                            act.wait_ge(s["MT"], u + 1)
                            nc.scalar.activation(mT[:, 0:width], pM[:, 0:width], ACT.Copy)
                            nc.scalar.activation(hT[:, 0:width], pT[:, 0:width], ACT.Copy).then_inc(s["mh"], 1)
                            act.wait_ge(s["gates"], u + 1)
                            for i in range(0, before, 2):
                                n = min(2, before - i)
                                last = nc.scalar.activation(rz[:, i:i + n, :],
                                                            pR[:, i // 2, 0:n * 2 * D].rearrange("p (i g) -> p i g", i=n),
                                                            ACT.Sigmoid)
                            last.then_inc(s["rz"], 1)
                            act.wait_ge(s["pre"], u + 1)
                            nc.scalar.activation(new[:, 0:before, :], pre[:, 0:before, :], ACT.Tanh).then_inc(s["new"], 1)
                            act.wait_ge(s["x"], u + 1)
                        if tiles:
                            act.wait_ge(s["used"], c * PIECES + 2 * PIECES)
                            nc.scalar.activation(agg[:, k, 0:tiles * P], sums[:, k, 0:tiles * P],
                                                 ACT.Copy).then_inc(s["out"], 1)
                    run_chunks(step)(act)

                @block.vector
                def _(dve):
                    dve.wait_ge(weights_in[0], 112)
                    nc.vector.tensor_tensor(bih[:, G2], bih[:, G2], bhh[:, G2], ALU.add).then_inc(s["bias"], 1)

                    def step(c, k, tiles, before):
                        if before:
                            gru(c - 1, before)
                        if tiles:
                            nc.vector.tensor_copy(held[:, k, 0:tiles, :],
                                                  h[:, bass.ds(c * 4, tiles), :]).then_inc(s["held"], 1)

                    def gru(u, before):
                        dve.wait_ge(s["rz"], u + 1)
                        b = slice(0, before)
                        for i in range(0, before, 2):
                            n = min(2, before - i)
                            pair = pN[:, i // 2, 0:n * 2 * D].rearrange("p (i g) -> p i g", i=n)
                            last = nc.vector.tensor_tensor(pre[:, i:i + n, :], rz[:, i:i + n, 0:D], pair[:, :, D:2 * D], ALU.mult)
                        last.then_inc(s["v"], 1)
                        dve.wait_ge(s["v"], u * 4 + 1)
                        for i in range(0, before, 2):
                            n = min(2, before - i)
                            pair = pN[:, i // 2, 0:n * 2 * D].rearrange("p (i g) -> p i g", i=n)
                            last = nc.vector.tensor_tensor(pre[:, i:i + n, :], pre[:, i:i + n, :], pair[:, :, 0:D], ALU.add)
                        last.then_inc(s["pre"], 1)
                        dve.wait_ge(s["new"], u + 1)
                        at = bass.ds(u * 4, before)
                        nc.vector.tensor_tensor(pre[:, b, :], h[:, at, :], new[:, b, :], ALU.subtract).then_inc(s["v"], 1)
                        nc.vector.tensor_tensor(x[:, at, :], x[:, at, :], new[:, b, :], ALU.add).then_inc(s["v"], 1)
                        dve.wait_ge(s["v"], u * 4 + 3)
                        nc.vector.tensor_tensor(pre[:, b, :], pre[:, b, :], rz[:, b, D:2 * D], ALU.mult).then_inc(s["v"], 1)
                        dve.wait_ge(s["v"], u * 4 + 4)
                        nc.vector.tensor_tensor(x[:, at, :], x[:, at, :], pre[:, b, :], ALU.add).then_inc(s["x"], 1)
                    run_chunks(step)(dve)

        with ExitStack() as st:
            s = norm_sems(st, "n4")
            st.callback(clear_semaphores)
            block = st.enter_context(nc.Block())

            @block.vector
            def _(dve):
                norm_vector(dve, s, h, extra_scale=dinv)

            @block.scalar
            def _(act):
                norm_scalar(act, s, h, scalings=2)
                act.wait_ge(s["h"], NT)

        h_b = h[:, :, :].rearrange("p t d -> p (t d)").bitcast(BF16)
        parts = [[sbuf(root, f"parts3{k}", [P, NT, D], BF16)[:, :, :] for k in range(3)],
                 [v.rearrange("p (t d) -> p t d", d=D) for v in
                  (h_b[:, 0:NP], h_b[:, NP:2 * NP], type_mem[:, :].bitcast(BF16)[:, 0:NP])]]
        split_all("split3", parts[0])
        for conv in range(3):
            last_conv = conv == 2
            with ExitStack() as st:
                now, then = parts[conv % 2], parts[(conv + 1) % 2]
                ring = sbuf(st, f"ring3{conv}", [P, PIECES, 2, PT, HALF], BF16)
                digit_ring = sbuf(st, f"digit_ring3{conv}", [P, 2, PT, HALF], BF16)
                agg = sbuf(st, f"c{conv}_agg", [P, 2, NCH])
                w = sbuf(st, f"c{conv}_w", [P, D])
                bias = sbuf(st, f"c{conv}_bias", [P, D])
                y = sbuf(st, f"c{conv}_y", [P, 4, D])
                gap = sbuf(st, f"c{conv}_gap", [P, 4, D])
                sums = psum(st, f"c{conv}_sums", [P, 2, BANK])
                pO = psum(st, f"c{conv}_pO")
                s = {n: sem(st, f"c{conv}_{n}") for n in
                     ("used", "out", "O", "y", "h", "part", "rest", "x", "begun",
                      "d_used", "d_loaded")}
                loaded = [sem(st, f"c{conv}_loaded{j}") for j in range(PIECES)]
                s_store = sem(st, f"c{conv}_store")
                w_base = weights_seen(32)
                st.callback(clear_semaphores)
                block = st.enter_context(nc.Block())

                @block.gpsimd
                def _(pool):
                    pool.dma_start(w[:, :], A[f"convT{conv}"]).then_inc(weights_in[0], 16)
                    pool.dma_start(bias[:, :], A[f"conv_b{conv}"].unsqueeze(0).to_broadcast([P, D])).then_inc(weights_in[0], 16)

                @block.sync
                def _(sp):
                    load_counts(sp, s, loaded, ring, digit_ring)
                    if last_conv:
                        sp.wait_ge(s["x"], whole_chunks + 1)
                        whole = N // P
                        sp.dma_start(A["out"][0:whole * P, :].rearrange("(t p) d -> p t d", p=P),
                                     x[:, 0:whole, :]).then_inc(s_store, 16)
                        sp.dma_start(A["out"][whole * P:N, :], x[0:N - whole * P, whole, :]).then_inc(s_store, 16)
                        sp.wait_ge(s_store, 32)

                @block.tensor
                def _(pe):
                    above = product_setup(pe, s)
                    pe.wait_ge(weights_in[0], w_base + 32)

                    def step(c, k, tiles, before):
                        if tiles:
                            product(pe, s, above, loaded, ring, digit_ring, now, sums, c, k, tiles, True)
                        if before:
                            pe.wait_ge(s["out"], c + 2)
                            for i in range(before):
                                last = nc.tensor.matmul(pO[:, i * P:(i + 1) * P],
                                                        agg[:, (k + 1) % 2, i * P:(i + 1) * P], w[:, :],
                                                        start=True, stop=True)
                            last.then_inc(s["O"], 1)
                    run_chunks(step)(pe)

                @block.scalar
                def _(act):
                    act.sem_inc(s["out"], 2)

                    def step(c, k, tiles, before):
                        if before:
                            u = c - 1
                            act.wait_ge(s["y"], u + 1)
                            if not last_conv:
                                for i in range(before):
                                    last = nc.scalar.activation(y[:, i, :], y[:, i, :], ACT.Relu,
                                                                scale=dinv[:, bass.ds(u * 4 + i, 1)])
                                last.then_inc(s["h"], 1)
                                act.wait_ge(s["h"], u + 1)
                                split_scalar(act, s, then, y[:, 0:before, :], u * 4, before, u, gap[:, 0:before, :])
                                act.wait_ge(s["part"], 3 * u + 3)
                        if tiles:
                            act.wait_ge(s["used"], c * PIECES + 2 * PIECES)
                            nc.scalar.activation(agg[:, k, 0:tiles * P], sums[:, k, 0:tiles * P],
                                                 ACT.Copy).then_inc(s["out"], 1)
                    run_chunks(step)(act)

                @block.vector
                def _(dve):
                    dve.wait_ge(weights_in[0], w_base + 32)

                    def step(c, k, tiles, before):
                        if not before:
                            return
                        u = c - 1
                        dve.wait_ge(s["O"], u + 1)
                        for i in range(before):
                            last = nc.vector.scalar_tensor_tensor(y[:, i, :], pO[:, i * P:(i + 1) * P],
                                                                  dinv[:, bass.ds(u * 4 + i, 1)], bias[:, :],
                                                                  ALU.mult, ALU.add)
                        last.then_inc(s["y"], 1)
                        if last_conv:
                            dve.wait_ge(s["y"], u + 1)
                            at = bass.ds(u * 4, before)
                            nc.vector.tensor_tensor(x[:, at, :], x[:, at, :], y[:, 0:before, :], ALU.add).then_inc(s["x"], 1)
                            dve.wait_ge(s["x"], u + 1)
                        else:
                            dve.wait_ge(s["h"], u + 1)
                            split_vector(dve, s, then, y[:, 0:before, :], u * 4, before, u, gap[:, 0:before, :])
                            dve.wait_ge(s["part"], 3 * u + 3)
                    run_chunks(step)(dve)


def kernel(**inputs):
    import numpy as np
    import concourse.bacc as bacc
    from concourse.bass_utils import run_bass_kernel_spmd

    a = {k: np.asarray(v) for k, v in inputs.items()}

    def edges(name, fill=0):
        v = a[name].reshape(E)
        return np.concatenate([v, np.broadcast_to(np.asarray(fill, v.dtype), (EP - E,))])

    def by_partition(v):
        return np.ascontiguousarray(v.reshape(COLS, P).T)

    dst = edges("dst", N)
    attr = np.concatenate([a["edge_attr_64"], np.zeros((EP - E, EC), np.float32)])
    arrays = {
        "x": np.concatenate([a["x"], np.zeros((NP - N, D), np.float32)]),
        "src_cols": by_partition(edges("src", np.arange(EP - E))),
        "rel_cols": by_partition(edges("edge_type_8")),
        "type_cols": by_partition(edges("edge_type_9")),
        "dst_cols": by_partition(dst),
        "dst_rows": dst.reshape(NC, CH),
        "weight_cols": by_partition(edges("edge_weight1")),
        "time_rows": edges("edge_weight").reshape(NC, CH),
        "edge_T": np.ascontiguousarray(attr.reshape(NC, CH, EC).transpose(0, 2, 1)),
        "w0": a["L0_gnn_weight"], "g0": a["L0_gnn_gate_weight"],
        "we1": a["L1_gnn_We1"], "be1": a["L1_gnn_be1"], "we2": a["L1_gnn_We2"], "be2": a["L1_gnn_be2"],
        "wt": a["L1_gnn_Wt"].reshape(D), "bt": a["L1_gnn_bt"],
        "wn1": a["L1_gnn_Wn1"], "bn1": a["L1_gnn_bn1"], "wn2": a["L1_gnn_Wn2"], "bn2": a["L1_gnn_bn2"],
        "wmsgT": a["L2_gnn_W_msg"].T, "bmsg": a["L2_gnn_b_msg"],
        "emb": np.concatenate([a["L2_gnn_edge_embed"], np.zeros((TP - NTYPE, D), np.float32)]),
        "wihT": a["L2_gnn_W_ih"].T, "whhT": a["L2_gnn_W_hh"].T, "bih": a["L2_gnn_b_ih"], "bhh": a["L2_gnn_b_hh"],
        "convT0": a["L3_gnn_W1"].T, "conv_b0": a["L3_gnn_b1"],
        "convT1": a["L3_gnn_W2"].T, "conv_b1": a["L3_gnn_b2"],
        "convT2": a["L3_gnn_W3"].T, "conv_b2": a["L3_gnn_b3"],
    }
    nc = bacc.Bacc("TRN2", target_bir_lowering=False, num_devices=1)
    aps = {}
    for name in arrays:
        arrays[name] = np.ascontiguousarray(arrays[name])
        aps[name] = nc.dram_tensor(f"in_{name}", arrays[name].shape, mybir.dt.from_np(arrays[name].dtype),
                                   kind="ExternalInput").ap()
    scratch = {"meta": ([NC, 2], I32), "groups": ([GROUNDS * 2, GPR], I32), "tiles": ([2, COLS], F32),
               "table0": ([NP * R, D], F32), "table1": ([NP, D], F32),
               "counts": ([PLANES * HALVES, P, NT * HALF], BF16)}
    for name, (shape, dt) in scratch.items():
        aps[name] = nc.dram_tensor(f"scratch_{name}", shape, dt, kind="Internal").ap()
    aps["out"] = nc.dram_tensor("out_x", [N, D], F32, kind="ExternalOutput").ap()
    bass_gnn(nc, aps)
    result = run_bass_kernel_spmd(nc, [{f"in_{k}": v for k, v in arrays.items()}], core_ids=[0])
    return result.results[0]["out_x"]
```

```python
import concourse.bass as bass
from concourse import mybir
from contextlib import ExitStack

F32 = mybir.dt.float32
I32 = mybir.dt.int32
ALU = mybir.AluOpType
ACT = mybir.ActivationFunctionType
AXX = mybir.AxisListType.X

P = 128
N = 6250
E = 206250
D = 128
NT = -(-N // P)
NP = NT * P
J = 4
CH = J * P
NB = 4
ROUNDS = -(-E // (CH * NB))
NC = ROUNDS * NB
EP = NC * CH
COLS = EP // P
W = 64
ACCW = NP + W
R = 8
NTYPE = 9
TP = 16
EC = 64
EPS = 1e-5
GD = 8
GROUPS = NP // GD
GPR = 8
GROUNDS = GROUPS // GPR
GW = NT * GD
HALF = 256
HALVES = -(-NP // HALF)
GPH = HALF // GD
PLANES = 3
PAIRS = 4
BANKS = 4
PIECES = 7
PT = NT // PIECES
NCH = 512
BF16 = mybir.dt.bfloat16
F16 = mybir.dt.float16
BANK = 512


def bass_gnn(nc, A):
    root = ExitStack()
    with root:
        used = []

        def sem(stack, name):
            used.append(stack.enter_context(nc.semaphore(name)))
            return used[-1]

        def clear_semaphores():
            for one in used:
                nc.gpsimd.sem_clear(one)
            used.clear()
            nc.all_engine_barrier()

        def sbuf(stack, name, shape, dt=F32):
            return stack.enter_context(nc.sbuf_tensor(name, shape, dt))

        def psum(stack, name, shape=(P, BANK), dt=F32):
            return stack.enter_context(nc.psum_tensor(name, list(shape), dt))

        x = sbuf(root, "x", [P, NT, D])
        type_mem = sbuf(root, "type_mem", [P, ACCW])
        typeT = type_mem[0:TP, :]
        ident = sbuf(root, "ident", [P, P])
        ident_b = sbuf(root, "ident_b", [P, P], BF16)
        mean = sbuf(root, "mean", [P, NT])
        ssq = sbuf(root, "ssq", [P, NT])
        var = sbuf(root, "var", [P, NT])
        std = sbuf(root, "std", [P, NT])
        rstd = sbuf(root, "rstd", [P, NT])
        dinv = sbuf(root, "dinv", [P, NT])
        square = sbuf(root, "square", [P, 2, PT, D])
        ones = sbuf(root, "ones", [P, P])
        h = sbuf(root, "h", [P, NT, D])
        more = sbuf(root, "more", [1, 1], I32)
        edge_scope = ExitStack()
        root.enter_context(edge_scope)
        acc = sbuf(edge_scope, "acc", [P, ACCW])
        dst_rel = sbuf(edge_scope, "dst_rel", [P, COLS])
        src_idx = sbuf(edge_scope, "src_idx", [P, COLS], I32)
        meta = sbuf(edge_scope, "meta", [1, NC, 2], I32)
        iota_w = sbuf(edge_scope, "iota_w", [P, W])
        over = sbuf(edge_scope, "over", [P, GROUPS])
        neg_w = sbuf(edge_scope, "neg_w", [P, NP // W + 2])

        QUADS = -(-NT // 4)

        def quad(q):
            return range(4 * q, min(4 * q + 4, NT))

        def norm_sems(st, tag):
            return {n: sem(st, f"{tag}_{n}") for n in
                    ("summed", "mean", "centered", "squared", "reduced", "var", "std", "rstd", "relu", "h")}

        def piece(k):
            return slice(k * PT, (k + 1) * PT)

        def norm_vector(dve, s, h, extra_scale=None):
            nc.vector.tensor_reduce(mean[:, :], x[:, :, :], AXX, ALU.add).then_inc(s["summed"], 1)
            dve.wait_ge(s["summed"], 1)
            nc.vector.tensor_scalar(mean[:, :], mean[:, :], 1.0 / D, None, ALU.mult).then_inc(s["mean"], 1)
            dve.wait_ge(s["mean"], 1)
            for k in range(PIECES):
                nc.vector.tensor_tensor(h[:, piece(k), :], x[:, piece(k), :],
                                        mean[:, piece(k)].unsqueeze(2).to_broadcast([P, PT, D]),
                                        ALU.subtract).then_inc(s["centered"], 1)
            for k in range(PIECES):
                dve.wait_ge(s["squared"], k + 1)
                nc.vector.tensor_reduce(ssq[:, piece(k)], square[:, k % 2, :, :], AXX, ALU.add).then_inc(s["reduced"], 1)
            dve.wait_ge(s["reduced"], PIECES)
            nc.vector.tensor_scalar(var[:, :], ssq[:, :], 1.0 / D, EPS, ALU.mult, ALU.add).then_inc(s["var"], 1)
            dve.wait_ge(s["std"], 1)
            nc.vector.reciprocal(rstd[:, :], std[:, :]).then_inc(s["rstd"], 1)
            dve.wait_ge(s["rstd"], 1)
            if extra_scale is not None:
                nc.vector.tensor_tensor(rstd[:, :], rstd[:, :], extra_scale[:, :], ALU.mult).then_inc(s["rstd"], 1)
                dve.wait_ge(s["rstd"], 2)
            for k in range(PIECES):
                dve.wait_ge(s["relu"], k + 1)
                nc.vector.tensor_tensor(h[:, piece(k), :], h[:, piece(k), :],
                                        rstd[:, piece(k)].unsqueeze(2).to_broadcast([P, PT, D]),
                                        ALU.mult).then_inc(s["h"], 1)

        def norm_scalar(act, s, h):
            for k in range(PIECES + 1):
                if k < PIECES:
                    act.wait_ge(s["centered"], k + 1)
                    if k >= 2:
                        act.wait_ge(s["reduced"], k - 1)
                    nc.scalar.activation(square[:, k % 2, :, :], h[:, piece(k), :], ACT.Square).then_inc(s["squared"], 1)
                if k >= 1:
                    act.wait_ge(s["squared"], k)
                    nc.scalar.activation(h[:, piece(k - 1), :], h[:, piece(k - 1), :], ACT.Relu).then_inc(s["relu"], 1)
            act.wait_ge(s["var"], 1)
            nc.scalar.activation(std[:, :], var[:, :], ACT.Sqrt).then_inc(s["std"], 1)

        def window_products(rows, onehot, win, counts, onehot_b):
            for j in range(J):
                last = nc.tensor.matmul(win[:, 0:W], rows[:, j, :], onehot[:, j, :],
                                        start=(j == 0), stop=(j == J - 1))
            for j in range(J if counts is not None else 0):
                last = nc.tensor.matmul(win[0:TP, W:2 * W], counts[:, j, :], onehot_b[:, j, :],
                                        start=(j == 0), stop=(j == J - 1))
            return last

        def window_tensor(pe, s, c, rows, onehot, win, counts=None, onehot_b=None):
            pe.wait_ge(s["onehot"], c + 1)
            window_products(rows, onehot, win, counts, onehot_b).then_inc(s["window"], 1)

        def more_windows_tensor(pe, s, q, span, rows, onehot, win, counts=None, onehot_b=None):
            with pe.If(span > W - 1):
                with pe.Fori(0, span >> 6):
                    n = pe.snap(q, min_val=0, max_val=1 << 24)
                    pe.wait_ge(s["x_onehot"], n + 1)
                    window_products(rows, onehot, win, counts, onehot_b).then_inc(s["x_window"], 1)
                    pe.reg_add(q, q, 1)

        def one_hot(c, w, onehot):
            return nc.vector.scalar_tensor_tensor(
                onehot[:, :, :], dst_rel[:, bass.ds(c * J, J)].unsqueeze(2).to_broadcast([P, J, W]),
                neg_w[:, bass.ds(w, 1)], iota_w[:, :].unsqueeze(1).to_broadcast([P, J, W]),
                ALU.add, ALU.is_equal)

        def weigh(c, onehot, weight):
            return nc.vector.tensor_tensor(onehot[:, :, :], onehot[:, :, :],
                                           weight[:, bass.ds(c * J, J)].unsqueeze(2)
                                           .to_broadcast([P, J, W]), ALU.mult)

        def open_window(s, c, onehot, onehot_b=None, made_sem="onehot"):
            if onehot_b is not None:
                one_hot(c, 0, onehot_b)
            one_hot(c, 0, onehot).then_inc(s[made_sem], 1)

        def add_window(at, win, counts):
            if counts:
                nc.vector.tensor_tensor(typeT[:, bass.ds(at, W)], typeT[:, bass.ds(at, W)],
                                        win[0:TP, W:2 * W], ALU.add)
            return nc.vector.tensor_tensor(acc[:, bass.ds(at, W)], acc[:, bass.ds(at, W)],
                                           win[:, 0:W], ALU.add)

        def close_window(dve, s, q, first, c, least, span, onehot, win, weight=None, onehot_b=None):
            dve.wait_ge(s["added"], c + 1)
            dve.wait_ge(s["window"], c + 1)
            add_window(least, win, onehot_b is not None).then_inc(s["added"], 1)
            with dve.If(span > W - 1):
                dve.reg_mov(first, least)
                with dve.Fori(1, (span >> 6) + 1) as w:
                    n = dve.snap(q, min_val=0, max_val=1 << 24)
                    if onehot_b is not None:
                        one_hot(c, w, onehot_b)
                    made = one_hot(c, w, onehot)
                    made.then_inc(s["x_made"], 1)
                    dve.wait_ge(s["x_made"], n + 1)
                    if weight is not None:
                        weigh(c, onehot, weight).then_inc(s["x_weighed"], 1)
                        dve.wait_ge(s["x_weighed"], n + 1)
                    dve.reg_add(first, first, W)
                    dve.sem_inc(s["x_onehot"], 1)
                    dve.wait_ge(s["x_window"], n + 1)
                    at = dve.snap(first, min_val=0, max_val=NP)
                    add_window(at, win, onehot_b is not None).then_inc(s["x_added"], 1)
                    dve.wait_ge(s["x_added"], n + 1)
                    dve.reg_add(q, q, 1)
            dve.sem_inc(s["chunk_done"], 1)

        WINDOW_SEMS = ("onehot", "added", "window", "compared", "cleared", "chunk_done", "begun",
                       "x_onehot", "x_window", "x_made", "x_weighed", "x_added")

        rows_in = [root.enter_context(nc.semaphore(f"rows_in{b}")) for b in range(NB)]
        passes = []
        weights_in = [root.enter_context(nc.semaphore("weights_in"))]
        seen = [112]

        def weights_seen(more_of):
            seen.append(seen[-1] + more_of)
            return seen[-2]

        def gathers():
            passes.append(len(passes) * 16 * J * ROUNDS)
            return passes[-1]

        def window_meta(eng, regs, first_chunk):
            eng.load(regs, meta[0:1, bass.ds(first_chunk, len(regs) // 2), :].rearrange("a c k -> a (c k)"))
            v = [eng.snap(r, min_val=0, max_val=NP - 1) for r in regs]
            return v[0::2], v[1::2]

        def load_flag(eng, s, reg):
            eng.sem_inc(s["begun"], 1)
            eng.load([reg], more[0:1, 0:1])
            return eng.snap(reg, min_val=0, max_val=1)

        with ExitStack() as l0:
            weight0 = sbuf(l0, "weight0", [P, COLS])
            idx8 = sbuf(l0, "idx8", [P, COLS], I32)
            keys = sbuf(l0, "keys", [P, COLS, 2])
            group_at = sbuf(l0, "group_at", [P, GROUPS, 2])
            iota_lo = sbuf(l0, "iota_lo", [P, P], BF16)
            iota_hi = sbuf(l0, "iota_hi", [P, GW], F16)
            record = sbuf(l0, "record", [1, ROUNDS, 3, GPR], I32)
            w0 = sbuf(l0, "w0", [P, R * D])
            g0 = sbuf(l0, "g0", [P, R])
            with ExitStack() as st:
                dst_rows = sbuf(st, "dst_rows", [ROUNDS, NB * J, P], I32)
                rel = sbuf(st, "rel", [P, COLS], I32)
                low_t = sbuf(st, "low_t", [ROUNDS, 2, NB * J])
                tiles_lo = h[:, :, :].rearrange("p t d -> p (t d)")[0:GROUNDS, 0 * COLS:1 * COLS]
                tiles_hi = h[:, :, :].rearrange("p t d -> p (t d)")[0:GROUNDS, 1 * COLS:2 * COLS]
                hit = h[:, :, :].rearrange("p t d -> p (t d)")[0:GROUNDS, 2 * COLS:3 * COLS]
                scratch_t = acc[:, :][0:GROUNDS, 2 * COLS:3 * COLS]
                up = acc[:, :][0:GROUNDS, 0 * COLS:1 * COLS]
                down = acc[:, :][0:GROUNDS, 1 * COLS:2 * COLS]
                edge_lo = sbuf(st, "edge_lo", [GROUNDS, GPR])
                edge_hi = sbuf(st, "edge_hi", [GROUNDS, GPR])
                gfirst = sbuf(st, "gfirst", [GROUNDS, GPR])
                glast = sbuf(st, "glast", [GROUNDS, GPR])
                gcount = sbuf(st, "gcount", [GROUNDS, GPR])
                gout = sbuf(st, "gout", [GROUNDS, 2, GPR], I32)
                part_a = sbuf(st, "part_a", [P, COLS], I32)
                part_b = sbuf(st, "part_b", [P, COLS], I32)
                dst_cols = sbuf(st, "dst_cols", [P, NC, J], I32)
                both = (square[:, :, :, :].rearrange("p a t d -> p (a t d)")[:, 0:NC * 2].bitcast(I32)
                        .rearrange("p (c k) -> p c k", k=2))
                low = sbuf(st, "low", [ROUNDS, NB, 2], I32)
                high = sbuf(st, "high", [ROUNDS, NB], I32)
                s_rows, s_cols, s_src, s_rel, s_x, s_w = (sem(st, f"in_{n}") for n in
                                                          ("rows", "cols", "src", "rel", "x", "w"))
                s_low, s_high, s_span, s_meta_out, s_meta_in, s_base_in, s_ready, s_id = (
                    sem(st, f"setup_{n}") for n in
                    ("low", "high", "span", "meta_out", "meta_in", "base_in", "ready", "id"))
                s_tile, s_tile_out, s_tile_in, s_hit, s_hits, s_gout, s_g_out, s_g_in, s_parts = (
                    sem(st, f"setup_{n}") for n in ("tile", "tile_out", "tile_in", "hit", "hits", "gout",
                                                    "g_out", "g_in", "parts"))
                st.callback(clear_semaphores)
                block = st.enter_context(nc.Block())

                @block.sync
                def _(sp):
                    sp.dma_start(dst_rows[:, :, :].rearrange("p t e -> p (t e)"),
                                 A["dst_rows"].rearrange("(p k) e -> p (k e)", k=NB)).then_inc(s_rows, 16)
                    sp.dma_start(dst_cols[:, :, :].rearrange("p c j -> p (c j)"), A["dst_cols"]).then_inc(s_cols, 16)
                    sp.dma_start(src_idx[:, :], A["src_cols"]).then_inc(s_src, 16)
                    sp.dma_start(rel[:, :], A["rel_cols"]).then_inc(s_rel, 16)
                    sp.wait_ge(s_span, 1)
                    sp.dma_start(A["meta"].rearrange("(r b) k -> r (b k)", b=NB),
                                 low[:, :, :].rearrange("r b k -> r (b k)")).then_inc(s_meta_out, 16)
                    sp.wait_ge(s_meta_out, 16)
                    sp.dma_start(meta[:, :, :], A["meta"].unsqueeze(0)).then_inc(s_meta_in, 16)
                    sp.dma_start(record[:, :, 2, :], A["meta"].rearrange("(r b) k -> r (b k)", b=NB)
                                 .unsqueeze(0)).then_inc(s_meta_in, 16)
                    sp.dma_start(both, A["meta"].unsqueeze(0).to_broadcast([P, NC, 2])).then_inc(s_base_in, 16)
                    sp.wait_ge(s_tile, 2)
                    for k in range(2):
                        sp.dma_start(A["tiles"][k:k + 1, :].rearrange("a (r t) -> (a r) t", r=ROUNDS),
                                     low_t[:, k, :]).then_inc(s_tile_out, 16)
                    sp.wait_ge(s_tile_out, 32)
                    for k, rows in enumerate((tiles_lo, tiles_hi)):
                        sp.dma_start(rows[:, :], A["tiles"][k:k + 1, :].to_broadcast([GROUNDS, COLS])).then_inc(s_tile_in, 16)
                    sp.wait_ge(s_gout, 2)
                    sp.dma_start(A["groups"].rearrange("(r a) b -> r a b", a=2), gout[:, :, :]).then_inc(s_g_out, 16)
                    sp.wait_ge(s_g_out, 16)
                    sp.dma_start(record[:, 0:GROUNDS, 0:2, :], A["groups"].rearrange("(r a) b -> r a b", a=2)
                                 .unsqueeze(0)).then_inc(s_g_in, 16)
                    sp.wait_ge(s_g_in, 16)
                    sp.wait_ge(s_meta_in, 32)

                @block.scalar
                def _(act):
                    act.dma_start(x[:, :, :], A["x"].rearrange("(t p) d -> p t d", p=P)).then_inc(s_x, 16)
                    act.dma_start(w0[:, :].rearrange("p (r d) -> p r d", r=R), A["w0"].rearrange("r k d -> k r d")).then_inc(s_w, 16)
                    with nc.allow_non_contiguous_dma(reason="1024 gate weights, once"):
                        act.dma_start(g0[:, :], A["g0"].rearrange("r k a -> k (r a)")).then_inc(s_w, 16)
                    act.dma_start(weight0[:, :], A["weight_cols"]).then_inc(s_w, 16)
                    act.wait_ge(s_x, 16)
                    act.wait_ge(s_w, 48)

                @block.gpsimd
                def _(pool):
                    pool.memset(ident[:, :], 0.0).then_inc(s_id, 1)
                    pool.memset(ones[:, :], 1.0).then_inc(s_id, 1)
                    pool.wait_ge(s_id, 2)
                    pool.affine_select(out=ident[:, :], in_=ident[:, :], compare_op=ALU.not_equal, fill=1.0,
                                       base=0, pattern=[[-1, P]], channel_multiplier=1).then_inc(s_id, 1)
                    pool.iota(iota_w[:, :], pattern=[[1, W]], base=0, channel_multiplier=0,
                              allow_small_or_imprecise_dtypes=True).then_inc(s_id, 1)
                    pool.iota(neg_w[:, :], pattern=[[-W, NP // W + 2]], base=0, channel_multiplier=0,
                              allow_small_or_imprecise_dtypes=True).then_inc(s_id, 1)
                    pool.iota(iota_lo[:, :], pattern=[[1, P]], base=0, channel_multiplier=0,
                              allow_small_or_imprecise_dtypes=True).then_inc(s_id, 1)
                    pool.iota(iota_hi[:, :], pattern=[[1, GW]], base=0, channel_multiplier=0,
                              allow_small_or_imprecise_dtypes=True).then_inc(s_id, 1)
                    pool.iota(group_at[:, :, :], pattern=[[P, GROUPS], [0, 2]], base=0, channel_multiplier=0,
                              allow_small_or_imprecise_dtypes=True).then_inc(s_id, 1)
                    pool.iota(up[:, :], pattern=[[1, COLS]], base=1, channel_multiplier=0,
                              allow_small_or_imprecise_dtypes=True).then_inc(s_id, 1)
                    pool.iota(down[:, :], pattern=[[-1, COLS]], base=COLS, channel_multiplier=0,
                              allow_small_or_imprecise_dtypes=True).then_inc(s_id, 1)
                    pool.iota(edge_lo[:, :], pattern=[[GD, GPR]], base=0, channel_multiplier=GD * GPR,
                              allow_small_or_imprecise_dtypes=True).then_inc(s_id, 1)
                    pool.iota(edge_hi[:, :], pattern=[[GD, GPR]], base=GD - 1, channel_multiplier=GD * GPR,
                              allow_small_or_imprecise_dtypes=True).then_inc(s_id, 1)
                    pool.wait_ge(s_id, 3)
                    pool.tensor_copy(ident_b[:, :], ident[:, :]).then_inc(s_id, 1)
                    pool.wait_ge(s_id, 13)
                    pool.memset(group_at[:, :, 1:2], 0.0).then_inc(s_id, 1)
                    pool.wait_ge(s_id, 14)

                @block.vector
                def _(dve):
                    dve.wait_ge(s_rows, 16)
                    nc.vector.tensor_reduce(low_t[:, 0, :], dst_rows[:, :, :], AXX, ALU.min).then_inc(s_tile, 1)
                    nc.vector.tensor_reduce(low_t[:, 1, :], dst_rows[:, :, :], AXX, ALU.max).then_inc(s_tile, 1)
                    dve.wait_ge(s_tile, 2)
                    by_chunk = low_t[:, :, :].rearrange("r a (b j) -> r a b j", j=J)
                    nc.vector.tensor_reduce(low[:, :, 0], by_chunk[:, 0, :, :], AXX, ALU.min).then_inc(s_low, 1)
                    nc.vector.tensor_reduce(high[:, :], by_chunk[:, 1, :, :], AXX, ALU.max).then_inc(s_high, 1)
                    dve.wait_ge(s_low, 1)
                    dve.wait_ge(s_high, 1)
                    nc.vector.tensor_tensor(low[:, :, 1], high[:, :], low[:, :, 0], ALU.subtract).then_inc(s_span, 1)
                    dve.wait_ge(s_src, 16)
                    dve.wait_ge(s_rel, 16)
                    nc.vector.scalar_tensor_tensor(idx8[:, :], src_idx[:, :], float(R), rel[:, :],
                                                   ALU.mult, ALU.add).then_inc(s_ready, 1)
                    dve.wait_ge(s_cols, 16)
                    dve.wait_ge(s_base_in, 16)
                    nc.vector.tensor_tensor(dst_rel[:, :].rearrange("p (c j) -> p c j", j=J), dst_cols[:, :, :],
                                            both[:, :, 0:1].to_broadcast([P, NC, J]),
                                            ALU.subtract).then_inc(s_ready, 1)
                    flat = dst_cols[:, :, :].rearrange("p c j -> p (c j)")
                    nc.vector.tensor_scalar(part_a[:, :], src_idx[:, :], P - 1, None, ALU.bitwise_and).then_inc(s_parts, 1)
                    nc.vector.tensor_scalar(part_b[:, :], flat, 3, None, ALU.logical_shift_right).then_inc(s_parts, 1)
                    dve.wait_ge(s_parts, 2)
                    nc.vector.scalar_tensor_tensor(keys[:, :, 0], part_b[:, :], float(P), part_a[:, :],
                                                   ALU.mult, ALU.add).then_inc(s_parts, 1)
                    dve.wait_ge(s_parts, 3)
                    nc.vector.tensor_scalar(part_a[:, :], src_idx[:, :], 7, None, ALU.logical_shift_right).then_inc(s_parts, 1)
                    nc.vector.tensor_scalar(part_b[:, :], flat, GD - 1, None, ALU.bitwise_and).then_inc(s_parts, 1)
                    dve.wait_ge(s_parts, 5)
                    nc.vector.scalar_tensor_tensor(keys[:, :, 1], part_a[:, :], float(GD), part_b[:, :],
                                                   ALU.mult, ALU.add).then_inc(s_parts, 1)
                    dve.wait_ge(s_tile_in, 32)
                    dve.wait_ge(s_id, 13)
                    for k in range(GPR):
                        nc.vector.tensor_scalar(hit[:, :], tiles_hi[:, :], edge_lo[:, k:k + 1], None,
                                                ALU.is_ge).then_inc(s_hit, 1)
                        dve.wait_ge(s_hit, 4 * k + 1)
                        nc.vector.scalar_tensor_tensor(hit[:, :], tiles_lo[:, :], edge_hi[:, k:k + 1], hit[:, :],
                                                       ALU.is_le, ALU.mult).then_inc(s_hit, 1)
                        dve.wait_ge(s_hit, 4 * k + 2)
                        for to, weight_of in ((glast, up), (gfirst, down)):
                            nc.vector.tensor_tensor(scratch_t[:, :], hit[:, :], weight_of[:, :], ALU.mult).then_inc(s_hit, 1)
                            dve.wait_ge(s_hit, 4 * k + (3 if to is glast else 4))
                            nc.vector.tensor_reduce(to[:, k:k + 1], scratch_t[:, :], AXX, ALU.max).then_inc(s_hits, 1)
                            dve.wait_ge(s_hits, 2 * k + (1 if to is glast else 2))
                    nc.vector.tensor_scalar(gfirst[:, :], gfirst[:, :], -1.0, float(COLS), ALU.mult, ALU.add).then_inc(s_parts, 1)
                    dve.wait_ge(s_parts, 7)
                    nc.vector.tensor_scalar(gfirst[:, :], gfirst[:, :], float(COLS - PAIRS), None, ALU.min).then_inc(s_parts, 1)
                    dve.wait_ge(s_parts, 8)
                    nc.vector.tensor_tensor(gcount[:, :], glast[:, :], gfirst[:, :], ALU.subtract).then_inc(s_parts, 1)
                    dve.wait_ge(s_parts, 9)
                    nc.vector.tensor_scalar(gout[:, 1, :], gcount[:, :], float(PAIRS), float(PAIRS), ALU.max, ALU.subtract).then_inc(s_gout, 1)
                    nc.vector.tensor_copy(gout[:, 0, :], gfirst[:, :]).then_inc(s_gout, 1)
                    dve.wait_ge(s_ready, 2)
                    dve.wait_ge(s_gout, 2)

            with ExitStack() as st:
                hT = sbuf(st, "h0T", [P, 2, P])
                gate = sbuf(st, "gate", [P, 2, R])
                out = sbuf(st, "table0_tile", [P, 2, R, D])
                pT = psum(st, "pT", [P, 2, BANK])
                pW = psum(st, "pW", [P, 4, BANK])
                pG = psum(st, "pG", [P, 2, BANK])
                s = norm_sems(st, "n0")
                s_T, s_hT, s_prod, s_gate, s_out = (sem(st, f"n0_{n}") for n in ("T", "hT", "prod", "gate", "out"))
                s_store = [sem(st, f"n0_store{k}") for k in range(2)]
                st.callback(clear_semaphores)
                block = st.enter_context(nc.Block())
                steps = range(NT)

                @block.vector
                def _(dve):
                    norm_vector(dve, s, h)
                    for t in steps:
                        if t >= 2:
                            dve.wait_ge(s_store[t % 2], 16 * (t // 2))
                        dve.wait_ge(s_gate, t + 1)
                        for k in range(2):
                            last = nc.vector.tensor_tensor(
                                out[:, t % 2, 4 * k:4 * k + 4, :],
                                pW[:, 2 * (t % 2) + k, :].rearrange("p (r d) -> p r d", d=D),
                                gate[:, t % 2, 4 * k:4 * k + 4].unsqueeze(2).to_broadcast([P, 4, D]), ALU.mult)
                        last.then_inc(s_out, 1)

                @block.scalar
                def _(act):
                    norm_scalar(act, s, h)
                    for t in range(NT + 1):
                        if t < NT:
                            act.wait_ge(s_T, t + 1)
                            if t >= 2:
                                act.wait_ge(s_prod, t - 1)
                            nc.scalar.activation(hT[:, t % 2, :], pT[:, t % 2, 0:P], ACT.Copy).then_inc(s_hT, 1)
                        if t >= 1:
                            u = t - 1
                            act.wait_ge(s_prod, u + 1)
                            if u >= 2:
                                act.wait_ge(s_out, u - 1)
                            nc.scalar.activation(gate[:, u % 2, :], pG[:, u % 2, 0:R], ACT.Sigmoid).then_inc(s_gate, 1)

                @block.tensor
                def _(pe):
                    pe.wait_ge(s["h"], PIECES)
                    for t in range(NT + 1):
                        if t < NT:
                            if t >= 2:
                                pe.wait_ge(s_hT, t - 1)
                            nc.tensor.transpose(pT[:, t % 2, 0:P], h[:, t, :], ident[:, :]).then_inc(s_T, 1)
                        if t >= 1:
                            u = t - 1
                            pe.wait_ge(s_hT, u + 1)
                            if u >= 2:
                                pe.wait_ge(s_out, u - 1)
                            for k in range(2):
                                nc.tensor.matmul(pW[:, 2 * (u % 2) + k, :], hT[:, u % 2, :],
                                                 w0[:, k * BANK:(k + 1) * BANK], start=True, stop=True)
                            nc.tensor.matmul(pG[:, u % 2, 0:R], hT[:, u % 2, :], g0[:, :],
                                             start=True, stop=True).then_inc(s_prod, 1)

                @block.sync
                def _(sp):
                    for t in steps:
                        sp.wait_ge(s_out, t + 1)
                        sp.dma_start(A["table0"][t * P * R:(t + 1) * P * R, :].rearrange("(p r) d -> p (r d)", r=R),
                                     out[:, t % 2, :, :].rearrange("p r d -> p (r d)")).then_inc(s_store[t % 2], 16)
                    for k in range(2):
                        sp.wait_ge(s_store[k], 16 * len(range(k, NT, 2)))

            def make_pair(key, lo_hot, hi_hot):
                nc.vector.tensor_scalar(lo_hot, iota_lo[:, :], key[:, 0:1], None, ALU.is_equal)
                return nc.vector.tensor_scalar(hi_hot, iota_hi[:, :], key[:, 1:2], None, ALU.is_equal)

            def group_keys(at, size, g, key):
                return nc.vector.tensor_tensor(key, keys[:, bass.ds(at, size), :],
                                               group_at[:, bass.ds(g, 1), :].to_broadcast([P, size, 2]),
                                               ALU.subtract)

            def take_keys(dve, s, g, k, first, key):
                dve.wait_ge(s["made"], g + 1)
                group_keys(first, PAIRS, g, key[:, k % 2, :, :]).then_inc(s["keyed"], 1)

            def group_vector(dve, s, r, t, g, k, first, more_tiles, key, lo_hot, hi_hot):
                half = k % 2
                dve.wait_ge(s["keyed"], g + 1)
                dve.wait_ge(s["taken"], g + 1)
                for j in range(PAIRS):
                    last = make_pair(key[:, half, j, :], lo_hot[:, half * PAIRS + j, :], hi_hot[:, half * PAIRS + j, :])
                last.then_inc(s["made"], 1)
                with dve.If(more_tiles > 0):
                    dve.reg_mov(t, first + PAIRS)
                    with dve.Fori(0, more_tiles):
                        n = dve.snap(r, min_val=0, max_val=1 << 24)
                        tile = dve.snap(t, min_val=0, max_val=COLS - 1)
                        group_keys(tile, 1, g, key[:, 2, 0:1, :]).then_inc(s["y_keyed"], 1)
                        dve.wait_ge(s["y_keyed"], n + 1)
                        make_pair(key[:, 2, 0, :], lo_hot[:, 2 * PAIRS, :], hi_hot[:, 2 * PAIRS, :]).then_inc(s["y_made"], 1)
                        dve.reg_add(t, t, 1)
                        dve.wait_ge(s["y_taken"], n + 1)
                        dve.reg_add(r, r, 1)

            def group_tensor(pe, s, r, g, k, more_tiles, bank, lo_hot, hi_hot):
                def product(slot, start, stop):
                    return nc.tensor.matmul(bank, lo_hot[:, slot, :], hi_hot[:, slot, :], start=start, stop=stop)
                half = k % 2
                pe.wait_ge(s["flushed"], g + 1)
                pe.wait_ge(s["made"], g + 3)
                for j in range(PAIRS - 1):
                    product(half * PAIRS + j, j == 0, False)
                with pe.If(more_tiles > 0):
                    with pe.Fori(0, more_tiles):
                        n = pe.snap(r, min_val=0, max_val=1 << 24)
                        pe.wait_ge(s["y_made"], n + 1)
                        product(2 * PAIRS, False, False).then_inc(s["y_taken"], 1)
                        pe.reg_add(r, r, 1)
                product(half * PAIRS + PAIRS - 1, False, True).then_inc(s["taken"], 1)

            def load_record(eng, regs, o, groups=True):
                at = 0 if groups else 2
                eng.load(regs[at * GPR:], record[0:1, bass.ds(o, 1), at:3, :].rearrange("a b c d -> a (b c d)"))
                v = [eng.snap(r, min_val=0, max_val=COLS - PAIRS) for r in regs[:GPR]] if groups else None
                m = [eng.snap(r, min_val=0, max_val=COLS) for r in regs[GPR:2 * GPR]] if groups else None
                c = [eng.snap(r, min_val=0, max_val=NP - 1) for r in regs[2 * GPR:]]
                return v, m, c[0::2], c[1::2]

            with ExitStack() as st:
                rows = sbuf(st, "e0_rows", [P, NB, J, D])
                staged = sbuf(st, "e0_staged", [P, NB, J], I32)
                onehot = sbuf(st, "e0_onehot", [P, 2, J, W])
                lo_hot = sbuf(st, "lo_hot", [P, 2 * PAIRS + 1, P], BF16)
                hi_hot = sbuf(st, "hi_hot", [P, 2 * PAIRS + 1, GW], BF16)
                key = sbuf(st, "key", [P, 3, PAIRS, 2])
                block_out = [h[:, :, :].bitcast(BF16),
                             type_mem[:, 0:NP].bitcast(BF16).rearrange("p (t d) -> p t d", d=HALF)]
                excess = sbuf(st, "excess", [P, 2, GW], BF16)
                limit = sbuf(st, "limit", [P, 1])
                win = psum(st, "e0_win")
                banks = psum(st, "e0_banks", [P, BANKS, BANK])
                s = {n: sem(st, f"e0_{n}") for n in WINDOW_SEMS +
                     ("taken", "made", "keyed", "flushed", "copied", "limit", "y_keyed", "y_made", "y_taken")}
                index_in = [sem(st, f"e0_index{b}") for b in range(NB)]
                stored = [sem(st, f"e0_stored{k}") for k in range(2)]
                base = gathers()
                st.callback(clear_semaphores)
                block = st.enter_context(nc.Block())

                @block.sync
                def _(sp):
                    def load(b, c):
                        sp.dma_start(staged[:, b, :], idx8[:, bass.ds(c * J, J)]).then_inc(index_in[b], 16)
                    for b in range(NB):
                        load(b, b)
                    with sp.Fori(1, ROUNDS) as o:
                        for b in range(NB):
                            sp.wait_ge(rows_in[b], base + 16 * J * o)
                            load(b, o * NB + b)

                @block.gpsimd
                def _(pool):
                    with pool.Fori(0, ROUNDS) as o:
                        for b in range(NB):
                            pool.wait_ge(index_in[b], 16 * o + 16)
                            pool.wait_ge(s["chunk_done"], o * NB + b + 1)
                            pool.sem_inc(s["begun"], 1)
                            for j in range(J):
                                pool.indirect_dma_start(
                                    rows[:, b, j, :], None, A["table0"],
                                    bass.IndirectOffsetOnAxis(ap=staged[:, b, j:j + 1], axis=0),
                                ).then_inc(rows_in[b], 16)

                @block.tensor
                def _(pe):
                    q = pe.alloc_register("e0_pe_q")
                    r = pe.alloc_register("e0_pe_r")
                    regs = [pe.alloc_register(f"e0_pe_m{k}") for k in range(3 * GPR)]
                    pe.reg_mov(q, 0)
                    pe.reg_mov(r, 0)
                    pe.sem_inc(s["taken"], 2)

                    def one_round(o, groups):
                        _, more_tiles, _, span = load_record(pe, regs, o, groups)
                        for b in range(NB):
                            pe.wait_ge(rows_in[b], base + 16 * J * o + 16 * J)
                            pe.wait_ge(s["added"], o * NB + b + 1)
                            pe.wait_ge(s["chunk_done"], o * NB + b + NB)
                            window_tensor(pe, s, o * NB + b, rows[:, b, :, :], onehot[:, b % 2, :, :], win)
                            for k in range(2 * b, 2 * b + 2) if groups else ():
                                group_tensor(pe, s, r, o * GPR + k, k, more_tiles[k], banks[:, k % BANKS, 0:GW],
                                             lo_hot, hi_hot)
                            more_windows_tensor(pe, s, q, span[b], rows[:, b, :, :], onehot[:, b % 2, :, :], win)
                    with pe.Fori(0, GROUNDS) as o:
                        one_round(o, True)
                    with pe.Fori(GROUNDS, ROUNDS) as o:
                        one_round(o, False)

                @block.vector
                def _(dve):
                    q = dve.alloc_register("e0_dve_q")
                    first = dve.alloc_register("e0_dve_first")
                    r = dve.alloc_register("e0_dve_r")
                    t = dve.alloc_register("e0_dve_t")
                    regs = [dve.alloc_register(f"e0_dve_m{k}") for k in range(3 * GPR)]
                    nc.vector.memset(acc[:, :], 0.0).then_inc(s["cleared"], 1)
                    nc.vector.memset(limit[:, :], -256.0).then_inc(s["limit"], 1)
                    dve.wait_ge(s["cleared"], 1)
                    dve.wait_ge(s["limit"], 1)
                    dve.reg_mov(q, 0)
                    dve.reg_mov(r, 0)
                    dve.sem_inc(s["added"], 1)
                    dve.sem_inc(s["made"], 2)
                    dve.sem_inc(s["chunk_done"], NB)

                    def one_round(o, groups, last=False):
                        gfirst, more_tiles, least, span = load_record(dve, regs, o, groups)
                        for b in range(NB):
                            for k in range(2 * b, 2 * b + 2) if groups else ():
                                take_keys(dve, s, o * GPR + k, k, gfirst[k], key)
                            if not (last and b == NB - 1):
                                open_window(s, o * NB + b + 1, onehot[:, (b + 1) % 2, :, :], made_sem="compared")
                            for k in range(2 * b, 2 * b + 2) if groups else ():
                                group_vector(dve, s, r, t, o * GPR + k, k, gfirst[k], more_tiles[k],
                                             key, lo_hot, hi_hot)
                            close_window(dve, s, q, first, o * NB + b, least[b], span[b],
                                         onehot[:, b % 2, :, :], win, weight0)
                    open_window(s, 0, onehot[:, 0, :, :], made_sem="compared")
                    with dve.Fori(0, GROUNDS) as o:
                        one_round(o, True)
                    with dve.Fori(GROUNDS, ROUNDS - 1) as o:
                        one_round(o, False)
                    one_round(ROUNDS - 1, False, last=True)

                @block.scalar
                def _(act):
                    act.sem_inc(s["flushed"], BANKS)
                    act.wait_ge(s["limit"], 1)

                    def weigh_chunk(c, half):
                        act.wait_ge(s["compared"], c + 1)
                        for j in range(J):
                            last = nc.scalar.activation(onehot[:, half, j, :], onehot[:, half, j, :], ACT.Copy,
                                                        scale=weight0[:, bass.ds(c * J + j, 1)])
                        last.then_inc(s["onehot"], 1)

                    def flush(g, k, half, at):
                        act.wait_ge(s["flushed"], g + BANKS - 1)
                        act.wait_ge(s["taken"], g + 3)
                        bank = banks[:, k % BANKS, 0:GW]
                        nc.scalar.activation(block_out[half][:, :, bass.ds(at, GD)],
                                             bank.rearrange("p (t d) -> p t d", d=GD), ACT.Copy).then_inc(s["copied"], 1)
                        nc.scalar.activation(excess[:, k % 2, :], bank, ACT.Relu, bias=limit[:, 0:1],
                                             accum_out=over[:, bass.ds(g, 1)]).then_inc(s["flushed"], 1)

                    def block_of(h, half, groups, before):
                        if before is not None:
                            act.wait_ge(stored[half], before)
                        with act.Fori(0, groups // GPR) as i:
                            for k in range(GPR):
                                if k % 2 == 0:
                                    weigh_chunk(h * (GPH // 2) + i * NB + k // 2 + 1, (k // 2 + 1) % 2)
                                flush(h * GPH + i * GPR + k, k, half, i * (GPR * GD) + k * GD)
                        act.wait_ge(s["copied"], h * GPH + groups)
                        cols = groups * GD
                        if cols == HALF:
                            act.dma_start(A["counts"][bass.ds(h, 1), :, :].rearrange("a p n -> (a p) n"),
                                          block_out[half].rearrange("p t d -> p (t d)")).then_inc(stored[half], 16)
                        else:
                            act.dma_start(A["counts"][h, :, :].rearrange("p (t d) -> p t d", d=HALF)[:, :, 0:cols],
                                          block_out[half][:, :, 0:cols]).then_inc(stored[half], 16)

                    whole = NP // HALF
                    weigh_chunk(0, 0)
                    block_of(0, 0, GPH, None)
                    block_of(1, 1, GPH, None)
                    with act.Fori(1, whole // 2) as i:
                        for half in range(2):
                            block_of(2 * i + half, half, GPH, 16 * i)
                    block_of(whole, 0, GROUPS - whole * GPH, 16 * (whole // 2))
                    for c in range(GROUPS // 2 + 1, NC):
                        weigh_chunk(c, c % 2)
                    act.wait_ge(stored[0], 16 * (whole // 2 + 1))
                    act.wait_ge(stored[1], 16 * (whole // 2))
                    act.wait_ge(s["flushed"], GROUPS + BANKS)

            with ExitStack() as st:
                lo_hot = sbuf(st, "m_lo_hot", [P, 2 * PAIRS + 1, P], BF16)
                hi_hot = sbuf(st, "m_hi_hot", [P, 2 * PAIRS + 1, GW], BF16)
                key = sbuf(st, "m_key", [P, 3, PAIRS, 2])
                first_digit = sbuf(st, "first_digit", [P, GW], BF16)
                rest = sbuf(st, "rest", [P, GW])
                digits = [h[:, :, :].bitcast(BF16),
                          type_mem[:, 0:NP].bitcast(BF16).rearrange("p (t d) -> p t d", d=HALF)]
                top = sbuf(st, "top", [P, 1])
                flag = sbuf(st, "flag", [1, 1])
                pF = psum(st, "m_pF")
                banks = psum(st, "m_banks", [P, 2, BANK])
                s = {n: sem(st, f"m_{n}") for n in
                     ("top", "row", "flag", "taken", "made", "keyed", "flushed", "split_a", "split_b", "split", "stored",
                      "y_keyed", "y_made", "y_taken", "begun")}
                st.callback(clear_semaphores)
                block = st.enter_context(nc.Block())

                @block.sync
                def _(sp):
                    flag_reg = sp.alloc_register("m_sp_flag")
                    sp.wait_ge(s["flag"], 2)
                    above = load_flag(sp, s, flag_reg)

                    def store(h_at, cols, groups):
                        sp.wait_ge(s["split"], groups)
                        for k in range(2):
                            sp.dma_start(A["counts"][bass.ds(h_at + (k + 1) * HALVES, 1), :, :]
                                         .rearrange("a p (t d) -> (a p) t d", d=HALF)[:, :, 0:cols],
                                         digits[k][:, :, 0:cols]).then_inc(s["stored"], 16)
                    with sp.If(above > 0):
                        sp.sem_inc(s["stored"], 1)
                        with sp.Fori(0, NP // HALF) as b:
                            store(b, HALF, b * GPH + GPH)
                        store(NP // HALF, NP % HALF, GROUPS)
                        sp.wait_ge(s["stored"], HALVES * 32 + 1)

                @block.tensor
                def _(pe):
                    r = pe.alloc_register("m_pe_r")
                    flag_reg = pe.alloc_register("m_pe_flag")
                    regs = [pe.alloc_register(f"m_pe_g{k}") for k in range(3 * GPR)]
                    pe.wait_ge(s["top"], 1)
                    nc.tensor.transpose(pF[0:1, 0:P], top[:, 0:1], ident[:, :]).then_inc(s["row"], 1)
                    pe.wait_ge(s["flag"], 2)
                    above = load_flag(pe, s, flag_reg)
                    with pe.If(above > 0):
                        pe.reg_mov(r, 0)
                        pe.sem_inc(s["taken"], 2)
                        with pe.Fori(0, GROUNDS) as o:
                            _, more_tiles, _, _ = load_record(pe, regs, o)
                            for k in range(GPR):
                                group_tensor(pe, s, r, o * GPR + k, k, more_tiles[k], banks[:, k % 2, 0:GW],
                                             lo_hot, hi_hot)

                @block.vector
                def _(dve):
                    r = dve.alloc_register("m_dve_r")
                    t = dve.alloc_register("m_dve_t")
                    flag_reg = dve.alloc_register("m_dve_flag")
                    regs = [dve.alloc_register(f"m_dve_g{k}") for k in range(3 * GPR)]
                    nc.vector.tensor_reduce(top[:, :], over[:, :], AXX, ALU.max).then_inc(s["top"], 1)
                    dve.wait_ge(s["row"], 1)
                    nc.vector.tensor_reduce(flag[:, :], pF[0:1, 0:P], AXX, ALU.max).then_inc(s["flag"], 1)
                    dve.wait_ge(s["flag"], 1)
                    nc.vector.tensor_scalar(more[:, :], flag[:, :], 0.0, None, ALU.is_gt).then_inc(s["flag"], 1)
                    dve.wait_ge(s["flag"], 2)
                    above = load_flag(dve, s, flag_reg)

                    def split(g, k, at):
                        bank = banks[:, k % 2, 0:GW]
                        dve.wait_ge(s["taken"], g + 3)
                        nc.vector.tensor_copy(first_digit[:, :], bank).then_inc(s["split_a"], 1)
                        dve.wait_ge(s["split_a"], g + 1)
                        nc.vector.tensor_tensor(rest[:, :], bank, first_digit[:, :], ALU.subtract).then_inc(s["flushed"], 1)
                        dve.wait_ge(s["flushed"], g + 3)
                        second, third = (v[:, :, bass.ds(at, GD)] for v in digits)
                        rest_td = rest[:, :].rearrange("p (t d) -> p t d", d=GD)
                        nc.vector.tensor_copy(second, rest_td).then_inc(s["split_b"], 1)
                        dve.wait_ge(s["split_b"], g + 1)
                        nc.vector.tensor_tensor(third, rest_td, second, ALU.subtract).then_inc(s["split"], 1)
                        dve.wait_ge(s["split"], g + 1)
                    with dve.If(above > 0):
                        dve.reg_mov(r, 0)
                        dve.sem_inc(s["made"], 2)
                        dve.sem_inc(s["flushed"], 2)
                        with dve.Fori(0, GROUNDS) as o:
                            gfirst, more_tiles, _, _ = load_record(dve, regs, o)
                            dve.wait_ge(s["stored"], (o >> 2) * 32 + 1)
                            for k in range(GPR):
                                take_keys(dve, s, o * GPR + k, k, gfirst[k], key)
                                group_vector(dve, s, r, t, o * GPR + k, k, gfirst[k], more_tiles[k],
                                             key, lo_hot, hi_hot)
                                split(o * GPR + k, k, (o & 3) * (GPR * GD) + k * GD)

        w_l1 = edge_scope
        wn1a = sbuf(w_l1, "wn1a", [P, D])
        wn1b = sbuf(w_l1, "wn1b", [P, D])
        wn2 = sbuf(w_l1, "wn2", [P, D])
        we1 = sbuf(w_l1, "we1", [EC, D])
        we2 = sbuf(w_l1, "we2", [P, D])
        cols1 = sbuf(w_l1, "cols1", [P, 4])
        bn1_row = sbuf(w_l1, "bn1_row", [P, D])
        bn2_row = sbuf(w_l1, "bn2_row", [TP, D])

        with ExitStack() as st:
            hT = sbuf(st, "h1T", [P, 2, NCH])
            relu_sum = sbuf(st, "relu_sum", [P, 2, 4, D])
            pT = psum(st, "p1T", [P, 2, BANK])
            pU = psum(st, "p1U", [P, 2, BANK])
            pO = psum(st, "p1O", [P, 2, BANK])
            s = norm_sems(st, "n1")
            s_w, s_T, s_relu, s_x, s_U, s_hT, s_prod, s_out, s_store, s_xh, s_w2 = (
                sem(st, f"n1_{n}") for n in ("w", "T", "sum_relu", "x", "U", "hT", "prod", "out", "store", "xh", "w2"))
            st.callback(clear_semaphores)
            block = st.enter_context(nc.Block())

            @block.sync
            def _(sp):
                sp.dma_start(wn1a[:, :], A["wn1"][0:D, :]).then_inc(s_w, 16)
                sp.dma_start(wn1b[:, :], A["wn1"][D:2 * D, :]).then_inc(s_w, 16)
                sp.dma_start(wn2[:, :], A["wn2"]).then_inc(s_w, 16)
                sp.dma_start(we1[:, :], A["we1"]).then_inc(s_w, 16)
                sp.dma_start(we2[:, :], A["we2"]).then_inc(s_w, 16)
                sp.dma_start(bn1_row[:, :], A["bn1"].unsqueeze(0).to_broadcast([P, D])).then_inc(s_w, 16)
                sp.dma_start(bn2_row[:, :], A["bn2"].unsqueeze(0).to_broadcast([TP, D])).then_inc(s_w, 16)
                with nc.allow_non_contiguous_dma(reason="four columns of biases, once"):
                    for k, name in enumerate(("be1", "be2", "wt", "bt")):
                        sp.dma_start(cols1[:, k:k + 1], A[name].unsqueeze(1)).then_inc(s_w2, 16)
                sp.wait_ge(s_w, 112)
                sp.wait_ge(s_w2, 64)
                sp.wait_ge(s_out, QUADS)
                sp.dma_start(A["table1"].rearrange("(t p) d -> p t d", p=P), h[:, :, :]).then_inc(s_store, 16)
                sp.wait_ge(s_store, 16)

            @block.tensor
            def _(pe):
                for q in range(QUADS):
                    if q >= 2:
                        pe.wait_ge(s_relu, q - 1)
                    for i, t in enumerate(quad(q)):
                        last = nc.tensor.transpose(pT[:, q % 2, i * P:(i + 1) * P],
                                                   acc[:, t * P:(t + 1) * P], ident[:, :])
                    last.then_inc(s_T, 1)
                pe.wait_ge(s["h"], PIECES)
                pe.wait_ge(s_w, 112)
                for q in range(QUADS + 1):
                    if q < QUADS:
                        if q >= 2:
                            pe.wait_ge(s_hT, q - 1)
                        for i, t in enumerate(quad(q)):
                            last = nc.tensor.transpose(pU[:, q % 2, i * P:(i + 1) * P], h[:, t, :], ident[:, :])
                        last.then_inc(s_U, 1)
                    if q >= 1:
                        u = q - 1
                        pe.wait_ge(s_hT, u + 1)
                        if u >= 2:
                            pe.wait_ge(s_out, u - 1)
                        for i, t in enumerate(quad(u)):
                            last = nc.tensor.matmul(pO[:, u % 2, i * D:(i + 1) * D],
                                                    hT[:, u % 2, i * P:(i + 1) * P], wn1a[:, :],
                                                    start=True, stop=True)
                        last.then_inc(s_prod, 1)

            @block.scalar
            def _(act):
                for q in range(QUADS):
                    n = len(quad(q))
                    act.wait_ge(s_T, q + 1)
                    if q >= 2:
                        act.wait_ge(s_x, q - 1)
                    nc.scalar.activation(relu_sum[:, q % 2, 0:n, :],
                                         pT[:, q % 2, 0:n * D].rearrange("p (t d) -> p t d", d=D),
                                         ACT.Relu).then_inc(s_relu, 1)
                norm_scalar(act, s, h)
                for q in range(QUADS):
                    n = len(quad(q)) * P
                    act.wait_ge(s_U, q + 1)
                    if q >= 2:
                        act.wait_ge(s_prod, q - 1)
                    nc.scalar.activation(hT[:, q % 2, 0:n], pU[:, q % 2, 0:n], ACT.Copy).then_inc(s_hT, 1)

            @block.vector
            def _(dve):
                for q in range(QUADS):
                    tiles = slice(quad(q)[0], quad(q)[-1] + 1)
                    dve.wait_ge(s_relu, q + 1)
                    nc.vector.tensor_tensor(x[:, tiles, :], x[:, tiles, :], relu_sum[:, q % 2, 0:len(quad(q)), :],
                                            ALU.add).then_inc(s_x, 1)
                dve.wait_ge(s_x, QUADS)
                norm_vector(dve, s, h)
                dve.wait_ge(s["h"], PIECES)
                nc.vector.tensor_tensor(x[:, :, :], x[:, :, :], h[:, :, :], ALU.add).then_inc(s_xh, 1)
                dve.wait_ge(s_xh, 1)
                for q in range(QUADS):
                    n = len(quad(q))
                    tiles = slice(quad(q)[0], quad(q)[-1] + 1)
                    dve.wait_ge(s_prod, q + 1)
                    nc.vector.tensor_tensor(h[:, tiles, :], pO[:, q % 2, 0:n * D].rearrange("p (t d) -> p t d", d=D),
                                            bn1_row[:, :].unsqueeze(1).to_broadcast([P, n, D]),
                                            ALU.add).then_inc(s_out, 1)

        with ExitStack() as st:
            type_f = sbuf(st, "type_f", [P, COLS])
            type_i = sbuf(st, "type_i", [P, COLS], I32)
            rows = sbuf(st, "e1_rows", [P, NB, J, D])
            staged = sbuf(st, "e1_staged", [P, NB, J], I32)
            onehot = sbuf(st, "e1_onehot", [P, 2, J, W])
            onehot_b = sbuf(st, "e1_onehot_b", [P, 2, J, W], BF16)
            oh_type = sbuf(st, "e1_oh_type", [P, 2, J, TP], BF16)
            edge_in = sbuf(st, "e1_edge", [EC, NB, CH])
            time_in = sbuf(st, "e1_time", [P, NB, CH])
            hid = sbuf(st, "e1_hid", [P, 2, CH])
            tw = sbuf(st, "e1_tw", [P, 2, CH])
            ef = sbuf(st, "e1_ef", [P, 2, CH])
            z = sbuf(st, "e1_z", [P, 2, CH])
            msg = sbuf(st, "e1_msg", [P, 2, J, D])
            win = psum(st, "e1_win")
            p1 = psum(st, "e1_p1", [P, 2, BANK])
            p2 = psum(st, "e1_p2", [P, 2, BANK])
            p3 = psum(st, "e1_p3", [P, 2, BANK])
            s = {n: sem(st, f"e1_{n}") for n in WINDOW_SEMS +
                 ("types", "p1", "hid", "p2", "tw", "ef", "p3", "z", "msg", "type_in")}
            index_in, edges_in, times_in = (
                [sem(st, f"e1_{n}{b}") for b in range(NB)] for n in ("index_in", "edges_in", "times_in"))
            base = gathers()
            st.callback(clear_semaphores)
            block = st.enter_context(nc.Block())

            LAG = 3
            SPR = 2 * NB

            def run_steps(eng, step, load_meta=lambda first: None):
                load_meta(0)
                for c in range(NB):
                    step(c, c, True)
                with eng.Fori(0, (NC - NB) // SPR) as o:
                    load_meta(o * SPR + NB - LAG)
                    for b in range(SPR):
                        step(o * SPR + NB + b, b, False)
                load_meta(NC - SPR)
                for c in range(NC, NC + LAG):
                    step(c, c, True)

            def summed(c, b, edge):
                return b if not edge else 0 if c < NB else c - LAG - (NC - SPR)

            def live(c, edge):
                return not edge or 0 <= c < NC

            @block.sync
            def _(sp):
                def load(b, c, o):
                    if o is not None:
                        sp.wait_ge(rows_in[b], base + 16 * J * o)
                    sp.dma_start(staged[:, b, :], src_idx[:, bass.ds(c * J, J)]).then_inc(index_in[b], 16)
                    if o is not None:
                        sp.wait_ge(s["p1"], c - (NB - 1))
                    sp.dma_start(edge_in[:, b, :], A["edge_T"][bass.ds(c, 1), :, :]
                                 .rearrange("a k e -> (a k) e")).then_inc(edges_in[b], 16)
                sp.dma_start(type_i[:, :], A["type_cols"]).then_inc(s["type_in"], 16)
                for b in range(NB):
                    load(b, b, None)
                with sp.Fori(1, ROUNDS) as o:
                    for b in range(NB):
                        load(b, o * NB + b, o)

            @block.gpsimd
            def _(pool):
                def gather(b, c, o, first):
                    pool.wait_ge(index_in[b], o * 16 + 16)
                    if not first:
                        pool.wait_ge(s["z"], c - (NB - 1))
                    pool.sem_inc(s["begun"], 1)
                    for j in range(J):
                        pool.indirect_dma_start(
                            rows[:, b, j, :], None, A["table1"],
                            bass.IndirectOffsetOnAxis(ap=staged[:, b, j:j + 1], axis=0),
                        ).then_inc(rows_in[b], 16)
                for b in range(NB):
                    gather(b, b, 0, True)
                with pool.Fori(1, ROUNDS) as o:
                    for b in range(NB):
                        gather(b, o * NB + b, o, False)

            @block.tensor
            def _(pe):
                q = pe.alloc_register("e1_pe_q")
                regs = [pe.alloc_register(f"e1_pe_m{k}") for k in range(2 * SPR)]
                pe.reg_mov(q, 0)
                spans = []

                def load_meta(first):
                    spans[:] = window_meta(pe, regs, first)[1]

                def step(c, b, edge):
                    if live(c, edge):
                        pe.wait_ge(edges_in[b % NB], (c - b % NB) * (16 // NB) + 16)
                        if not edge or c >= 2:
                            pe.wait_ge(s["hid"], c - 1)
                        nc.tensor.matmul(p1[:, b % 2, :], we1[:, :], edge_in[:, b % NB, :],
                                         start=True, stop=True).then_inc(s["p1"], 1)
                    if live(c - 1, edge):
                        pe.wait_ge(s["hid"], c)
                        if not edge or c - 1 >= 2:
                            pe.wait_ge(s["ef"], c - 2)
                        nc.tensor.matmul(p2[:, (b - 1) % 2, :], we2[:, :], hid[:, (b - 1) % 2, :],
                                         start=True, stop=True).then_inc(s["p2"], 1)
                    if live(c - 3, edge):
                        pe.wait_ge(s["msg"], c - 2)
                        sources = msg[:, (b - 3) % 2, :, :], onehot[:, (b - 3) % 2, :, :], win, \
                            oh_type[:, (b - 3) % 2, :, :], onehot_b[:, (b - 3) % 2, :, :]
                        window_tensor(pe, s, c - 3, *sources)
                    if live(c - 2, edge):
                        pe.wait_ge(s["ef"], c - 1)
                        if not edge or c - 2 >= 2:
                            pe.wait_ge(s["z"], c - 3)
                        for j in range(J):
                            last = nc.tensor.matmul(p3[:, (b - 2) % 2, j * P:(j + 1) * P],
                                                    ef[:, (b - 2) % 2, j * P:(j + 1) * P], wn1b[:, :],
                                                    start=True, stop=True)
                        last.then_inc(s["p3"], 1)
                    if live(c - 3, edge):
                        more_windows_tensor(pe, s, q, spans[summed(c, b, edge)], *sources)
                run_steps(pe, step, load_meta)

            @block.scalar
            def _(act):
                def load_time(c, b):
                    act.dma_start(time_in[:, b % NB, :], A["time_rows"][bass.ds(c, 1), :]
                                  .to_broadcast([P, CH])).then_inc(times_in[b % NB], 16)
                for b in range(NB - 1):
                    load_time(b, b)

                def step(c, b, edge):
                    if not edge or c + NB - 1 < NC:
                        if not edge or c >= 1:
                            act.wait_ge(s["tw"], c)
                        load_time(c + NB - 1, b + NB - 1)
                    if live(c, edge):
                        act.wait_ge(times_in[b % NB], (c - b % NB) * (16 // NB) + 16)
                        if not edge or c >= 2:
                            act.wait_ge(s["ef"], c - 1)
                        nc.scalar.activation(tw[:, b % 2, :], time_in[:, b % NB, :], ACT.Sigmoid,
                                             bias=cols1[:, 3:4], scale=cols1[:, 2:3]).then_inc(s["tw"], 1)
                        act.wait_ge(s["p1"], c + 1)
                        if not edge or c >= 2:
                            act.wait_ge(s["p2"], c - 1)
                        nc.scalar.activation(hid[:, b % 2, :], p1[:, b % 2, :], ACT.Relu,
                                             bias=cols1[:, 0:1]).then_inc(s["hid"], 1)
                    if live(c - 2, edge):
                        act.wait_ge(s["z"], c - 1)
                        if not edge or c - 2 >= 2:
                            act.wait_ge(s["chunk_done"], c - 3)
                        nc.scalar.activation(msg[:, (b - 2) % 2, :, :].rearrange("p j d -> p (j d)"),
                                             z[:, (b - 2) % 2, :], ACT.Relu).then_inc(s["msg"], 1)

                for c in range(NB):
                    step(c, c, True)
                with act.Fori(0, (NC - NB) // SPR - 1) as o:
                    for b in range(SPR):
                        step(o * SPR + NB + b, NB + b, False)
                for c in range(NC - SPR, NC + LAG):
                    step(c, c, True)

            @block.vector
            def _(dve):
                q = dve.alloc_register("e1_dve_q")
                first = dve.alloc_register("e1_dve_first")
                regs = [dve.alloc_register(f"e1_dve_m{k}") for k in range(2 * SPR)]
                nc.vector.memset(acc[:, :], 0.0).then_inc(s["cleared"], 1)
                nc.vector.memset(typeT[:, :], 0.0).then_inc(s["cleared"], 1)
                dve.wait_ge(s["type_in"], 16)
                nc.vector.tensor_scalar(type_f[:, :], type_i[:, :], 0.0, float(NTYPE - 1),
                                        ALU.max, ALU.min).then_inc(s["cleared"], 1)
                dve.wait_ge(s["cleared"], 3)
                dve.reg_mov(q, 0)
                dve.sem_inc(s["added"], 1)
                m = []

                def load_meta(first_chunk):
                    m[:] = window_meta(dve, regs, first_chunk)

                def step(c, b, edge):
                    if live(c - 2, edge):
                        k = (b - 2) % 2
                        nc.vector.tensor_tensor(
                            oh_type[:, k, :, :], iota_w[:, 0:TP].unsqueeze(1).to_broadcast([P, J, TP]),
                            type_f[:, bass.ds((c - 2) * J, J)].unsqueeze(2).to_broadcast([P, J, TP]),
                            ALU.is_equal).then_inc(s["types"], 1)
                        open_window(s, c - 2, onehot[:, k, :, :], onehot_b[:, k, :, :])
                    if live(c - 1, edge):
                        dve.wait_ge(s["p2"], c)
                        dve.wait_ge(s["tw"], c)
                        if not edge or c - 1 >= 2:
                            dve.wait_ge(s["p3"], c - 2)
                        k = (b - 1) % 2
                        nc.vector.scalar_tensor_tensor(ef[:, k, :], p2[:, k, :], cols1[:, 1:2], tw[:, k, :],
                                                       ALU.add, ALU.mult).then_inc(s["ef"], 1)
                    if live(c - 3, edge):
                        least, span = (v[summed(c, b, edge)] for v in m)
                        k = (b - 3) % 2
                        close_window(dve, s, q, first, c - 3, least, span, onehot[:, k, :, :], win,
                                     onehot_b=onehot_b[:, k, :, :])
                    if live(c - 2, edge):
                        dve.wait_ge(s["p3"], c - 1)
                        k = (b - 2) % 2
                        slot = (b - 2) % NB
                        dve.wait_ge(rows_in[slot], base + (c - 2 - slot) * (16 * J // NB) + 16 * J)
                        if not edge or c - 2 >= 2:
                            dve.wait_ge(s["msg"], c - 3)
                        nc.vector.tensor_tensor(z[:, k, :], p3[:, k, :],
                                                rows[:, (b - 2) % NB, :, :].rearrange("p j d -> p (j d)"),
                                                ALU.add).then_inc(s["z"], 1)
                run_steps(dve, step, load_meta)

        with ExitStack() as st:
            pO = psum(st, "p2O", [P, 2, BANK])
            pD = psum(st, "p2D")
            s = norm_sems(st, "n2")
            s_O, s_x, s_D, s_deg, s_root = (sem(st, f"n2_{n}") for n in ("O", "x", "D", "deg", "root"))
            st.callback(clear_semaphores)
            block = st.enter_context(nc.Block())

            @block.tensor
            def _(pe):
                for t in range(NT):
                    nc.tensor.matmul(pD[:, t:t + 1], typeT[:, t * P:(t + 1) * P], ones[0:TP, 0:1],
                                     start=True, stop=True).then_inc(s_D, 1)
                for q in range(QUADS):
                    if q >= 2:
                        pe.wait_ge(s_x, q - 1)
                    for i, t in enumerate(quad(q)):
                        to = pO[:, q % 2, i * D:(i + 1) * D]
                        nc.tensor.matmul(to, acc[:, t * P:(t + 1) * P], wn2[:, :], start=True, stop=False)
                        last = nc.tensor.matmul(to, typeT[:, t * P:(t + 1) * P], bn2_row[:, :], start=False, stop=True)
                    last.then_inc(s_O, 1)

            @block.vector
            def _(dve):
                dve.wait_ge(s_D, NT)
                nc.vector.tensor_scalar(dinv[:, :], pD[:, 0:NT], 1.0, 1.0, ALU.add, ALU.max).then_inc(s_deg, 1)
                for q in range(QUADS):
                    n = len(quad(q))
                    tiles = slice(quad(q)[0], quad(q)[-1] + 1)
                    dve.wait_ge(s_O, q + 1)
                    nc.vector.tensor_tensor(x[:, tiles, :], x[:, tiles, :],
                                            pO[:, q % 2, 0:n * D].rearrange("p (t d) -> p t d", d=D),
                                            ALU.add).then_inc(s_x, 1)
                dve.wait_ge(s_x, QUADS)
                norm_vector(dve, s, h)
                dve.wait_ge(s_root, 1)
                nc.vector.reciprocal(dinv[:, :], dinv[:, :]).then_inc(s_deg, 1)
                dve.wait_ge(s_deg, 2)

            @block.scalar
            def _(act):
                act.wait_ge(s_deg, 1)
                nc.scalar.activation(dinv[:, :], dinv[:, :], ACT.Sqrt).then_inc(s_root, 1)
                norm_scalar(act, s, h)
                act.wait_ge(s["h"], PIECES)

        edge_scope.close()

        def split_scalar(act, s, parts, source, at, size, count, gap):
            dst = [parts[k][:, bass.ds(at, size), :] for k in range(3)]
            nc.scalar.activation(dst[0], source, ACT.Copy).then_inc(s["part"], 1)
            act.wait_ge(s["rest"], 2 * count + 1)
            nc.scalar.activation(dst[1], gap, ACT.Copy).then_inc(s["part"], 1)
            act.wait_ge(s["rest"], 2 * count + 2)
            nc.scalar.activation(dst[2], gap, ACT.Copy).then_inc(s["part"], 1)

        def split_vector(dve, s, parts, source, at, size, count, gap):
            dve.wait_ge(s["part"], 3 * count + 1)
            nc.vector.tensor_tensor(gap, source, parts[0][:, bass.ds(at, size), :], ALU.subtract).then_inc(s["rest"], 1)
            dve.wait_ge(s["part"], 3 * count + 2)
            nc.vector.tensor_tensor(gap, gap, parts[1][:, bass.ds(at, size), :], ALU.subtract).then_inc(s["rest"], 1)

        def split_all(tag, parts):
            with ExitStack() as st:
                gap = sbuf(st, f"{tag}_gap", [P, 3, PT, D])
                s = {n: sem(st, f"{tag}_{n}") for n in ("part0", "part1", "part2", "gap1", "gap2")}
                st.callback(clear_semaphores)
                block = st.enter_context(nc.Block())

                @block.scalar
                def _(act):
                    for k in range(PIECES + 2):
                        if k < PIECES:
                            nc.scalar.activation(parts[0][:, piece(k), :], h[:, piece(k), :], ACT.Copy).then_inc(s["part0"], 1)
                        if 0 <= k - 1 < PIECES:
                            act.wait_ge(s["gap1"], k)
                            nc.scalar.activation(parts[1][:, piece(k - 1), :], gap[:, (k - 1) % 3, :, :],
                                                 ACT.Copy).then_inc(s["part1"], 1)
                        if 0 <= k - 2 < PIECES:
                            act.wait_ge(s["gap2"], k - 1)
                            nc.scalar.activation(parts[2][:, piece(k - 2), :], gap[:, (k - 2) % 3, :, :],
                                                 ACT.Copy).then_inc(s["part2"], 1)
                    act.wait_ge(s["part2"], PIECES)

                @block.vector
                def _(dve):
                    for k in range(PIECES + 1):
                        if k < PIECES:
                            dve.wait_ge(s["part0"], k + 1)
                            if k >= 3:
                                dve.wait_ge(s["part2"], k - 2)
                            nc.vector.tensor_tensor(gap[:, k % 3, :, :], h[:, piece(k), :], parts[0][:, piece(k), :],
                                                    ALU.subtract).then_inc(s["gap1"], 1)
                        if k >= 1:
                            dve.wait_ge(s["part1"], k)
                            nc.vector.tensor_tensor(gap[:, (k - 1) % 3, :, :], gap[:, (k - 1) % 3, :, :],
                                                    parts[1][:, piece(k - 1), :], ALU.subtract).then_inc(s["gap2"], 1)

        whole_chunks = NP // NCH
        last_tiles = NT - whole_chunks * (NCH // P)

        def run_chunks(step):
            def go(eng):
                tiles = NCH // P
                step(0, 0, tiles, 0)
                with eng.Fori(0, (whole_chunks - 2) // 2) as i:
                    step(2 * i + 1, 1, tiles, tiles)
                    step(2 * i + 2, 0, tiles, tiles)
                step(whole_chunks - 1, 1, tiles, tiles)
                step(whole_chunks, 0, last_tiles, tiles)
                step(whole_chunks + 1, 1, 0, last_tiles)
            return go

        def counts_in(to, c, plane, at, tiles):
            n = PT * HALF
            if tiles == NCH // P:
                src = A["counts"][bass.ds(c * 2 + plane * HALVES, 2), :, bass.ds(at, n)]
                return to[:, :, :, :].rearrange("p h t d -> p h (t d)"), src.rearrange("h p n -> p h n")
            src = A["counts"][bass.ds(c * 2 + plane * HALVES, 1), :, bass.ds(at, n)]
            return (to[:, 0, :, 0:tiles * P],
                    src.rearrange("h p (t d) -> (h p) t d", d=HALF)[:, :, 0:tiles * P])

        def load_counts(sp, s, loaded, ring, digit_ring):
            flag_reg = sp.alloc_register(f"flag_{s['used'].name}")
            above = load_flag(sp, s, flag_reg)

            def chunk(c, tiles):
                for j in range(PIECES):
                    sp.wait_ge(s["used"], c * PIECES + j + 1)
                    sp.dma_start(*counts_in(ring[:, j, :, :, :], c, 0, j * PT * HALF, tiles)).then_inc(loaded[j], 16)
                with sp.If(above > 0):
                    with sp.Fori(1, PLANES) as plane:
                        with sp.Fori(0, PIECES) as j:
                            sp.wait_ge(s["d_used"], (c * (PLANES - 1) + plane - 1) * PIECES + j + 1)
                            sp.dma_start(*counts_in(digit_ring, c, plane, j * (PT * HALF), tiles)).then_inc(s["d_loaded"], 16)
            with sp.Fori(0, whole_chunks) as c:
                chunk(c, NCH // P)
            chunk(whole_chunks, last_tiles)

        def product_setup(pe, s):
            pe.sem_inc(s["used"], PIECES)
            pe.sem_inc(s["d_used"], 1)
            return load_flag(pe, s, pe.alloc_register(f"flag_pe_{s['used'].name}"))

        def product(pe, s, above, loaded, ring, digit_ring, parts, sums, c, k, tiles, self_loops):
            width = tiles * P

            def tile_products(block, i, t, start=False, stop=False):
                if tiles == NCH // P:
                    counts, to = block[:, :, i, :], sums[:, k, :].rearrange("p (h d) -> p h d", d=HALF)
                else:
                    counts, to = block[:, 0, i, 0:width], sums[:, k, 0:width]
                for part in range(3):
                    last = nc.tensor.matmul(to, parts[part][:, bass.ds(t, 1), :], counts,
                                            start=(start and part == 0), stop=(stop and part == 2))
                return last

            pe.wait_ge(s["out"], c + 1)
            for j in range(PIECES):
                pe.wait_ge(loaded[j], c * 16 + 16)
                if j == PIECES - 1:
                    with pe.If(above > 0):
                        with pe.Fori(1, PLANES) as plane:
                            with pe.Fori(0, PIECES) as m:
                                n = (c * (PLANES - 1) + plane - 1) * PIECES + m
                                pe.wait_ge(s["d_loaded"], n * 16 + 16)
                                for i in range(PT):
                                    last = tile_products(digit_ring, i, m * PT + i)
                                last.then_inc(s["d_used"], 1)
                for i in range(PT):
                    t = j * PT + i
                    last = tile_products(ring[:, j, :, :, :], i, t, t == 0, t == NT - 1)
                last.then_inc(s["used"], 1)
                for i in range(tiles if self_loops and j == 0 else 0):
                    for part in range(3):
                        nc.tensor.matmul(sums[:, k, i * P:(i + 1) * P],
                                         parts[part][:, bass.ds(c * (NCH // P) + i, 1), :], ident_b[:, :],
                                         start=False, stop=False, skip_group_check=True)

        with ExitStack() as l2:
            parts = [sbuf(l2, f"parts2{k}", [P, NT, D], BF16)[:, :, :] for k in range(3)]
            split_all("split2", parts)
            with ExitStack() as st:
                ring = sbuf(st, "ring2", [P, PIECES, 2, PT, HALF], BF16)
                digit_ring = sbuf(st, "digit_ring2", [P, 2, PT, HALF], BF16)
                agg = sbuf(st, "agg2", [P, 2, NCH])
                wmsg = sbuf(st, "wmsg", [P, D])
                emb = sbuf(st, "emb", [TP, D])
                bmsg = sbuf(st, "bmsg", [TP, D])
                wih = sbuf(st, "wih", [P, 3 * D])
                whh = sbuf(st, "whh", [P, 3 * D])
                bih = sbuf(st, "bih", [P, 3 * D])
                bhh = sbuf(st, "bhh", [P, 3 * D])
                held = sbuf(st, "held", [P, 2, 4, D])
                mT = sbuf(st, "mT", [P, NCH])
                hT = sbuf(st, "hT", [P, NCH])
                rz = sbuf(st, "rz", [P, 4, 2 * D])
                pre = sbuf(st, "pre", [P, 4, D])
                new_in = sbuf(st, "new_in", [P, 4, D])
                new = sbuf(st, "new", [P, 4, D])
                sums = psum(st, "p3S", [P, 2, BANK])
                pM = psum(st, "p3M")
                pT = psum(st, "p3T")
                pR = psum(st, "p3R", [P, 2, BANK])
                pN = psum(st, "p3N", [P, 2, BANK])
                s = {n: sem(st, f"n3_{n}") for n in
                     ("used", "out", "w", "bias", "MT", "mh", "gates", "biased", "rz_in", "rz", "pre", "new", "v", "x", "held",
                      "begun", "d_used", "d_loaded")}
                loaded = [sem(st, f"n3_loaded{j}") for j in range(PIECES)]
                st.callback(clear_semaphores)
                block = st.enter_context(nc.Block())
                G2 = slice(0, 2 * D)
                G1 = slice(2 * D, 3 * D)

                @block.sync
                def _(sp):
                    load_counts(sp, s, loaded, ring, digit_ring)

                @block.gpsimd
                def _(pool):
                    pool.dma_start(wmsg[:, :], A["wmsgT"]).then_inc(weights_in[0], 16)
                    pool.dma_start(emb[:, :], A["emb"]).then_inc(weights_in[0], 16)
                    pool.dma_start(bmsg[:, :], A["bmsg"].unsqueeze(0).to_broadcast([TP, D])).then_inc(weights_in[0], 16)
                    pool.dma_start(wih[:, :], A["wihT"]).then_inc(weights_in[0], 16)
                    pool.dma_start(whh[:, :], A["whhT"]).then_inc(weights_in[0], 16)
                    pool.dma_start(bih[:, :], A["bih"].unsqueeze(0).to_broadcast([P, 3 * D])).then_inc(weights_in[0], 16)
                    pool.dma_start(bhh[:, :], A["bhh"].unsqueeze(0).to_broadcast([P, 3 * D])).then_inc(weights_in[0], 16)

                @block.tensor
                def _(pe):
                    above = product_setup(pe, s)
                    pe.wait_ge(weights_in[0], 112)

                    def step(c, k, tiles, before):
                        if tiles:
                            product(pe, s, above, loaded, ring, digit_ring, parts, sums, c, k, tiles, False)
                        if not before:
                            return
                        u = c - 1
                        width = before * P
                        cols = bass.ds(u * NCH, width)
                        pe.wait_ge(s["out"], u + 3)
                        pe.wait_ge(s["held"], u + 1)
                        nc.tensor.matmul(pM[:, 0:width], wmsg[:, :], agg[:, (k + 1) % 2, 0:width], start=True, stop=False)
                        nc.tensor.matmul(pM[:, 0:width], emb[:, :], typeT[:, cols], start=False, stop=True)
                        for i in range(before):
                            last = nc.tensor.transpose(pT[:, i * P:(i + 1) * P],
                                                       held[:, (k + 1) % 2, i, :], ident[:, :])
                        last.then_inc(s["MT"], 1)
                        pe.wait_ge(s["mh"], u + 1)
                        for i in range(before):
                            tile = slice(i * P, (i + 1) * P)
                            to = pR[:, i // 2, (i % 2) * 2 * D:(i % 2 + 1) * 2 * D]
                            nc.tensor.matmul(to, mT[:, tile], wih[:, G2], start=True, stop=False)
                            nc.tensor.matmul(to, hT[:, tile], whh[:, G2], start=False, stop=True)
                            to = pN[:, i // 2, (i % 2) * 2 * D:(i % 2) * 2 * D + D]
                            nc.tensor.matmul(to, mT[:, tile], wih[:, G1], start=True, stop=True)
                            to = pN[:, i // 2, (i % 2) * 2 * D + D:(i % 2 + 1) * 2 * D]
                            last = nc.tensor.matmul(to, hT[:, tile], whh[:, G1], start=True, stop=True)
                        last.then_inc(s["gates"], 1)
                    pe.wait_ge(s["bias"], 2)
                    run_chunks(step)(pe)

                @block.scalar
                def _(act):
                    act.sem_inc(s["out"], 2)

                    def step(c, k, tiles, before):
                        if before:
                            u = c - 1
                            width = before * P
                            act.wait_ge(s["MT"], u + 1)
                            nc.scalar.activation(mT[:, 0:width], pM[:, 0:width], ACT.Copy)
                            nc.scalar.activation(hT[:, 0:width], pT[:, 0:width], ACT.Copy).then_inc(s["mh"], 1)
                            act.wait_ge(s["rz_in"], u + 1)
                            nc.scalar.activation(rz[:, 0:before, :], rz[:, 0:before, :], ACT.Sigmoid).then_inc(s["rz"], 1)
                            act.wait_ge(s["pre"], u + 1)
                            nc.scalar.activation(new[:, 0:before, :], pre[:, 0:before, :], ACT.Tanh).then_inc(s["new"], 1)
                            act.wait_ge(s["x"], u + 1)
                        if tiles:
                            act.wait_ge(s["used"], c * PIECES + 2 * PIECES)
                            nc.scalar.activation(agg[:, k, 0:tiles * P], sums[:, k, 0:tiles * P],
                                                 ACT.Copy).then_inc(s["out"], 1)
                    run_chunks(step)(act)

                @block.vector
                def _(dve):
                    dve.wait_ge(weights_in[0], 112)
                    nc.vector.tensor_tensor(bih[:, G2], bih[:, G2], bhh[:, G2], ALU.add).then_inc(s["bias"], 1)
                    nc.vector.tensor_tensor(emb[:, :], emb[:, :], bmsg[:, :], ALU.add).then_inc(s["bias"], 1)
                    dve.wait_ge(s["bias"], 2)

                    def step(c, k, tiles, before):
                        if before:
                            gru(c - 1, before)
                        if tiles:
                            nc.vector.tensor_copy(held[:, k, 0:tiles, :],
                                                  h[:, bass.ds(c * 4, tiles), :]).then_inc(s["held"], 1)

                    def gru(u, before):
                        dve.wait_ge(s["gates"], u + 1)
                        b = slice(0, before)

                        def add_bias(to, bank, part, row):
                            for i in range(0, before, 2):
                                n = min(2, before - i)
                                pair = bank[:, i // 2, 0:n * 2 * D].rearrange("p (i g) -> p i g", i=n)[:, :, part]
                                last = nc.vector.tensor_tensor(
                                    to[:, i:i + n, :], pair,
                                    row.unsqueeze(1).to_broadcast([P, n, part.stop - part.start]), ALU.add)
                            return last
                        add_bias(rz, pR, slice(0, 2 * D), bih[:, G2]).then_inc(s["rz_in"], 1)
                        add_bias(pre, pN, slice(D, 2 * D), bhh[:, G1])
                        add_bias(new_in, pN, slice(0, D), bih[:, G1]).then_inc(s["biased"], 1)
                        dve.wait_ge(s["biased"], u + 1)
                        dve.wait_ge(s["rz"], u + 1)
                        nc.vector.tensor_tensor(pre[:, b, :], rz[:, b, 0:D], pre[:, b, :], ALU.mult).then_inc(s["v"], 1)
                        dve.wait_ge(s["v"], u * 4 + 1)
                        nc.vector.tensor_tensor(pre[:, b, :], pre[:, b, :], new_in[:, b, :], ALU.add).then_inc(s["pre"], 1)
                        dve.wait_ge(s["new"], u + 1)
                        at = bass.ds(u * 4, before)
                        nc.vector.tensor_tensor(pre[:, b, :], h[:, at, :], new[:, b, :], ALU.subtract).then_inc(s["v"], 1)
                        nc.vector.tensor_tensor(x[:, at, :], x[:, at, :], new[:, b, :], ALU.add).then_inc(s["v"], 1)
                        dve.wait_ge(s["v"], u * 4 + 3)
                        nc.vector.tensor_tensor(pre[:, b, :], pre[:, b, :], rz[:, b, D:2 * D], ALU.mult).then_inc(s["v"], 1)
                        dve.wait_ge(s["v"], u * 4 + 4)
                        nc.vector.tensor_tensor(x[:, at, :], x[:, at, :], pre[:, b, :], ALU.add).then_inc(s["x"], 1)
                    run_chunks(step)(dve)

        with ExitStack() as st:
            s = norm_sems(st, "n4")
            st.callback(clear_semaphores)
            block = st.enter_context(nc.Block())

            @block.vector
            def _(dve):
                norm_vector(dve, s, h, extra_scale=dinv)

            @block.scalar
            def _(act):
                norm_scalar(act, s, h)
                act.wait_ge(s["h"], PIECES)

        h_b = h[:, :, :].rearrange("p t d -> p (t d)").bitcast(BF16)
        parts = [[sbuf(root, f"parts3{k}", [P, NT, D], BF16)[:, :, :] for k in range(3)],
                 [v.rearrange("p (t d) -> p t d", d=D) for v in
                  (h_b[:, 0:NP], h_b[:, NP:2 * NP], type_mem[:, :].bitcast(BF16)[:, 0:NP])]]
        split_all("split3", parts[0])
        for conv in range(3):
            last_conv = conv == 2
            with ExitStack() as st:
                now, then = parts[conv % 2], parts[(conv + 1) % 2]
                ring = sbuf(st, f"ring3{conv}", [P, PIECES, 2, PT, HALF], BF16)
                digit_ring = sbuf(st, f"digit_ring3{conv}", [P, 2, PT, HALF], BF16)
                agg = sbuf(st, f"c{conv}_agg", [P, 2, NCH])
                w = sbuf(st, f"c{conv}_w", [P, D])
                bias = sbuf(st, f"c{conv}_bias", [P, D])
                y = sbuf(st, f"c{conv}_y", [P, 4, D])
                gap = sbuf(st, f"c{conv}_gap", [P, 4, D])
                sums = psum(st, f"c{conv}_sums", [P, 2, BANK])
                pO = psum(st, f"c{conv}_pO")
                s = {n: sem(st, f"c{conv}_{n}") for n in
                     ("used", "out", "O", "y", "h", "part", "rest", "x", "begun",
                      "d_used", "d_loaded")}
                loaded = [sem(st, f"c{conv}_loaded{j}") for j in range(PIECES)]
                s_store = sem(st, f"c{conv}_store")
                w_base = weights_seen(32)
                st.callback(clear_semaphores)
                block = st.enter_context(nc.Block())

                @block.gpsimd
                def _(pool):
                    pool.dma_start(w[:, :], A[f"convT{conv}"]).then_inc(weights_in[0], 16)
                    pool.dma_start(bias[:, :], A[f"conv_b{conv}"].unsqueeze(0).to_broadcast([P, D])).then_inc(weights_in[0], 16)

                @block.sync
                def _(sp):
                    load_counts(sp, s, loaded, ring, digit_ring)
                    if last_conv:
                        sp.wait_ge(s["x"], whole_chunks + 1)
                        whole = N // P
                        sp.dma_start(A["out"][0:whole * P, :].rearrange("(t p) d -> p t d", p=P),
                                     x[:, 0:whole, :]).then_inc(s_store, 16)
                        sp.dma_start(A["out"][whole * P:N, :], x[0:N - whole * P, whole, :]).then_inc(s_store, 16)
                        sp.wait_ge(s_store, 32)

                @block.tensor
                def _(pe):
                    above = product_setup(pe, s)
                    pe.wait_ge(weights_in[0], w_base + 32)

                    def step(c, k, tiles, before):
                        if tiles:
                            product(pe, s, above, loaded, ring, digit_ring, now, sums, c, k, tiles, True)
                        if before:
                            pe.wait_ge(s["out"], c + 2)
                            for i in range(before):
                                last = nc.tensor.matmul(pO[:, i * P:(i + 1) * P],
                                                        agg[:, (k + 1) % 2, i * P:(i + 1) * P], w[:, :],
                                                        start=True, stop=True)
                            last.then_inc(s["O"], 1)
                    run_chunks(step)(pe)

                @block.scalar
                def _(act):
                    act.sem_inc(s["out"], 2)

                    def step(c, k, tiles, before):
                        if before:
                            u = c - 1
                            act.wait_ge(s["y"], u + 1)
                            if not last_conv:
                                for i in range(before):
                                    last = nc.scalar.activation(y[:, i, :], y[:, i, :], ACT.Relu,
                                                                scale=dinv[:, bass.ds(u * 4 + i, 1)])
                                last.then_inc(s["h"], 1)
                                act.wait_ge(s["h"], u + 1)
                                split_scalar(act, s, then, y[:, 0:before, :], u * 4, before, u, gap[:, 0:before, :])
                                act.wait_ge(s["part"], 3 * u + 3)
                        if tiles:
                            act.wait_ge(s["used"], c * PIECES + 2 * PIECES)
                            nc.scalar.activation(agg[:, k, 0:tiles * P], sums[:, k, 0:tiles * P],
                                                 ACT.Copy).then_inc(s["out"], 1)
                    run_chunks(step)(act)

                @block.vector
                def _(dve):
                    dve.wait_ge(weights_in[0], w_base + 32)

                    def step(c, k, tiles, before):
                        if not before:
                            return
                        u = c - 1
                        dve.wait_ge(s["O"], u + 1)
                        for i in range(before):
                            last = nc.vector.scalar_tensor_tensor(y[:, i, :], pO[:, i * P:(i + 1) * P],
                                                                  dinv[:, bass.ds(u * 4 + i, 1)], bias[:, :],
                                                                  ALU.mult, ALU.add)
                        last.then_inc(s["y"], 1)
                        if last_conv:
                            dve.wait_ge(s["y"], u + 1)
                            at = bass.ds(u * 4, before)
                            nc.vector.tensor_tensor(x[:, at, :], x[:, at, :], y[:, 0:before, :], ALU.add).then_inc(s["x"], 1)
                            dve.wait_ge(s["x"], u + 1)
                        else:
                            dve.wait_ge(s["h"], u + 1)
                            split_vector(dve, s, then, y[:, 0:before, :], u * 4, before, u, gap[:, 0:before, :])
                            dve.wait_ge(s["part"], 3 * u + 3)
                    run_chunks(step)(dve)


def kernel(**inputs):
    import numpy as np
    import concourse.bacc as bacc
    from concourse.bass_utils import run_bass_kernel_spmd

    a = {k: np.asarray(v) for k, v in inputs.items()}

    def edges(name, fill=0):
        v = a[name].reshape(E)
        return np.concatenate([v, np.broadcast_to(np.asarray(fill, v.dtype), (EP - E,))])

    def by_partition(v):
        return np.ascontiguousarray(v.reshape(COLS, P).T)

    dst = edges("dst", N)
    attr = np.concatenate([a["edge_attr_64"], np.zeros((EP - E, EC), np.float32)])
    arrays = {
        "x": np.concatenate([a["x"], np.zeros((NP - N, D), np.float32)]),
        "src_cols": by_partition(edges("src", np.arange(EP - E))),
        "rel_cols": by_partition(edges("edge_type_8")),
        "type_cols": by_partition(edges("edge_type_9")),
        "dst_cols": by_partition(dst),
        "dst_rows": dst.reshape(NC, CH),
        "weight_cols": by_partition(edges("edge_weight1")),
        "time_rows": edges("edge_weight").reshape(NC, CH),
        "edge_T": np.ascontiguousarray(attr.reshape(NC, CH, EC).transpose(0, 2, 1)),
        "w0": a["L0_gnn_weight"], "g0": a["L0_gnn_gate_weight"],
        "we1": a["L1_gnn_We1"], "be1": a["L1_gnn_be1"], "we2": a["L1_gnn_We2"], "be2": a["L1_gnn_be2"],
        "wt": a["L1_gnn_Wt"].reshape(D), "bt": a["L1_gnn_bt"],
        "wn1": a["L1_gnn_Wn1"], "bn1": a["L1_gnn_bn1"], "wn2": a["L1_gnn_Wn2"], "bn2": a["L1_gnn_bn2"],
        "wmsgT": a["L2_gnn_W_msg"].T, "bmsg": a["L2_gnn_b_msg"],
        "emb": np.concatenate([a["L2_gnn_edge_embed"], np.zeros((TP - NTYPE, D), np.float32)]),
        "wihT": a["L2_gnn_W_ih"].T, "whhT": a["L2_gnn_W_hh"].T, "bih": a["L2_gnn_b_ih"], "bhh": a["L2_gnn_b_hh"],
        "convT0": a["L3_gnn_W1"].T, "conv_b0": a["L3_gnn_b1"],
        "convT1": a["L3_gnn_W2"].T, "conv_b1": a["L3_gnn_b2"],
        "convT2": a["L3_gnn_W3"].T, "conv_b2": a["L3_gnn_b3"],
    }
    nc = bacc.Bacc("TRN2", target_bir_lowering=False, num_devices=1)
    aps = {}
    for name in arrays:
        arrays[name] = np.ascontiguousarray(arrays[name])
        aps[name] = nc.dram_tensor(f"in_{name}", arrays[name].shape, mybir.dt.from_np(arrays[name].dtype),
                                   kind="ExternalInput").ap()
    scratch = {"meta": ([NC, 2], I32), "groups": ([GROUNDS * 2, GPR], I32), "tiles": ([2, COLS], F32),
               "table0": ([NP * R, D], F32), "table1": ([NP, D], F32),
               "counts": ([PLANES * HALVES, P, NT * HALF], BF16)}
    for name, (shape, dt) in scratch.items():
        aps[name] = nc.dram_tensor(f"scratch_{name}", shape, dt, kind="Internal").ap()
    aps["out"] = nc.dram_tensor("out_x", [N, D], F32, kind="ExternalOutput").ap()
    bass_gnn(nc, aps)
    result = run_bass_kernel_spmd(nc, [{f"in_{k}": v for k, v in arrays.items()}], core_ids=[0])
    return result.results[0]["out_x"]
```
